# Optimizing a Trainium2 kernel written in Bass

```python
import numpy as np
import jax
import jax.numpy as jnp

def _softmax(x, axis=-1):
    return jax.nn.softmax(x, axis=axis)

def _gelu(x):
    return jax.nn.gelu(x, approximate=True)

def _silu(x):
    return jax.nn.silu(x)

def _sigmoid(x):
    return jax.nn.sigmoid(x)

def _layernorm(x, axis=-1, eps=1e-05):
    m = jnp.mean(x, axis=axis, keepdims=True)
    v = jnp.var(x, axis=axis, keepdims=True)
    return (x - m) / jnp.sqrt(v + eps)

def _scatter_add(tgt, idx, src, axis=0):
    return tgt.at[idx].add(src)

def _segment_sum(src, seg, n):
    return jax.ops.segment_sum(src, seg, n)
kernel_name = 'mk_decoder_preln_d1_seqx_r4_d2cd27'

def setup_inputs(seed: int=0):
    np.random.seed(seed)
    _w = jnp.asarray

    def _rec_inputs():
        import jax
        import jax.numpy as jnp
        _rk = jax.random.key(seed)
        x = 2.818e-05 + 1 * jax.random.normal(jax.random.fold_in(_rk, 1), (16, 256, 256), jnp.float32)
        _lenS = 256 - jax.random.randint(jax.random.fold_in(_rk, 7), (16,), 0, max(1, 256 // 4) + 1, jnp.int32)
        _lenS2 = 256 - jax.random.randint(jax.random.fold_in(_rk, 8), (16,), 0, max(1, 256 // 4) + 1, jnp.int32)
        _ctx_2048P = jax.random.normal(jax.random.fold_in(_rk, 11), (16, 16, 512), jnp.float32)
        _ctx_2048c = jax.random.dirichlet(jax.random.fold_in(_rk, 511), 0.3 * jnp.ones((16,), jnp.float32), (16, 256))
        _ctx_2048t = jnp.einsum('bsk,bkd->bsd', _ctx_2048c, _ctx_2048P)
        _ctx_2048t = _ctx_2048t * jax.lax.rsqrt(jnp.mean(jnp.square(_ctx_2048t)) + 1e-12) * 0.953939
        ctx_2048 = -0.000125008 + 0.999885 * (_ctx_2048t + 0.3 * jax.random.normal(jax.random.fold_in(_rk, 611), (16, 256, 512), jnp.float32))
        _validS = jnp.arange(256)[None, :] < _lenS[:, None]
        _validS2 = jnp.arange(256)[None, :] < _lenS2[:, None]
        _causal = jnp.tril(jnp.ones((256, 256), dtype=bool))
        mask_BxS2_fk1 = jnp.where(jnp.broadcast_to(_validS2[:, :], (16, 256)), 1.0, 0.0).astype(jnp.float32)
        return (x, ctx_2048, mask_BxS2_fk1)
    x, ctx_2048, mask_BxS2_fk1 = _rec_inputs()

    def _L0_attn_setup():
        import jax, jax.numpy as jnp
        import numpy as np
        B, T, HS = (2, 512, 256)
        QK, VD, NH = (256, 512, 8)
        HD_QK, HD_V = (QK // NH, VD // NH)
        SCALE_BASE = 512.0
        EPS = 1e-05

        def _xpos(q, k, offset=0):
            L, D = (q.shape[1], q.shape[-1])
            half = D // 2
            scale_vec = (jnp.arange(0, D, 2, dtype=jnp.float32) + 0.4 * D) / (1.4 * D)
            pos = jnp.arange(L + offset, dtype=jnp.float32)
            scale = scale_vec[None, :] ** (pos[:, None] / SCALE_BASE)
            inv_freq = 1.0 / 10000.0 ** (jnp.arange(half, dtype=jnp.float32) / half)
            sinus = pos[:, None] * inv_freq[None, :]
            sin, cos = (jnp.sin(sinus), jnp.cos(sinus))
            scale, sin, cos = (scale[-L:], sin[-L:], cos[-L:])

            def dup(m):
                return jnp.repeat(m, 2, axis=-1)

            def rot(x):
                x1, x2 = (x[..., ::2], x[..., 1::2])
                return jnp.stack((-x2, x1), axis=-1).reshape(x.shape)

            def apply(x, s):
                return x * dup(cos * s) + rot(x) * dup(sin * s)
            return (apply(q, scale), apply(k, 1.0 / scale))

        def _reference_tuple_inner(hidden_states, w_qkv, w_gated, w_proj, decay):
            Bsz, L, _ = hidden_states.shape
            qkv = hidden_states @ w_qkv.T
            q, k, v = (qkv[..., :QK], qkv[..., QK:2 * QK], qkv[..., 2 * QK:])
            q, k = _xpos(q, k)
            q = q.reshape(Bsz, L, NH, HD_QK).transpose(0, 2, 1, 3)
            k = k.reshape(Bsz, L, NH, HD_QK).transpose(0, 2, 1, 3)
            v = v.reshape(Bsz, L, NH, HD_V).transpose(0, 2, 1, 3)
            idx = jnp.arange(L)
            expo = idx[:, None] - idx[None, :]
            causal = expo >= 0
            dm = jnp.where(causal[None], decay[:, None, None] ** jnp.where(causal, expo, 0).astype(jnp.float32)[None], 0.0)
            scale = HD_QK ** (-0.5)
            retention = jnp.einsum('bhtd,bhsd->bhts', q, k) * scale * dm[None]
            out = jnp.einsum('bhts,bhsv->bhtv', retention, v)
            curr_kv = jnp.einsum('bhsd,bhsv,hs->bhdv', k, v, dm[:, -1, :])
            x = out.transpose(0, 2, 1, 3).reshape(Bsz, L, NH, HD_V)
            mu = x.mean(-1, keepdims=True)
            var = ((x - mu) ** 2).mean(-1, keepdims=True)
            normed = ((x - mu) / jnp.sqrt(var + EPS)).reshape(Bsz, L, VD)
            gate = jax.nn.silu(hidden_states @ w_gated.T)
            y = gate * normed @ w_proj.T
            return (y, curr_kv)
        key = jax.random.key(seed)
        ks = jax.random.split(key, 4)
        hidden_states = jax.random.normal(ks[0], (B, T, HS), dtype=jnp.float32)
        w_qkv = jax.random.normal(ks[1], (2 * QK + VD, HS), dtype=jnp.float32) * 0.02
        w_gated = jax.random.normal(ks[2], (VD, HS), dtype=jnp.float32) * 0.02
        w_proj = jax.random.normal(ks[3], (HS, VD), dtype=jnp.float32) * 0.02
        decay = jnp.asarray(1.0 - np.exp(np.linspace(np.log(1 / 32), np.log(1 / 128), NH)), dtype=jnp.float32)
        return {'hidden_states': hidden_states, 'w_qkv': w_qkv, 'w_gated': w_gated, 'w_proj': w_proj, 'decay': decay}
    _L0_attn_all = _L0_attn_setup()
    _L0_attn_in = {k: v for k, v in _L0_attn_all.items() if k in ('w_qkv', 'w_gated', 'w_proj', 'decay')}
    del _L0_attn_all

    def _L0_xattn_setup():
        import jax, jax.numpy as jnp
        import numpy as np
        B, S, T = (32, 128, 128)
        SRC_SIZE, TGT_SIZE, OUT_SIZE, NUM_HEAD = (512, 256, 256, 8)
        HEAD_DIM = OUT_SIZE // NUM_HEAD
        key = jax.random.key(seed)
        ks = jax.random.split(key, 12)
        src = jax.random.normal(ks[0], (B, S, SRC_SIZE), dtype=jnp.float32)
        tgt = jax.random.normal(ks[1], (B, T, TGT_SIZE), dtype=jnp.float32)
        src_mask = (jax.random.uniform(ks[2], (B, S)) > 0.3).astype(jnp.float32)
        src_mask = src_mask.at[:, 0].set(1.0)
        tgt_mask = (jax.random.uniform(ks[3], (B, T)) > 0.3).astype(jnp.float32)
        tgt_mask = tgt_mask.at[:, 0].set(1.0)

        def lin(k, out_f, in_f):
            return jax.random.normal(k, (out_f, in_f), dtype=jnp.float32) / np.sqrt(in_f)
        W_src = lin(ks[4], 2 * OUT_SIZE, SRC_SIZE)
        b_src = jnp.zeros((2 * OUT_SIZE,), jnp.float32)
        W_tgt = lin(ks[5], OUT_SIZE, TGT_SIZE)
        b_tgt = jnp.zeros((OUT_SIZE,), jnp.float32)
        W_out = lin(ks[6], OUT_SIZE, OUT_SIZE + TGT_SIZE)
        b_out = jnp.zeros((OUT_SIZE,), jnp.float32)
        return {'src': src, 'tgt': tgt, 'src_mask': src_mask, 'tgt_mask': tgt_mask, 'W_src': W_src, 'b_src': b_src, 'W_tgt': W_tgt, 'b_tgt': b_tgt, 'W_out': W_out, 'b_out': b_out}
    _L0_xattn_all = _L0_xattn_setup()
    _L0_xattn_in = {k: v for k, v in _L0_xattn_all.items() if k in ('W_src', 'b_src', 'W_tgt', 'b_tgt', 'W_out', 'b_out')}
    del _L0_xattn_all

    def _L0_ffn_setup():
        import jax, jax.numpy as jnp
        import numpy as np
        B, F, D, H, E, K = (4, 512, 256, 512, 8, 2)
        key = jax.random.key(seed)
        ks = jax.random.split(key, 9)
        sc = lambda k, shape, fan_in: jax.random.normal(k, shape, jnp.float32) * fan_in ** (-0.5)
        return {'x': jax.random.normal(ks[0], (B, F, D), jnp.float32), 'rw1': sc(ks[1], (D, D), D), 'rb1': jnp.zeros((D,), jnp.float32), 'rw2': sc(ks[2], (D, E), D), 'rb2': jnp.zeros((E,), jnp.float32), 'ew1': sc(ks[3], (E, D, H), D), 'eb1': jnp.zeros((E, H), jnp.float32), 'ew2': sc(ks[4], (E, H, D), H), 'eb2': jnp.zeros((E, D), jnp.float32)}
    _L0_ffn_all = _L0_ffn_setup()
    _L0_ffn_in = {k: v for k, v in _L0_ffn_all.items() if k in ('rw1', 'rb1', 'rw2', 'rb2', 'ew1', 'eb1', 'ew2', 'eb2')}
    del _L0_ffn_all
    return {'x': x, 'ctx_2048': ctx_2048, 'mask_BxS2_fk1': mask_BxS2_fk1, 'L0_attn_w_qkv': _L0_attn_in['w_qkv'], 'L0_attn_w_gated': _L0_attn_in['w_gated'], 'L0_attn_w_proj': _L0_attn_in['w_proj'], 'L0_attn_decay': _L0_attn_in['decay'], 'L0_xattn_W_src': _L0_xattn_in['W_src'], 'L0_xattn_b_src': _L0_xattn_in['b_src'], 'L0_xattn_W_tgt': _L0_xattn_in['W_tgt'], 'L0_xattn_b_tgt': _L0_xattn_in['b_tgt'], 'L0_xattn_W_out': _L0_xattn_in['W_out'], 'L0_xattn_b_out': _L0_xattn_in['b_out'], 'L0_ffn_rw1': _L0_ffn_in['rw1'], 'L0_ffn_rb1': _L0_ffn_in['rb1'], 'L0_ffn_rw2': _L0_ffn_in['rw2'], 'L0_ffn_rb2': _L0_ffn_in['rb2'], 'L0_ffn_ew1': _L0_ffn_in['ew1'], 'L0_ffn_eb1': _L0_ffn_in['eb1'], 'L0_ffn_ew2': _L0_ffn_in['ew2'], 'L0_ffn_eb2': _L0_ffn_in['eb2']}

def reference(x, ctx_2048, mask_BxS2_fk1, L0_attn_w_qkv, L0_attn_w_gated, L0_attn_w_proj, L0_attn_decay, L0_xattn_W_src, L0_xattn_b_src, L0_xattn_W_tgt, L0_xattn_b_tgt, L0_xattn_W_out, L0_xattn_b_out, L0_ffn_rw1, L0_ffn_rb1, L0_ffn_rw2, L0_ffn_rb2, L0_ffn_ew1, L0_ffn_eb1, L0_ffn_ew2, L0_ffn_eb2):
    import jax
    import jax.numpy as jnp

    def _L0_attn_ref(hidden_states, w_qkv, w_gated, w_proj, decay):
        import jax, jax.numpy as jnp
        import numpy as np
        B, T, HS = (2, 512, 256)
        QK, VD, NH = (256, 512, 8)
        HD_QK, HD_V = (QK // NH, VD // NH)
        SCALE_BASE = 512.0
        EPS = 1e-05

        def _xpos(q, k, offset=0):
            L, D = (q.shape[1], q.shape[-1])
            half = D // 2
            scale_vec = (jnp.arange(0, D, 2, dtype=jnp.float32) + 0.4 * D) / (1.4 * D)
            pos = jnp.arange(L + offset, dtype=jnp.float32)
            scale = scale_vec[None, :] ** (pos[:, None] / SCALE_BASE)
            inv_freq = 1.0 / 10000.0 ** (jnp.arange(half, dtype=jnp.float32) / half)
            sinus = pos[:, None] * inv_freq[None, :]
            sin, cos = (jnp.sin(sinus), jnp.cos(sinus))
            scale, sin, cos = (scale[-L:], sin[-L:], cos[-L:])

            def dup(m):
                return jnp.repeat(m, 2, axis=-1)

            def rot(x):
                x1, x2 = (x[..., ::2], x[..., 1::2])
                return jnp.stack((-x2, x1), axis=-1).reshape(x.shape)

            def apply(x, s):
                return x * dup(cos * s) + rot(x) * dup(sin * s)
            return (apply(q, scale), apply(k, 1.0 / scale))

        def _reference_tuple_inner(hidden_states, w_qkv, w_gated, w_proj, decay):
            Bsz, L, _ = hidden_states.shape
            qkv = hidden_states @ w_qkv.T
            q, k, v = (qkv[..., :QK], qkv[..., QK:2 * QK], qkv[..., 2 * QK:])
            q, k = _xpos(q, k)
            q = q.reshape(Bsz, L, NH, HD_QK).transpose(0, 2, 1, 3)
            k = k.reshape(Bsz, L, NH, HD_QK).transpose(0, 2, 1, 3)
            v = v.reshape(Bsz, L, NH, HD_V).transpose(0, 2, 1, 3)
            idx = jnp.arange(L)
            expo = idx[:, None] - idx[None, :]
            causal = expo >= 0
            dm = jnp.where(causal[None], decay[:, None, None] ** jnp.where(causal, expo, 0).astype(jnp.float32)[None], 0.0)
            scale = HD_QK ** (-0.5)
            retention = jnp.einsum('bhtd,bhsd->bhts', q, k) * scale * dm[None]
            out = jnp.einsum('bhts,bhsv->bhtv', retention, v)
            curr_kv = jnp.einsum('bhsd,bhsv,hs->bhdv', k, v, dm[:, -1, :])
            x = out.transpose(0, 2, 1, 3).reshape(Bsz, L, NH, HD_V)
            mu = x.mean(-1, keepdims=True)
            var = ((x - mu) ** 2).mean(-1, keepdims=True)
            normed = ((x - mu) / jnp.sqrt(var + EPS)).reshape(Bsz, L, VD)
            gate = jax.nn.silu(hidden_states @ w_gated.T)
            y = gate * normed @ w_proj.T
            return (y, curr_kv)
        return _reference_tuple_inner(hidden_states, w_qkv, w_gated, w_proj, decay)[0]

    def _L0_xattn_ref(src, tgt, src_mask, tgt_mask, W_src, b_src, W_tgt, b_tgt, W_out, b_out):
        import jax, jax.numpy as jnp
        import numpy as np
        B, S, T = (32, 128, 128)
        SRC_SIZE, TGT_SIZE, OUT_SIZE, NUM_HEAD = (512, 256, 256, 8)
        HEAD_DIM = OUT_SIZE // NUM_HEAD
        b, s, _ = src.shape
        t = tgt.shape[1]
        src_trans = jnp.einsum('bsf,of->bso', src, W_src) + b_src
        tgt_trans = jnp.einsum('btf,of->bto', tgt, W_tgt) + b_tgt
        src_trans = src_trans * src_mask[:, :, None]
        tgt_trans = tgt_trans * tgt_mask[:, :, None]
        src_key, src_val = jnp.split(src_trans, 2, axis=2)
        k = src_key.reshape(b, s, NUM_HEAD, HEAD_DIM)
        v = src_val.reshape(b, s, NUM_HEAD, HEAD_DIM)
        q = tgt_trans.reshape(b, t, NUM_HEAD, HEAD_DIM)
        scores = jnp.einsum('bthd,bshd->bhts', q, k) / np.sqrt(HEAD_DIM)
        scores = jnp.where(src_mask[:, None, None, :] == 0, -jnp.inf, scores)
        attn = jax.nn.softmax(scores, axis=-1)
        tgt_update = jnp.einsum('bhts,bshd->bthd', attn, v).reshape(b, t, OUT_SIZE)
        cat_tgt = jnp.concatenate([tgt, tgt_update], axis=2)
        return jnp.einsum('btf,of->bto', cat_tgt, W_out) + b_out

    def _L0_ffn_ref(x, rw1, rb1, rw2, rb2, ew1, eb1, ew2, eb2):
        import jax, jax.numpy as jnp
        import numpy as np
        B, F, D, H, E, K = (4, 512, 256, 512, 8, 2)
        b, f, d = x.shape
        t = x.reshape(b * f, d)
        logits = jax.nn.silu(t @ rw1 + rb1) @ rw2 + rb2
        vals, idx = jax.lax.top_k(logits, K)
        rows = jnp.arange(t.shape[0])[:, None]
        masked = jnp.full_like(logits, -jnp.inf).at[rows, idx].set(vals)
        w = jax.nn.softmax(masked, axis=1)
        eh = jax.nn.silu(jnp.einsum('td,edh->teh', t, ew1) + eb1[None])
        eo = jnp.einsum('teh,ehd->ted', eh, ew2) + eb2[None]
        y = t + jnp.einsum('te,ted->td', w, eo)
        return y.reshape(b, f, d)
    x = x + _L0_attn_ref(_layernorm(x, axis=-1), L0_attn_w_qkv, L0_attn_w_gated, L0_attn_w_proj, L0_attn_decay)
    x = x + _L0_xattn_ref(ctx_2048, _layernorm(x, axis=-1), mask_BxS2_fk1, mask_BxS2_fk1, L0_xattn_W_src, L0_xattn_b_src, L0_xattn_W_tgt, L0_xattn_b_tgt, L0_xattn_W_out, L0_xattn_b_out)
    x = x + _L0_ffn_ref(_layernorm(x, axis=-1), L0_ffn_rw1, L0_ffn_rb1, L0_ffn_rw2, L0_ffn_rb2, L0_ffn_ew1, L0_ffn_eb1, L0_ffn_ew2, L0_ffn_eb2)
    return x

_drawn_inputs = setup_inputs


def setup_inputs(seed=0):
    import zlib

    import numpy as np

    out = dict(_drawn_inputs(seed))
    spreads = {'L0_xattn_b_src': (0.0, 0.1),
     'L0_xattn_b_tgt': (0.0, 0.361),
     'L0_xattn_b_out': (0.0, 0.1),
     'L0_ffn_rb1': (0.0, 0.1),
     'L0_ffn_rb2': (0.0, 0.1),
     'L0_ffn_eb1': (0.0, 0.418),
     'L0_ffn_eb2': (0.0, 0.1)}
    factors = {}
    for name, (base, spread) in spreads.items():
        noise = np.random.default_rng([zlib.crc32(name.encode()), seed]).standard_normal(out[name].shape)
        drawn = base * np.exp(spread * noise) if base else spread * noise
        out[name] = jnp.asarray(drawn.astype(out[name].dtype))
    for name, factor in factors.items():
        out[name] = (out[name] * factor).astype(out[name].dtype)
    return out
```

```python
import concourse.bass as bass
from concourse import mybir
from contextlib import ExitStack

B, T, D, CTX = 16, 256, 256, 512
P = 128
NT = B * T // P
TPB = T // P
KD, KC = D // P, CTX // P
NH = 8
DV = 512 // NH
DH = D // NH
HPG = P // DH
KV = 512 // P
E, H = 8, 512
KH = H // P
SC = T + P
EPS = 1e-5
BANK = 512
NEG = -1e30

R_ITEMS = (["act"] + ["dve"] * 2 + ["act"] * 2 + ["dve"] * 2 + ["act"] * 2 + ["dve"] * 8
           + ["dve"] * 2 + ["dve", "dve", "act"] + ["dve"] * 2 + ["dve"] + ["act"])
(R_XT, R_QK, R_V, R_G, R_QT, R_KT, R_S, R_O, R_VAR, R_VT, R_GT, R_RB, R_Y, R_T2) = (
    0, 1, 3, 5, 7, 8, 9, 17, 19, 20, 21, 22, 24, 25)
X_ITEMS = (["dve", "act", "dve"] + ["act"] * 4 + ["act", "dve"] * 2 + ["act"] * 4 + ["act", "dve"] * 2
           + ["act", "act", "dve", "dve", "act", "act", "dve"])
(X_K, X_V, X_Q, X_S, X_P, X_RS, X_U, X_RB, X_O, X_T3, X_R1, X_LG) = (0, 1, 2, 3, 7, 19, 20, 21, 22, 23, 24, 25)
X_TT = 8
RING = 4
F_ITEMS = ["act", "dve", "act", "act"] + ["act", "act", "dve"] * (E - 1) + ["dve"]
F_W, F_B = 0, 1
F_H = [2] + [3 * e + 1 for e in range(1, E)]
F_O = [3 * e + 6 for e in range(E - 1)] + [3 * E + 1]
F_RING = 8
SCALE = DH ** -0.5


def previous(items, n, ring):
    m = n - ring
    if m < 0:
        m = max(i for i in range(len(items)) if i % ring == n % ring)
        return items[m], items[:m + 1].count(items[m]) - items.count(items[m])
    return items[m], items[:m + 1].count(items[m])


def build(nc, x, ctxT, maskrow, maskcol, wqkT, wvT, wgT, wpT, decay, wsT, bsk, bsv, wtT, bt, woT, bo,
          rw1, rb1, rw2, rb2, ew1, eb1, ew2, eb2, rot_c, rot_s, delta, ident_in, sel64_in, sel8_in,
          selh_in, iota_in, out):
    f32, bf16, u32 = mybir.dt.float32, mybir.dt.bfloat16, mybir.dt.uint32
    ALU = mybir.AluOpType
    ACT = mybir.ActivationFunctionType
    AX = mybir.AxisListType

    t3_dram = nc.dram_tensor("t3_dram", (B, P, KD * T), f32, kind="Internal").ap()

    ctx = ExitStack()
    with ctx:
        def sb(name, shape, dt=f32, stack=None):
            return (stack or ctx).enter_context(nc.sbuf_tensor(name, shape, dt))

        def sem(name):
            return ctx.enter_context(nc.semaphore(name))

        psum = ctx.enter_context(nc.psum_tensor("psum", [P, 8, BANK], f32))

        x_all = sb("x_all", [P, NT, D])
        route = sb("route", [P, NT, E])
        ident = sb("ident", [P, P])

        one = ExitStack()

        def s1(name, shape, dt=f32):
            return sb(name, shape, dt, one)

        w_qk = s1("w_qk", [P, KD, 2 * D])
        w_v = s1("w_v", [P, KD, 512])
        w_vc = s1("w_vc", [P, KD, 512])
        w_g = s1("w_g", [P, KD, 512])
        w_p = s1("w_p", [P, KV, D])
        w_s = s1("w_s", [P, KC, 2 * D])
        w_t = s1("w_t", [P, KD, D])
        w_o = s1("w_o", [P, 2 * KD, D])
        w_r1 = s1("w_r1", [P, KD, D])
        w_r2 = s1("w_r2", [P, KD, E])
        b_k = s1("b_k", [P, KD])
        b_q = s1("b_q", [P, KD])
        b_r1 = s1("b_r1", [P, KD])
        b_r1h = s1("b_r1h", [P, KD])
        b_v = s1("b_v", [1, D])
        b_o = s1("b_o", [1, D])
        b_r2 = s1("b_r2", [1, E])
        mcol = s1("mcol", [P, NT])
        rc = s1("rc", [P, TPB, 2 * D])
        rs = s1("rs", [P, TPB, 2 * D])
        DM = s1("DM", [P, NH, SC])
        dec = s1("dec", [P, NH])
        sel64 = s1("sel64", [P, KV, NH])
        sel8 = s1("sel8", [NH, KV, P])
        selh = s1("selh", [NH, KD, P])
        ones1 = s1("ones1", [1, P])
        ones1b = s1("ones1b", [P, P], bf16)
        iota8 = s1("iota8", [P, E])
        xn3 = s1("xn3", [P, TPB, D])
        vmean = s1("vmean", [P, KD, NH])

        stats = s1("stats", [P, TPB, 6])
        mv = s1("mv", [P, TPB, 2])
        veps = s1("veps", [P, TPB])
        rstd = s1("rstd", [P, TPB])
        mhalf = s1("mhalf", [P, TPB * NH])
        xn = s1("xn", [P, TPB, D])
        xnT = s1("xnT", [P, KD, T])
        rot_a = s1("rot_a", [P, TPB, 2 * D])
        rot_b = s1("rot_b", [P, TPB, 2 * D])
        vc = s1("vc", [P, TPB, 512])
        gth = s1("gth", [P, KV, T])
        gate = s1("gate", [P, KV, T])
        qT = s1("qT", [P, KD, T])
        kT = s1("kT", [P, KD, T])
        R = s1("R", [P, NH, SC])
        sq = s1("sq", [P, KV, T])
        z = s1("z", [P, KV, T])
        gv = s1("gv", [NH, T])
        gr = s1("gr", [NH, T])
        gvt = s1("gvt", [P, TPB, NH])
        grt = s1("grt", [P, TPB, NH])
        yT = s1("yT", [P, KV, T])
        t2T = s1("t2T", [P, KD, T])

        delta_sb = R[:, 0, 0:T]

        ctx_sb = s1("ctx_sb", [P, KC, T])
        mrow = s1("mrow", [P, T])
        neg = s1("neg", [P, T], bf16)
        k2T = s1("k2T", [P, KD, T])
        q2T = s1("q2T", [P, KD, T])
        v2 = s1("v2", [P, TPB, D])
        mx = s1("mx", [P, 2, NH])
        nmx = s1("nmx", [P, 2, NH])
        rsum = s1("rsum", [P, TPB, NH])
        rinv = s1("rinv", [P, TPB, NH])
        riT = s1("riT", [NH, T])
        pr = s1("pr", [P, NH, T])
        pT = s1("pT", [P, TPB, NH, T])
        u_raw = s1("u_raw", [P, KD, T])
        uT = s1("uT", [P, KD, T])
        t3T = s1("t3T", [P, KD, T])
        r1 = s1("r1", [P, KD, T])
        r1th = s1("r1th", [P, KD, T])
        lg = s1("lg", [P, TPB, E])
        top = s1("top", [P, TPB, E])
        topi = s1("topi", [P, TPB, E], u32)
        topf = s1("topf", [P, TPB, 2])
        dlt = s1("dlt", [P, TPB])
        e2 = s1("e2", [P, TPB])
        den = s1("den", [P, TPB])
        wt1 = s1("wt1", [P, TPB])
        wt2 = s1("wt2", [P, TPB])
        oh1 = s1("oh1", [P, TPB, E])
        oh2 = s1("oh2", [P, TPB, E])

        one.close()
        two = ctx

        def s2(name, shape, dt=f32):
            return sb(name, shape, dt, two)

        w1 = s2("w1", [P, E, KD, H])
        w2 = s2("w2", [P, E, KH, D])
        b1 = s2("b1", [P, E, KH])
        b2 = s2("b2", [E, D])
        tf = s2("tf", [P, 2, KD, T])
        hT = s2("hT", [P, 2, KH, T])
        rt = s2("rt", [P, TPB, E])
        wT = s2("wT", [E, T])

        ld = {n: sem("ld_" + n) for n in ("x", "const", "wqk", "wv", "wg", "wp", "ws", "wt", "wo", "r", "ffn")}
        r_filled = sem("r_filled")
        x_filled = sem("x_filled")
        f_filled = sem("f_filled")
        r_by_act = sem("r_by_act")
        r_by_dve = sem("r_by_dve")
        x_by_act = sem("x_by_act")
        x_by_dve = sem("x_by_dve")
        f_by_act = sem("f_by_act")
        f_by_dve = sem("f_by_dve")
        dm_scan = sem("dm_scan")
        dm_done = sem("dm_done")
        vmean_s = sem("vmean_s")
        wvc_done = sem("wvc_done")
        setup = sem("setup")
        setup2 = sem("setup2")
        neg_done = sem("neg_done")
        rotab = sem("rotab")
        rot = sem("rot")
        th_g = sem("th_g")
        sq_done = sem("sq_done")
        gr_s = sem("gr_s")
        mx_s = sem("mx_s")
        nmx_s = sem("nmx_s")
        ri_s = sem("ri_s")
        t3_out = sem("t3_out")
        r1_s = sem("r1_s")
        top_s = sem("top_s")
        topi_s = sem("topi_s")
        topf_s = sem("topf_s")
        dlt_s = sem("dlt_s")
        e2_s = sem("e2_s")
        den_s = sem("den_s")
        wt1_s = sem("wt1_s")
        wt2_s = sem("wt2_s")
        oh_s = sem("oh_s")
        route_s = sem("route_s")
        phase1 = sem("phase1")
        rt_s = sem("rt_s")
        out_s = sem("out_s")
        held = sem("held")
        ctx_in = sem("ctx_in")
        mrow_in = sem("mrow_in")
        x2t_s = sem("x2t_s")
        stat = [sem(f"stat{n}") for n in range(3)]
        aggr = [sem(f"aggr{n}") for n in range(3)]
        veps_s = [sem(f"veps{n}") for n in range(3)]
        rstd_s = [sem(f"rstd{n}") for n in range(3)]
        xn_s = [sem(f"xn{n}") for n in range(3)]
        tf_in = [sem(f"tf_in{n}") for n in range(2)]

        r_all = {"act": R_ITEMS.count("act"), "dve": R_ITEMS.count("dve")}
        x_all_ = {"act": X_ITEMS.count("act"), "dve": X_ITEMS.count("dve")}
        f_all = {"act": F_ITEMS.count("act"), "dve": F_ITEMS.count("dve")}

        def r_act(b, k):
            return (b + 1) * r_all["act"] + k

        def r_dve(b, k):
            return (b + 1) * r_all["dve"] + k

        def x_act(b, k):
            return (b + 1) * x_all_["act"] + k

        def x_dve(b, k):
            return (b + 1) * x_all_["dve"] + k

        def f_act(b, k):
            return (b + 1) * f_all["act"] + k

        def f_dve(b, k):
            return (b + 1) * f_all["dve"] + k

        def r_item(b, n):
            return b * len(R_ITEMS) + n + 1

        def x_item(b, n):
            return b * len(X_ITEMS) + n + 1

        def f_item(b, n):
            return b * len(F_ITEMS) + n + 1

        def r_free(b, n):
            who, k = previous(R_ITEMS, n, RING)
            return (r_by_act, r_act(b, k)) if who == "act" else (r_by_dve, r_dve(b, k))

        def x_free(b, n):
            who, k = previous(X_ITEMS, n, RING)
            return (x_by_act, x_act(b, k)) if who == "act" else (x_by_dve, x_dve(b, k))

        def f_free(b, n):
            who, k = previous(F_ITEMS, n, F_RING)
            return (f_by_act, f_act(b, k)) if who == "act" else (f_by_dve, f_dve(b, k))

        def hold(eng):
            eng.sem_inc(held, 1)

        def rbank(n):
            return psum[:, n % RING, :]

        def xbank(n):
            return psum[:, RING + n % RING, :]

        def tiles(b):
            return bass.ds(b * TPB, TPB)

        block = ctx.enter_context(nc.Block())

        @block.sync
        def _(sp):
            xv = x.rearrange("(n p) d -> p n d", p=P)

            def load(name, dst, src):
                sp.dma_start(dst, src).then_inc(ld[name], 16)

            load("x", x_all[:, 0:8, :], xv[:, 0:8, :])
            for dst, src in ((ident, ident_in), (rc, rot_c), (rs, rot_s), (dec, decay.partition_broadcast(P)),
                             (sel64, sel64_in), (sel8, sel8_in), (selh, selh_in), (iota8, iota_in), (mcol, maskcol),
                             (b_k, bsk), (b_q, bt), (b_r1, rb1), (b_v, bsv), (b_o, bo), (b_r2, rb2)):
                load("const", dst[:], src)
            load("const", delta_sb, delta)
            load("wqk", w_qk[:], wqkT)
            load("wv", w_v[:], wvT)
            load("wg", w_g[:], wgT)
            load("wp", w_p[:], wpT)
            load("ws", w_s[:], wsT)
            load("x", x_all[:, 8:NT, :], xv[:, 8:NT, :])
            load("wt", w_t[:], wtT)
            load("wo", w_o[:], woT)
            load("r", w_r1[:], rw1)
            load("r", w_r2[:], rw2)

            def context(b):
                sp.dma_start(ctx_sb[:], ctxT[bass.ds(b, 1)].rearrange("a p f -> (a p) f")
                             .rearrange("p (c s) -> p c s", c=KC)).then_inc(ctx_in, 16)
                sp.dma_start(mrow[:], maskrow[bass.ds(b, 1)].rearrange("a s -> (a s)").partition_broadcast(P)
                             ).then_inc(mrow_in, 16)

            def store_t3(b):
                sp.wait_ge(x_by_act, x_act(b, 16))
                sp.dma_start(t3_dram[bass.ds(b, 1)].rearrange("a p f -> (a p) f"),
                             t3T[:].rearrange("p c s -> p (c s)")).then_inc(t3_out, 16)

            context(0)
            with sp.Fori(1, B) as b:
                sp.wait_ge(x_filled, x_item(b - 1, X_V))
                sp.wait_ge(x_by_dve, x_dve(b - 1, 2))
                context(b)
                store_t3(b - 1)
            store_t3(B - 1)

            sp.wait_ge(phase1, 4)
            for dst, src in ((w1, ew1), (w2, ew2), (b1, eb1), (b2, eb2)):
                load("ffn", dst[:], src)
            sp.wait_ge(t3_out, 16 * B)

            def load_t3(b, slot):
                sp.dma_start(tf[:, slot].rearrange("p c s -> p (c s)"),
                             t3_dram[bass.ds(b, 1)].rearrange("a p f -> (a p) f")).then_inc(tf_in[slot], 16)

            outv = out.rearrange("(n p) d -> p n d", p=P)

            def store(b):
                sp.wait_ge(f_by_dve, f_dve(b + 1, 0))
                sp.dma_start(outv[:, tiles(b), :], x_all[:, tiles(b), :]).then_inc(out_s, 16)

            load_t3(0, 0)
            load_t3(1, 1)
            with sp.Fori(1, B // 2) as h:
                sp.wait_ge(f_filled, f_item(2 * h - 1, -1))
                load_t3(2 * h, 0)
                store(2 * h - 2)
                sp.wait_ge(f_filled, f_item(2 * h, -1))
                load_t3(2 * h + 1, 1)
                store(2 * h - 1)
            store(B - 2)
            store(B - 1)
            sp.wait_ge(out_s, 16 * B)

        @block.tensor
        def _(pe):
            def mm(o, l, r, first, last):
                return nc.tensor.matmul(o, l, r, start=first, stop=last)

            def transpose_rows(bank, src, chunks):
                for c in range(chunks):
                    for t in range(TPB):
                        last = nc.tensor.transpose(bank[:, c * T + t * P:c * T + (t + 1) * P],
                                                   src[:, t, c * P:(c + 1) * P], ident[:])
                return last

            def filled(ring, ins):
                ins.then_inc((r_filled if ring == "r" else x_filled), 1)

            def r_xt(b):
                pe.wait_ge(xn_s[0], b * TPB + TPB)
                pe.wait_ge(*r_free(b, R_XT))
                filled("r", transpose_rows(rbank(R_XT), xn, KD))

            def r_qk(b):
                pe.wait_ge(r_by_act, r_act(b, 1))
                for t in range(TPB):
                    pe.wait_ge(*r_free(b, R_QK + t))
                    for k in range(KD):
                        last = mm(rbank(R_QK + t), xnT[:, k, t * P:(t + 1) * P], w_qk[:, k, :], k == 0, k == KD - 1)
                    filled("r", last)

            def r_v(b):
                for t in range(TPB):
                    pe.wait_ge(*r_free(b, R_V + t))
                    for k in range(KD):
                        last = mm(rbank(R_V + t), xnT[:, k, t * P:(t + 1) * P], w_vc[:, k, :], k == 0, k == KD - 1)
                    filled("r", last)

            def r_g(b):
                for n in range(2):
                    pe.wait_ge(*r_free(b, R_G + n))
                    for j in range(2):
                        g = 2 * n + j
                        for k in range(KD):
                            last = mm(rbank(R_G + n)[:, j * T:(j + 1) * T], w_g[:, k, g * P:(g + 1) * P],
                                      xnT[:, k, :], k == 0, k == KD - 1)
                    filled("r", last)

            def r_qkt(b):
                pe.wait_ge(rot, TPB * (b + 1))
                for n in range(2):
                    pe.wait_ge(*r_free(b, R_QT + n))
                    filled("r", transpose_rows(rbank(R_QT + n), rot_a[:, :, n * D:(n + 1) * D], KD))

            def r_scores(b, heads):
                pe.wait_ge(r_by_act, r_act(b, 5))
                for h in heads:
                    pe.wait_ge(*r_free(b, R_S + h))
                    g, r = h // HPG, DH * (h % HPG)
                    o = rbank(R_S + h)
                    mm(o[:, 0:T], kT[r:r + DH, g, 0:P], qT[r:r + DH, g, :], True, True)
                    filled("r", mm(o[:, T:SC], kT[r:r + DH, g, P:T], qT[r:r + DH, g, P:T], True, True))

            def r_out(b):
                pe.wait_ge(r_by_dve, r_dve(b, 12))
                for n in range(2):
                    pe.wait_ge(*r_free(b, R_O + n))
                    for j in range(2):
                        for half in range(2):
                            h = 2 * (2 * n + j) + half
                            o = rbank(R_O + n)[DV * half:DV * (half + 1), j * T:(j + 1) * T]
                            mm(o, vc[:, 0, h * DV:(h + 1) * DV], R[:, h, 0:T], True, False)
                            last = mm(o[:, P:T], vc[:, 1, h * DV:(h + 1) * DV], R[:, h, T:SC], False, True)
                    filled("r", last)

            def r_var(b):
                pe.wait_ge(sq_done, 2 * (b + 1))
                pe.wait_ge(*r_free(b, R_VAR))
                for g in range(KV):
                    last = mm(rbank(R_VAR)[0:NH, 0:T], sel64[:, g, :], sq[:, g, :], g == 0, g == KV - 1)
                filled("r", last)

            def r_vt(b):
                pe.wait_ge(r_by_dve, r_dve(b, 15))
                hold(pe)
                for t in range(TPB):
                    last = nc.tensor.transpose(rbank(R_VT)[:, t * NH:(t + 1) * NH], gv[:, t * P:(t + 1) * P],
                                               ident[0:NH, 0:NH])
                filled("r", last)

            def r_gt(b):
                pe.wait_ge(gr_s, b + 1)
                pe.wait_ge(*r_free(b, R_GT))
                for t in range(TPB):
                    last = nc.tensor.transpose(rbank(R_GT)[0:NH, t * P:(t + 1) * P], grt[:, t, :], ident[:])
                filled("r", last)

            def r_rb(b):
                pe.wait_ge(r_by_act, r_act(b, 6))
                for n in range(2):
                    pe.wait_ge(*r_free(b, R_RB + n))
                    for j in range(2):
                        last = mm(rbank(R_RB + n)[:, j * T:(j + 1) * T], sel8[:, 2 * n + j, :], gr[:], True, True)
                    filled("r", last)

            def r_y(b):
                pe.wait_ge(r_by_dve, r_dve(b, 18))
                pe.wait_ge(*r_free(b, R_Y))
                for t in range(TPB):
                    for g in range(KV):
                        last = mm(rbank(R_Y)[:, t * D:(t + 1) * D], yT[:, g, t * P:(t + 1) * P], w_p[:, g, :],
                                  g == 0, g == KV - 1)
                filled("r", last)

            def r_t2(b):
                pe.wait_ge(xn_s[1], TPB * (b + 1))
                pe.wait_ge(*r_free(b, R_T2))
                filled("r", transpose_rows(rbank(R_T2), xn, KD))

            def x_k(b):
                pe.wait_ge(ctx_in, 16 * (b + 1))
                pe.wait_ge(*x_free(b, X_K))
                for g in range(KD):
                    for k in range(KC):
                        last = mm(xbank(X_K)[:, g * T:(g + 1) * T], w_s[:, k, g * P:(g + 1) * P], ctx_sb[:, k, :],
                                  k == 0, k == KC - 1)
                filled("x", last)

            def x_v(b):
                pe.wait_ge(*x_free(b, X_V))
                for t in range(TPB):
                    o = xbank(X_V)[:, t * D:(t + 1) * D]
                    for k in range(KC):
                        mm(o, ctx_sb[:, k, t * P:(t + 1) * P], w_s[:, k, D:2 * D], k == 0, False)
                    last = mm(o, ones1[:], b_v[:], False, True)
                filled("x", last)

            def x_q(b):
                pe.wait_ge(r_by_act, r_act(b + 1, 0))
                pe.wait_ge(*x_free(b, X_Q))
                for g in range(KD):
                    for k in range(KD):
                        last = mm(xbank(X_Q)[:, g * T:(g + 1) * T], w_t[:, k, g * P:(g + 1) * P], t2T[:, k, :],
                                  k == 0, k == KD - 1)
                filled("x", last)

            def x_scores(b, t):
                if t == 0:
                    pe.wait_ge(x_by_dve, x_dve(b, 2))
                    pe.wait_ge(neg_done, b + 1)
                for r in range(HPG):
                    n = X_S + X_TT * t + r
                    pe.wait_ge(*x_free(b, n))
                    o = xbank(n)
                    for g in range(KD):
                        mm(o[:, g * T:(g + 1) * T], q2T[DH * r:DH * (r + 1), g, t * P:(t + 1) * P],
                           k2T[DH * r:DH * (r + 1), g, :], True, False)
                        last = mm(o[:, g * T:(g + 1) * T], ones1b[DH * r:DH * r + 1, :],
                                  neg[DH * r:DH * r + 1, :], False, True)
                    filled("x", last)

            def x_probs(b, t):
                for r in range(HPG):
                    n = X_P + X_TT * t + r
                    pe.wait_ge(x_by_act, x_act(b, 1 + 6 * t + r + 1))
                    pe.wait_ge(*x_free(b, n))
                    for s in range(TPB):
                        for g in range(KD):
                            last = nc.tensor.transpose(xbank(n)[:, (s * KD + g) * P:(s * KD + g + 1) * P],
                                                       pr[:, g * HPG + r, s * P:(s + 1) * P], ident[:])
                    filled("x", last)

            def x_u(b):
                pe.wait_ge(ri_s, b + 1)
                pe.wait_ge(*x_free(b, X_RS))
                for t in range(TPB):
                    last = nc.tensor.transpose(xbank(X_RS)[0:NH, t * P:(t + 1) * P], rinv[:, t, :], ident[:])
                filled("x", last)
                pe.wait_ge(x_by_act, x_act(b, 13))
                pe.wait_ge(x_by_dve, x_dve(b, 6))
                pe.wait_ge(*x_free(b, X_U))
                for h in range(NH):
                    g, r = h // HPG, DH * (h % HPG)
                    for s in range(TPB):
                        last = mm(xbank(X_U)[r:r + DH, g * T:(g + 1) * T], v2[:, s, h * DH:(h + 1) * DH],
                                  pT[:, s, h, :], s == 0, s == TPB - 1)
                filled("x", last)

            def x_rb(b):
                pe.wait_ge(x_by_act, x_act(b, 14))
                pe.wait_ge(*x_free(b, X_RB))
                for g in range(KD):
                    last = mm(xbank(X_RB)[:, g * T:(g + 1) * T], selh[:, g, :], riT[:], True, True)
                filled("x", last)

            def x_out(b):
                pe.wait_ge(x_by_dve, x_dve(b, 7))
                pe.wait_ge(*x_free(b, X_O))
                for t in range(TPB):
                    o = xbank(X_O)[:, t * D:(t + 1) * D]
                    for k in range(2 * KD):
                        src = t2T if k < KD else uT
                        mm(o, src[:, k % KD, t * P:(t + 1) * P], w_o[:, k, :], k == 0, False)
                    last = mm(o, ones1[:], b_o[:], False, True)
                filled("x", last)

            def x_t3(b):
                pe.wait_ge(xn_s[2], TPB * (b + 1))
                pe.wait_ge(*x_free(b, X_T3))
                filled("x", transpose_rows(xbank(X_T3), xn3, KD))

            def x_r1(b):
                pe.wait_ge(x_by_act, x_act(b, 16))
                pe.wait_ge(*x_free(b, X_R1))
                for g in range(KD):
                    for k in range(KD):
                        last = mm(xbank(X_R1)[:, g * T:(g + 1) * T], w_r1[:, k, g * P:(g + 1) * P], t3T[:, k, :],
                                  k == 0, k == KD - 1)
                filled("x", last)

            def x_lg(b):
                pe.wait_ge(r1_s, b + 1)
                pe.wait_ge(*x_free(b, X_LG))
                for t in range(TPB):
                    o = xbank(X_LG)[:, t * E:(t + 1) * E]
                    for k in range(KD):
                        mm(o, r1[:, k, t * P:(t + 1) * P], w_r2[:, k, :], k == 0, False)
                    last = mm(o, ones1[:], b_r2[:], False, True)
                filled("x", last)

            def both(i, r, x):
                j = i - 1
                if x: x_k(j)
                if r: r_xt(i)
                if x: x_v(j)
                if r: r_qk(i)
                if x: x_q(j)
                if r: r_v(i)
                if x: x_scores(j, 0)
                if r: r_g(i)
                if r: r_qkt(i)
                if x: x_probs(j, 0)
                if r: r_scores(i, range(0, 4))
                if x: x_scores(j, 1)
                if r: r_scores(i, range(4, 8))
                if x: x_probs(j, 1)
                if r: r_out(i)
                if r: r_var(i)
                if x: x_u(j)
                if r: r_vt(i)
                if x: x_rb(j)
                if r: r_gt(i)
                if x: x_out(j)
                if r: r_rb(i)
                if x: x_t3(j)
                if x: x_r1(j)
                if r: r_y(i)
                if x: x_lg(j)
                if r: r_t2(i)

            for n, k in (("const", 16), ("wqk", 1), ("wv", 1), ("wg", 1), ("wp", 1)):
                pe.wait_ge(ld[n], 16 * k)
            pe.wait_ge(setup, 1)
            pe.wait_ge(wvc_done, KD)
            both(0, True, False)
            for n, k in (("ws", 1), ("wt", 1), ("wo", 1), ("r", 2)):
                pe.wait_ge(ld[n], 16 * k)
            with pe.Fori(1, B) as i:
                both(i, True, True)
            both(B, False, True)
            pe.drain().then_inc(phase1, 1)

            def fbank(n):
                return psum[:, n % F_RING, :]

            def f_bias(b):
                pe.wait_ge(*f_free(b, F_W))
                for t in range(TPB):
                    last = nc.tensor.transpose(fbank(F_W)[0:E, t * P:(t + 1) * P], rt[:, t, :], ident[:])
                last.then_inc(f_filled, 1)

            def f_bias_sum(b):
                pe.wait_ge(f_by_act, f_act(b, 1))
                pe.wait_ge(*f_free(b, F_B))
                for t in range(TPB):
                    last = mm(fbank(F_B)[:, t * D:(t + 1) * D], wT[:, t * P:(t + 1) * P], b2[:], True, True)
                last.then_inc(f_filled, 1)

            def f_hidden(b, slot, e):
                for n in range(2):
                    item = F_H[e] + n
                    pe.wait_ge(*f_free(b, item))
                    for j in range(2):
                        c = 2 * n + j
                        for k in range(KD):
                            last = mm(fbank(item)[:, j * T:(j + 1) * T], w1[:, e, k, c * P:(c + 1) * P],
                                      tf[:, slot, k, :], k == 0, k == KD - 1)
                    last.then_inc(f_filled, 1)

            def f_output(b, e):
                item = F_O[e]
                pe.wait_ge(f_by_act, f_act(b, 1 + 2 * (e + 1)))
                pe.wait_ge(*f_free(b, item))
                for t in range(TPB):
                    for c in range(KH):
                        last = mm(fbank(item)[:, t * D:(t + 1) * D], hT[:, e % 2, c, t * P:(t + 1) * P],
                                  w2[:, e, c, :], c == 0, c == KH - 1)
                last.then_inc(f_filled, 1)

            def f_batch(h, slot):
                b = 2 * h + slot
                pe.wait_ge(rt_s, b + 1)
                f_bias(b)
                pe.wait_ge(tf_in[slot], 16 * (h + 1))
                f_bias_sum(b)
                f_hidden(b, slot, 0)
                for e in range(1, E):
                    f_hidden(b, slot, e)
                    f_output(b, e - 1)
                f_output(b, E - 1)

            pe.wait_ge(ld["ffn"], 16 * 4)
            f_batch(0, 0)
            f_batch(0, 1)
            with pe.Fori(1, B // 2) as h:
                f_batch(h, 0)
                f_batch(h, 1)

        @block.vector
        def _(dve):
            V = nc.vector

            def norm(b, n, src, dst):
                hold(dve)
                for t in range(TPB):
                    V.bn_stats(stats[:, t, :], src(t)).then_inc(stat[n], 1)
                dve.wait_ge(stat[n], TPB * (b + 1))
                hold(dve)
                for t in range(TPB):
                    V.bn_aggr(mv[:, t, :], stats[:, t, :]).then_inc(aggr[n], 1)
                dve.wait_ge(rstd_s[n], b + 1)
                for t in range(TPB):
                    V.tensor_scalar(dst[:, t, :], src(t), mv[:, t, 0:1], rstd[:, t:t + 1],
                                    ALU.subtract, ALU.mult).then_inc(xn_s[n], 1)

            def tile_of(b):
                return lambda t: x_all[:, bass.ds(b * TPB + t, 1), :].rearrange("p a d -> p (a d)")

            def r_norm1(b):
                dve.wait_ge(r_filled, r_item(b - 1, R_T2))
                norm(b, 0, tile_of(b), xn)

            def r_rotate(b):
                for t in range(TPB):
                    dve.wait_ge(r_filled, r_item(b, R_QK + t))
                    p = rbank(R_QK + t)
                    V.tensor_tensor(rot_a[:, t, :], p, rc[:, t, :], ALU.mult).then_inc(rotab, 1)
                    pv = p.rearrange("p (h two j) -> p h two j", two=2, j=DH // 2)
                    sv = rs[:, t, :].rearrange("p (h two j) -> p h two j", two=2, j=DH // 2)
                    bv = rot_b[:, t, :].rearrange("p (h two j) -> p h two j", two=2, j=DH // 2)
                    V.tensor_tensor(bv[:, :, 0, :], pv[:, :, 1, :], sv[:, :, 0, :], ALU.mult).then_inc(rotab, 1)
                    V.tensor_tensor(bv[:, :, 1, :], pv[:, :, 0, :], sv[:, :, 1, :], ALU.mult
                                    ).then_inc(r_by_dve, 1)

            def r_gate(b):
                for n in range(2):
                    dve.wait_ge(th_g, 2 * b + n + 1)
                    V.scalar_tensor_tensor(gate[:, 2 * n:2 * n + 2, :].rearrange("p a s -> p (a s)"),
                                           gth[:, 2 * n:2 * n + 2, :].rearrange("p a s -> p (a s)"), 1.0,
                                           rbank(R_G + n), ALU.add, ALU.mult).then_inc(r_by_dve, 1)

            def r_decay(b, heads):
                for h in heads:
                    dve.wait_ge(r_filled, r_item(b, R_S + h))
                    V.tensor_tensor(R[:, h, :], rbank(R_S + h)[:, 0:SC], DM[:, h, :], ALU.mult
                                    ).then_inc(r_by_dve, 1)

            def r_z(b):
                for n in range(2):
                    dve.wait_ge(sq_done, 2 * b + n + 1)
                    V.tensor_tensor(z[:, 2 * n:2 * n + 2, :].rearrange("p a s -> p (a s)"), rbank(R_O + n),
                                    gate[:, 2 * n:2 * n + 2, :].rearrange("p a s -> p (a s)"), ALU.mult
                                    ).then_inc(r_by_dve, 1)

            def r_var(b):
                dve.wait_ge(r_filled, r_item(b, R_VAR))
                V.tensor_scalar(gv[:], rbank(R_VAR)[0:NH, 0:T], EPS, 4.0, ALU.add, ALU.mult).then_inc(r_by_dve, 1)

            def r_vt(b):
                dve.wait_ge(r_filled, r_item(b, R_VT))
                V.tensor_copy(gvt[:].rearrange("p t h -> p (t h)"), rbank(R_VT)[:, 0:TPB * NH]).then_inc(r_by_dve, 1)

            def r_y(b):
                dve.wait_ge(r_by_dve, r_dve(b, 14))
                for n in range(2):
                    dve.wait_ge(r_filled, r_item(b, R_RB + n))
                    V.tensor_tensor(yT[:, 2 * n:2 * n + 2, :].rearrange("p a s -> p (a s)"), rbank(R_RB + n),
                                    z[:, 2 * n:2 * n + 2, :].rearrange("p a s -> p (a s)"), ALU.mult
                                    ).then_inc(r_by_dve, 1)

            def r_x1(b):
                dve.wait_ge(r_filled, r_item(b, R_Y))
                xt = x_all[:, tiles(b), :].rearrange("p a d -> p (a d)")
                V.tensor_tensor(xt, rbank(R_Y), xt, ALU.add).then_inc(r_by_dve, 1)
                dve.wait_ge(r_by_dve, r_dve(b + 1, 0))
                norm(b, 1, tile_of(b), xn)

            def x_k(b):
                dve.wait_ge(x_filled, x_item(b, X_K))
                dve.wait_ge(mrow_in, 16 * (b + 1))
                V.tensor_scalar(neg[:], mrow[:], 0.0, NEG, ALU.is_equal, ALU.mult).then_inc(neg_done, 1)
                for g in range(KD):
                    ins = V.scalar_tensor_tensor(k2T[:, g, :], xbank(X_K)[:, g * T:(g + 1) * T], b_k[:, g:g + 1],
                                                 mrow[:], ALU.add, ALU.mult)
                ins.then_inc(x_by_dve, 1)

            def x_q(b):
                dve.wait_ge(x_filled, x_item(b, X_Q))
                for g in range(KD):
                    ins = V.scalar_tensor_tensor(q2T[:, g, :], xbank(X_Q)[:, g * T:(g + 1) * T], b_q[:, g:g + 1],
                                                 mrow[:], ALU.add, ALU.mult)
                ins.then_inc(x_by_dve, 1)

            def x_max(b, t):
                for r in range(HPG):
                    n = X_S + X_TT * t + r
                    dve.wait_ge(x_filled, x_item(b, n))
                    V.tensor_reduce(mx[:, t, r::HPG], xbank(n).rearrange("p (g s) -> p g s", g=KD), AX.X, ALU.max
                                    ).then_inc(mx_s, 1)
                    dve.wait_ge(mx_s, HPG * (TPB * b + t) + r + 1)
                    V.tensor_scalar(nmx[:, t, r::HPG], mx[:, t, r::HPG], -SCALE, None, ALU.mult
                                    ).then_inc(nmx_s, 1)

            def x_probs(b, t):
                for r in (1, 3):
                    n = X_P + X_TT * t + r
                    dve.wait_ge(x_filled, x_item(b, n))
                    V.tensor_copy(pT[:, :, r::HPG, t * P:(t + 1) * P],
                                  xbank(n).rearrange("p (s g t) -> p s g t", s=TPB, g=KD)).then_inc(x_by_dve, 1)

            def x_rinv(b):
                dve.wait_ge(x_by_act, x_act(b, 11))
                V.reciprocal(rinv[:].rearrange("p t h -> p (t h)"), rsum[:].rearrange("p t h -> p (t h)")
                             ).then_inc(ri_s, 1)

            def x_u(b):
                dve.wait_ge(x_by_act, x_act(b, 15))
                dve.wait_ge(x_filled, x_item(b, X_RB))
                V.tensor_tensor(uT[:].rearrange("p g t -> p (g t)"), xbank(X_RB),
                                u_raw[:].rearrange("p g t -> p (g t)"), ALU.mult).then_inc(x_by_dve, 1)

            def x_x2(b):
                dve.wait_ge(x_filled, x_item(b, X_O))
                xt = x_all[:, tiles(b), :].rearrange("p a d -> p (a d)")
                V.tensor_tensor(xt, xbank(X_O), xt, ALU.add).then_inc(x_by_dve, 1)
                dve.wait_ge(x_by_dve, x_dve(b, 8))
                norm(b, 2, tile_of(b), xn3)
                dve.wait_ge(xn_s[2], TPB * (b + 1))
                V.tensor_tensor(xt, xt, xn3[:].rearrange("p a d -> p (a d)"), ALU.add).then_inc(x2t_s, 1)

            def x_r1(b):
                dve.wait_ge(x_by_act, x_act(b + 1, 0))
                V.scalar_tensor_tensor(r1[:].rearrange("p g t -> p (g t)"), r1th[:].rearrange("p g t -> p (g t)"), 1.0,
                                       r1[:].rearrange("p g t -> p (g t)"), ALU.add, ALU.mult).then_inc(r1_s, 1)

            def x_route(b):
                dve.wait_ge(x_filled, x_item(b, X_LG))
                V.tensor_copy(lg[:].rearrange("p t e -> p (t e)"), xbank(X_LG)[:, 0:TPB * E]
                              ).then_inc(x_by_dve, 1)
                dve.wait_ge(x_by_dve, x_dve(b + 1, 0))
                hold(dve)
                for t in range(TPB):
                    V.max(top[:, t, :], lg[:, t, :]).then_inc(top_s, 1)
                dve.wait_ge(top_s, TPB * (b + 1))
                hold(dve)
                for t in range(TPB):
                    V.max_index(topi[:, t, :], top[:, t, :], lg[:, t, :]).then_inc(topi_s, 1)
                V.tensor_tensor(dlt[:], top[:, :, 1], top[:, :, 0], ALU.subtract).then_inc(dlt_s, 1)
                dve.wait_ge(topi_s, TPB * (b + 1))
                V.tensor_copy(topf[:], topi[:, :, 0:2]).then_inc(topf_s, 1)
                dve.wait_ge(e2_s, b + 1)
                V.tensor_scalar(den[:], e2[:], 1.0, None, ALU.add).then_inc(den_s, 1)
                dve.wait_ge(den_s, b + 1)
                V.reciprocal(wt1[:], den[:]).then_inc(wt1_s, 1)
                dve.wait_ge(wt1_s, b + 1)
                V.tensor_tensor(wt2[:], wt1[:], e2[:], ALU.mult).then_inc(wt2_s, 1)
                dve.wait_ge(topf_s, b + 1)
                dve.wait_ge(wt2_s, b + 1)
                for t in range(TPB):
                    V.tensor_scalar(oh1[:, t, :], iota8[:], topf[:, t, 0:1], wt1[:, t:t + 1], ALU.is_equal, ALU.mult)
                    V.tensor_scalar(oh2[:, t, :], iota8[:], topf[:, t, 1:2], wt2[:, t:t + 1], ALU.is_equal, ALU.mult
                                    ).then_inc(oh_s, 1)
                dve.wait_ge(oh_s, TPB * (b + 1))
                V.tensor_tensor(route[:, tiles(b), :], oh1[:], oh2[:], ALU.add).then_inc(route_s, 1)

            def both(i, r, x):
                j = i - 1
                if r: r_norm1(i)
                if x: x_k(j)
                if r: r_rotate(i)
                if x: x_q(j)
                if x: x_max(j, 0)
                if r: r_gate(i)
                if x: x_probs(j, 0)
                if r: r_decay(i, range(0, 4))
                if x: x_max(j, 1)
                if r: r_decay(i, range(4, 8))
                if x: x_rinv(j)
                if x: x_probs(j, 1)
                if r: r_z(i)
                if r: r_var(i)
                if r: r_vt(i)
                if x: x_u(j)
                if x: x_x2(j)
                if r: r_y(i)
                if x: x_r1(j)
                if r: r_x1(i)
                if x: x_route(j)

            dve.sem_inc(r_by_dve, r_all["dve"])
            dve.sem_inc(x_by_dve, x_all_["dve"])
            dve.sem_inc(f_by_dve, f_all["dve"])
            V.memset(mhalf[:], -0.5)
            V.memset(ones1b[:], 1.0)
            V.memset(ones1[:], 1.0).then_inc(setup, 1)
            dve.wait_ge(ld["wv"], 16)
            wv_heads = w_v[:].rearrange("p k (h j) -> p (k h) j", h=NH)
            V.tensor_reduce(vmean[:].rearrange("p k h -> p (k h)"), wv_heads, AX.X, ALU.add).then_inc(vmean_s, 1)
            dve.wait_ge(vmean_s, 1)
            V.tensor_scalar(vmean[:], vmean[:], 1.0 / DV, None, ALU.mult).then_inc(vmean_s, 1)
            dve.wait_ge(vmean_s, 2)
            for k in range(KD):
                V.tensor_tensor(w_vc[:, k, :].rearrange("p (h j) -> p h j", h=NH),
                                w_v[:, k, :].rearrange("p (h j) -> p h j", h=NH),
                                vmean[:, k, :].unsqueeze(2).to_broadcast([P, NH, DV]), ALU.subtract
                                ).then_inc(wvc_done, 1)
            dve.wait_ge(ld["const"], 16 * 16)
            dve.wait_ge(ld["r"], 32)
            V.tensor_scalar(b_r1h[:], b_r1[:], 0.5, None, ALU.mult)
            V.tensor_scalar(w_r2[:], w_r2[:], 0.5, None, ALU.mult).then_inc(setup2, 1)
            for h in range(NH):
                V.tensor_tensor_scan(DM[:, h, 0:T], dec[:, h:h + 1].to_broadcast([P, T]), delta_sb, 0.0,
                                     ALU.mult, ALU.add).then_inc(dm_scan, 1)
            dve.wait_ge(dm_scan, NH)
            V.tensor_copy(DM[:, :, T:SC], DM[:, :, 0:P]).then_inc(dm_done, 1)
            dve.wait_ge(dm_done, 1)
            dve.wait_ge(ld["x"], 16)
            both(0, True, False)
            dve.wait_ge(ld["x"], 32)
            with dve.Fori(1, B) as i:
                both(i, True, True)
            both(B, False, True)
            dve.drain().then_inc(phase1, 1)

            def f_weights(b):
                dve.wait_ge(f_filled, len(F_ITEMS) * b)
                dve.wait_ge(f_by_dve, f_dve(b, 0))
                V.tensor_copy(rt[:], route[:, tiles(b), :]).then_inc(rt_s, 1)
                dve.wait_ge(rt_s, b + 1)

            def f_bias_sum(b):
                dve.wait_ge(f_filled, f_item(b, F_B))
                xt = x_all[:, tiles(b), :].rearrange("p a d -> p (a d)")
                V.tensor_tensor(xt, psum[:, F_B, :], xt, ALU.add).then_inc(f_by_dve, 1)

            def f_sum(b, e):
                item = F_O[e]
                dve.wait_ge(f_filled, f_item(b, item))
                dve.wait_ge(f_by_dve, f_dve(b, 1 + e))
                for t in range(TPB):
                    xt = tile_of(b)(t)
                    ins = V.scalar_tensor_tensor(xt, psum[:, item % F_RING, t * D:(t + 1) * D], rt[:, t, e:e + 1],
                                                 xt, ALU.mult, ALU.add)
                ins.then_inc(f_by_dve, 1)

            def f_batch(b):
                f_weights(b)
                f_bias_sum(b)
                for e in range(E):
                    f_sum(b, e)

            dve.wait_ge(phase1, 4)
            f_batch(0)
            with dve.Fori(1, B) as b:
                f_batch(b)

        @block.scalar
        def _(act):
            A = nc.scalar

            def copy(dst, src, ring, name=None):
                A.activation(dst, src, ACT.Copy).then_inc({"r": r_by_act, "x": x_by_act, "f": f_by_act}[ring], 1)

            def flat(a):
                return a.rearrange("p c s -> p (c s)")

            def r_xt(b):
                act.wait_ge(r_filled, r_item(b, R_XT))
                copy(flat(xnT[:]), rbank(R_XT), "r")

            def r_v(b):
                for t in range(TPB):
                    act.wait_ge(r_filled, r_item(b, R_V + t))
                    copy(vc[:, t, :], rbank(R_V + t), "r")

            def r_g(b):
                for n in range(2):
                    act.wait_ge(r_filled, r_item(b, R_G + n))
                    A.activation(flat(gth[:, 2 * n:2 * n + 2, :]), rbank(R_G + n), ACT.Tanh, scale=0.5
                                 ).then_inc(th_g, 1)

            def r_qkt(b):
                act.wait_ge(r_filled, r_item(b, R_QT))
                copy(flat(qT[:]), rbank(R_QT), "r")
                act.wait_ge(r_filled, r_item(b, R_KT))
                copy(flat(kT[:]), rbank(R_KT), "r")

            def r_sq(b):
                for n in range(2):
                    act.wait_ge(r_filled, r_item(b, R_O + n))
                    A.activation(flat(sq[:, 2 * n:2 * n + 2, :]), rbank(R_O + n), ACT.Square
                                 ).then_inc(sq_done, 1)

            def r_gt(b):
                act.wait_ge(r_filled, r_item(b, R_GT))
                copy(gr[:], rbank(R_GT)[0:NH, 0:T], "r")

            def r_t2(b):
                act.wait_ge(r_filled, r_item(b, R_T2))
                copy(flat(t2T[:]), rbank(R_T2), "r")

            def x_v(b):
                act.wait_ge(x_filled, x_item(b, X_V))
                for t in range(TPB):
                    ins = A.activation(v2[:, t, :], xbank(X_V)[:, t * D:(t + 1) * D], ACT.Copy,
                                       scale=mcol[:, bass.ds(b * TPB + t, 1)])
                ins.then_inc(x_by_act, 1)

            def x_exp(b, t):
                for r in range(HPG):
                    n = X_S + X_TT * t + r
                    act.wait_ge(nmx_s, HPG * (TPB * b + t) + r + 1)
                    if t:
                        act.wait_ge(x_filled, x_item(b, X_P + r))
                    for g in range(KD):
                        h = g * HPG + r
                        ins = A.activation(pr[:, h, :], xbank(n)[:, g * T:(g + 1) * T], ACT.Exp,
                                           bias=nmx[:, t, h:h + 1], scale=SCALE, accum_out=rsum[:, t, h:h + 1])
                    ins.then_inc(x_by_act, 1)

            def x_probs(b, t):
                for r in (0, 2):
                    n = X_P + X_TT * t + r
                    act.wait_ge(x_filled, x_item(b, n))
                    for s in range(TPB):
                        ins = A.activation(pT[:, s, r::HPG, t * P:(t + 1) * P],
                                           xbank(n)[:, s * 2 * P:(s + 1) * 2 * P].rearrange("p (g t) -> p g t", g=KD),
                                           ACT.Copy)
                    ins.then_inc(x_by_act, 1)

            def x_u(b):
                act.wait_ge(x_filled, x_item(b, X_RS))
                copy(riT[:], xbank(X_RS)[0:NH, 0:T], "x")
                act.wait_ge(x_filled, x_item(b, X_U))
                copy(flat(u_raw[:]), xbank(X_U), "x")

            def x_t3(b):
                act.wait_ge(x_filled, x_item(b, X_T3))
                act.wait_ge(t3_out, 16 * b)
                copy(flat(t3T[:]), xbank(X_T3), "x")

            def x_r1(b):
                act.wait_ge(x_filled, x_item(b, X_R1))
                for g in range(KD):
                    A.activation(r1th[:, g, :], xbank(X_R1)[:, g * T:(g + 1) * T], ACT.Tanh, bias=b_r1h[:, g:g + 1],
                                 scale=0.5)
                    ins = A.activation(r1[:, g, :], xbank(X_R1)[:, g * T:(g + 1) * T], ACT.Identity,
                                       bias=b_r1[:, g:g + 1])
                ins.then_inc(x_by_act, 1)

            def x_route(b):
                act.wait_ge(dlt_s, b + 1)
                A.activation(e2[:], dlt[:], ACT.Exp).then_inc(e2_s, 1)

            def both(i, r, x):
                j = i - 1
                if r: r_xt(i)
                if x: x_v(j)
                if r: r_v(i)
                if x: x_exp(j, 0)
                if r: r_g(i)
                if r: r_qkt(i)
                if x: x_probs(j, 0)
                if x: x_exp(j, 1)
                if x: x_probs(j, 1)
                if r: r_sq(i)
                if x: x_u(j)
                if r: r_gt(i)
                if x: x_t3(j)
                if x: x_r1(j)
                if r: r_t2(i)
                if x: x_route(j)

            act.sem_inc(r_by_act, r_all["act"])
            act.sem_inc(x_by_act, x_all_["act"])
            act.sem_inc(f_by_act, f_all["act"])
            act.wait_ge(ld["const"], 16 * 16)
            act.wait_ge(setup2, 1)
            both(0, True, False)
            with act.Fori(1, B) as i:
                both(i, True, True)
            both(B, False, True)
            act.drain().then_inc(phase1, 1)

            def f_weights(b):
                act.wait_ge(f_filled, f_item(b, F_W))
                copy(wT[:], psum[0:E, F_W, 0:T], "f")

            def f_hidden(b, e):
                if e >= 2:
                    act.wait_ge(f_filled, f_item(b, F_O[e - 2]))
                for n in range(2):
                    item = F_H[e] + n
                    act.wait_ge(f_filled, f_item(b, item))
                    for j in range(2):
                        c = 2 * n + j
                        ins = A.activation(hT[:, e % 2, c, :], psum[:, item % F_RING, j * T:(j + 1) * T], ACT.Silu,
                                           bias=b1[:, e, c:c + 1])
                    ins.then_inc(f_by_act, 1)

            def f_batch(b):
                f_weights(b)
                for e in range(E):
                    f_hidden(b, e)

            act.wait_ge(ld["ffn"], 16 * 4)
            f_batch(0)
            with act.Fori(1, B) as b:
                f_batch(b)

        @block.gpsimd
        def _(pool):
            G = nc.gpsimd

            def root(b, n):
                pool.wait_ge(aggr[n], TPB * (b + 1))
                hold(pool)
                G.tensor_scalar(veps[:], mv[:, :, 1], EPS, None, ALU.add).then_inc(veps_s[n], 1)
                pool.wait_ge(veps_s[n], b + 1)
                G.tensor_tensor(rstd[:], veps[:], mhalf[:, 0:TPB], ALU.pow).then_inc(rstd_s[n], 1)

            def rotate(b):
                for t in range(TPB):
                    pool.wait_ge(r_by_dve, r_dve(b, t + 1))
                    G.tensor_tensor(rot_a[:, t, :], rot_a[:, t, :], rot_b[:, t, :], ALU.add).then_inc(rot, 1)

            def groups(b):
                pool.wait_ge(r_by_dve, r_dve(b, 16))
                G.tensor_tensor(grt[:].rearrange("p t h -> p (t h)"), gvt[:].rearrange("p t h -> p (t h)"),
                                mhalf[:], ALU.pow).then_inc(gr_s, 1)

            def both(i, r, x):
                if r: root(i, 0)
                if r: rotate(i)
                if r: groups(i)
                if x: root(i - 1, 2)
                if r: root(i, 1)

            pool.wait_ge(setup, 1)
            both(0, True, False)
            with pool.Fori(1, B) as i:
                both(i, True, True)
            both(B, False, True)
            pool.drain().then_inc(phase1, 1)

    return nc


def shape_constants():
    import numpy as np

    f = np.float32
    vec = (np.arange(0, D, 2, dtype=f) + f(0.4 * D)) / f(1.4 * D)
    pos = np.arange(T, dtype=f)
    scale = vec[None, :] ** (pos[:, None] / f(512.0))
    half = D // 2
    inv = f(1.0) / f(10000.0) ** (np.arange(half, dtype=f) / f(half))
    ang = pos[:, None] * inv[None, :]
    sin, cos = np.sin(ang), np.cos(ang)
    cs, sn = [], []
    for s in (scale, f(1.0) / scale):
        c = (cos * s).reshape(T, NH, 1, DH // 2)
        n = (sin * s).reshape(T, NH, 1, DH // 2)
        cs.append(np.concatenate([c, c], 2).reshape(T, D))
        sn.append(np.concatenate([-n, n], 2).reshape(T, D))
    rot_c = np.concatenate(cs, 1).reshape(TPB, P, 2 * D).transpose(1, 0, 2)
    rot_s = np.concatenate(sn, 1).reshape(TPB, P, 2 * D).transpose(1, 0, 2)
    delta = (np.arange(P)[:, None] == np.arange(T)).astype(f) * f(DH ** -0.5)
    v = np.arange(512).reshape(KV, P)
    head = v // DV
    sel64 = (head[:, :, None] == np.arange(NH)).astype(f).transpose(1, 0, 2) / f(DV)
    sel8 = (head[None] == np.arange(NH)[:, None, None]).astype(f)
    selh = ((np.arange(D) // DH).reshape(1, KD, P) == np.arange(NH)[:, None, None]).astype(f)
    iota = np.tile(np.arange(E, dtype=f), (P, 1))
    return {"rot_c": rot_c, "rot_s": rot_s, "delta": delta, "ident_in": np.eye(P, dtype=f),
            "sel64_in": sel64, "sel8_in": sel8, "selh_in": selh, "iota_in": iota}


def kernel(**inputs):
    import numpy as np
    import concourse.bacc as bacc
    from concourse import mybir as mb
    from concourse.bass_utils import run_bass_kernel_spmd as run

    a = {k: np.asarray(v) for k, v in inputs.items()}

    def chunks(w):
        return w.reshape(w.shape[0] // P, P, w.shape[1]).transpose(1, 0, 2)

    def halves(w):
        return w.reshape(NH, DH // 2, 2, D).transpose(0, 2, 1, 3).reshape(D, D)

    wqkv = a["L0_attn_w_qkv"]
    wsrc, bsrc = a["L0_xattn_W_src"], a["L0_xattn_b_src"]
    mask = a["mask_BxS2_fk1"]
    arrays = {
        "x": a["x"].reshape(B * T, D),
        "ctxT": a["ctx_2048"].reshape(B, T, KC, P).transpose(0, 3, 2, 1).reshape(B, P, KC * T),
        "maskrow": mask, "maskcol": mask.reshape(NT, P).T,
        "wqkT": chunks(np.concatenate([halves(wqkv[0:D]), halves(wqkv[D:2 * D])], 0).T),
        "wvT": chunks(wqkv[2 * D:].T), "wgT": chunks(a["L0_attn_w_gated"].T), "wpT": chunks(a["L0_attn_w_proj"].T),
        "decay": a["L0_attn_decay"], "wsT": chunks(wsrc.T), "bsk": bsrc[0:D].reshape(KD, P).T,
        "bsv": bsrc[D:].reshape(1, D), "wtT": chunks(a["L0_xattn_W_tgt"].T),
        "bt": a["L0_xattn_b_tgt"].reshape(KD, P).T, "woT": chunks(a["L0_xattn_W_out"].T),
        "bo": a["L0_xattn_b_out"].reshape(1, D), "rw1": chunks(a["L0_ffn_rw1"]),
        "rb1": a["L0_ffn_rb1"].reshape(KD, P).T, "rw2": chunks(a["L0_ffn_rw2"]), "rb2": a["L0_ffn_rb2"].reshape(1, E),
        "ew1": a["L0_ffn_ew1"].reshape(E, KD, P, H).transpose(2, 0, 1, 3),
        "eb1": a["L0_ffn_eb1"].reshape(E, KH, P).transpose(2, 0, 1),
        "ew2": a["L0_ffn_ew2"].reshape(E, KH, P, D).transpose(2, 0, 1, 3), "eb2": a["L0_ffn_eb2"],
        **shape_constants(),
    }
    nc = bacc.Bacc("TRN2", target_bir_lowering=False, num_devices=1)
    feed, args = {}, {}
    for name, v in arrays.items():
        v = np.ascontiguousarray(v)
        feed["in_" + name] = v
        args[name] = nc.dram_tensor("in_" + name, v.shape, mb.dt.from_np(v.dtype), kind="ExternalInput").ap()
    args["out"] = nc.dram_tensor("out", (B * T, D), mb.dt.float32, kind="ExternalOutput").ap()
    build(nc, **args)
    r = run(nc, [feed], core_ids=[0])
    return r.results[0]["out"].reshape(B, T, D)
```

```python
import concourse.bass as bass
from concourse import mybir
from contextlib import ExitStack

B, T, D, CTX = 16, 256, 256, 512
P = 128
NT = B * T // P
TPB = T // P
KD, KC = D // P, CTX // P
NH = 8
DV = 512 // NH
DH = D // NH
HPG = P // DH
KV = 512 // P
E, H = 8, 512
KH = H // P
SC = T + P
EPS = 1e-5
BANK = 512
NEG = -1e30

R_ITEMS = (["act"] + ["dve"] * 3 + ["act"] * 3 + ["dve"] * 5 + ["act"] + ["dve"] * 4 + ["dve"] * 3 + ["act"]
           + ["dve"] * 2)
(R_XT, R_QK, R_G, R_QT, R_KT, R_V, R_S, R_O, R_VAR, R_GT, R_RB) = (
    0, 1, (3, 9), 4, 5, (6, 12), (7, 8, 10, 11, 13, 14, 15, 16), 17, 19, 20, 21)
X_ITEMS = (["act", "dve", "act", "dve"] + ["act"] * 5 + ["act", "dve"] * 2 + ["act"] * 4 + ["act", "dve"] * 2
           + ["act", "act", "dve", "dve", "dve"])
(X_V, X_Y, X_T2, X_Q, X_S, X_P, X_RS, X_U, X_RB, X_O, X_NK) = (
    (0, 5), 1, 2, 3, ((4, 6, 7, 8), (13, 14, 15, 16)), (9, 17), 21, 22, 23, 24, 25)
Z_ITEMS = ["act", "act", "dve", "dve"]
Z_T3, Z_R1, Z_LG, Z_RK = 0, 1, 2, 3
R_BANKS, X_BANKS, Z_BANKS = 3, 4, 1
TOPK = 2
CAP = B * T + P
FT = (TOPK * B * T + E * (P - 1)) // P
FT += FT % 2
ROWS = E * CAP
CB = 8
SCALE = DH ** -0.5


def previous(items, n, ring):
    m = n - ring
    if m < 0:
        m = max(i for i in range(len(items)) if i % ring == n % ring)
        return items[m], items[:m + 1].count(items[m]) - items.count(items[m])
    return items[m], items[:m + 1].count(items[m])


def build(nc, x, ctxT, maskrow, maskcol, wqkT, wvT, wgT, wpT, decay, wsT, bsk, bsv, wtT, bt, woT, bo,
          rw1, rb1, rw2, rb2, ew1, eb1, ew2, eb2, rot_c, rot_s, delta, ident_in, sel64_in, sel8_in,
          selh_in, iota_in, iota_t_in, before_in, base_in, out):
    f32, bf16, u32 = mybir.dt.float32, mybir.dt.bfloat16, mybir.dt.uint32
    ALU = mybir.AluOpType
    ACT = mybir.ActivationFunctionType
    AX = mybir.AxisListType

    x2_dram = nc.dram_tensor("x2_dram", (B * T, D), f32, kind="Internal").ap()
    slot_in = nc.dram_tensor("slot_in", (ROWS, D), f32, kind="Internal").ap()
    slot_out = nc.dram_tensor("slot_out", (FT * P, D), f32, kind="Internal").ap()

    ctx = ExitStack()
    with ctx:
        def sb(name, shape, dt=f32, stack=None):
            return (stack or ctx).enter_context(nc.sbuf_tensor(name, shape, dt))

        def sem(name):
            return ctx.enter_context(nc.semaphore(name))

        psum = ctx.enter_context(nc.psum_tensor("psum", [P, 8, BANK], f32))

        wts = sb("wts", [P, NT, TOPK])
        eid = sb("eid", [P, NT, TOPK])
        rows_in = sb("rows_in", [P, NT, TOPK])
        run = sb("run", [P, E])
        base = sb("base", [P, E])
        zrow = sb("zrow", [P, D])
        b1_bc = sb("b1_bc", [P, E, H])
        b2_bc = sb("b2_bc", [P, E, D])
        ident = sb("ident", [P, P])

        one = ExitStack()

        def s1(name, shape, dt=f32):
            return sb(name, shape, dt, one)

        w_qk = s1("w_qk", [P, KD, 2 * D])
        w_vc = s1("w_vc", [P, KD, 512])
        w_g = s1("w_g", [P, KD, 512])
        w_p = s1("w_p", [P, KV, D])
        w_s = s1("w_s", [P, KC, 2 * D])
        w_t = s1("w_t", [P, KD, D])
        w_o = s1("w_o", [P, 2 * KD, D])
        w_r1 = s1("w_r1", [P, KD, D])
        w_r2 = s1("w_r2", [P, KD, E])
        b_k = s1("b_k", [P, KD])
        b_q = s1("b_q", [P, KD])
        b_r1 = s1("b_r1", [P, KD])
        b_r1h = s1("b_r1h", [P, KD])
        b_v = s1("b_v", [1, D])
        b_o = s1("b_o", [1, D])
        b_r2 = s1("b_r2", [1, E])
        mcol = s1("mcol", [P, NT])
        rc = s1("rc", [P, TPB, 2 * D])
        rs = s1("rs", [P, TPB, 2 * D])
        DM = s1("DM", [P, NH, SC])
        dec = s1("dec", [P, NH])
        sel64 = s1("sel64", [P, KV, NH])
        sel8 = s1("sel8", [NH, KV, P])
        selh = s1("selh", [NH, KD, P])
        ones1 = s1("ones1", [1, P])
        ones1b = s1("ones1b", [P, P], bf16)
        iota8 = s1("iota8", [P, E])
        xa = s1("xa", [P, TPB, D])
        xr = s1("xr", [P, TPB, D])
        xb = s1("xb", [P, TPB, D])
        xc = s1("xc", [P, TPB, D])
        before = s1("before", [P, P], bf16)
        onesb = s1("onesb", [P, P], bf16)
        xn3 = s1("xn3", [P, TPB, D])
        vmean = s1("vmean", [P, KD, NH])

        stats = s1("stats", [P, 3, TPB, 6])
        mv = s1("mv", [P, 3, TPB, 2])
        veps = s1("veps", [P, 3, TPB])
        rstd = s1("rstd", [P, 3, TPB])
        mhalf = s1("mhalf", [P, TPB * NH])
        xn = s1("xn", [P, TPB, D])
        xn2 = s1("xn2", [P, TPB, D])
        xnT = s1("xnT", [P, KD, T])
        rot_a = s1("rot_a", [P, TPB, 2 * D])
        rot_b = s1("rot_b", [P, TPB, 2 * D])
        vc = s1("vc", [P, TPB, 512])
        gate = s1("gate", [P, KV, T])
        qT = s1("qT", [P, KD, T])
        kT = s1("kT", [P, KD, T])
        R = s1("R", [P, NH, SC])
        before_f = R[:, 5, 0:P]
        w_v = R[:, 0:3, :].rearrange("p h s -> p (h s)")[:, 0:KD * 512].rearrange("p (k v) -> p k v", k=KD)
        sq = s1("sq", [P, KV, T])
        gr = s1("gr", [NH, T])
        gvt = s1("gvt", [P, TPB, NH])
        grt = s1("grt", [P, TPB, NH])
        yT = s1("yT", [P, KV, T])
        t2T = s1("t2T", [P, KD, T])

        delta_sb = R[:, 4, 0:T]

        ctx_sb = s1("ctx_sb", [P, KC, T])
        mrow = s1("mrow", [P, T])
        neg = s1("neg", [P, T], bf16)
        k2T = s1("k2T", [P, KD, T])
        q2T = s1("q2T", [P, KD, T])
        v2 = s1("v2", [P, TPB, D])
        mx = s1("mx", [P, 2, NH])
        nmx = s1("nmx", [P, 2, NH])
        rsum = s1("rsum", [P, TPB, NH])
        rinv = s1("rinv", [P, TPB, NH])
        riT = s1("riT", [NH, T])
        pr = s1("pr", [P, NH, T])
        pT = s1("pT", [P, TPB, NH, T])
        u_raw = s1("u_raw", [P, KD, T])
        uT = s1("uT", [P, KD, T])
        t3T = s1("t3T", [P, KD, T])
        r1 = s1("r1", [P, KD, T])
        r1th = s1("r1th", [P, KD, T])
        lg = s1("lg", [P, TPB, E])
        top = s1("top", [P, TPB, E])
        topi = s1("topi", [P, TPB, E], u32)
        topf = s1("topf", [P, TPB, 2])
        dlt = s1("dlt", [P, TPB])
        e2 = s1("e2", [P, TPB])
        den = s1("den", [P, TPB])
        wt = s1("wt", [P, TPB, TOPK])
        oh = s1("oh", [P, TPB, TOPK, E])
        pick = s1("pick", [P, TPB, E], bf16)
        row = s1("row", [P, TPB, E])
        pm = s1("pm", [P, TPB, TOPK, E])
        posf = s1("posf", [P, TPB, TOPK])
        posu = s1("posu", [P, TPB, TOPK], u32)

        one.close()
        two = ctx

        def s2(name, shape, dt=f32):
            return sb(name, shape, dt, two)

        f32r, i32 = mybir.dt.float32r, mybir.dt.int32
        w1 = s2("w1", [P, E, 2, KD * H], f32r)
        w2 = s2("w2", [P, E, 2, KH * D], f32r)
        stage = s2("stage", [P, 2, KD * H])
        xt = s2("xt", [P, 2, D])
        xT = s2("xT", [P, 2, 2, KD * P], f32r)
        hid = s2("hid", [P, 2, H])
        hT = s2("hT", [P, 2, 2, KH * P], f32r)
        yo = s2("yo", [P, 2, D])
        n_sl = s2("n_sl", [P, E])
        n_i = s2("n_i", [P, E], i32)
        n_t = s2("n_t", [P, E])
        cum = s2("cum", [P, E])
        ones_e = s2("ones_e", [P, E])
        past = s2("past", [P, FT, E])
        past_t = s2("past_t", [P, FT, E])
        t_e = s2("t_e", [P, FT])
        t_s = s2("t_s", [P, FT])
        t_ok = s2("t_ok", [P, FT])
        t_row = s2("t_row", [P, FT])
        iota_t = s2("iota_t", [P, FT])
        shift = s2("shift", [P, E])
        part = s2("part", [P, NT * TOPK])
        slots = s2("slots", [P, NT, TOPK], u32)
        tab = s2("tab", [P, 2, FT], i32)
        run_i = s2("run_i", [P, E], i32)
        gi = s2("gi", [P, CB, TOPK], u32)
        g_in = s2("g_in", [P, CB, TOPK, D])
        g_x = stage[:].rearrange("p w (c d) -> p (w c) d", d=D)[:, 0:CB, :]

        ld = {n: sem("ld_" + n) for n in ("x", "const", "wqk", "wv", "wg", "wp", "ws", "wt", "wo", "r", "ffn")}
        r_filled = sem("r_filled")
        x_filled = sem("x_filled")
        r_by_act = sem("r_by_act")
        r_by_dve = sem("r_by_dve")
        x_by_act = sem("x_by_act")
        z_filled = sem("z_filled")
        z_by_act = sem("z_by_act")
        z_by_dve = sem("z_by_dve")
        x_by_dve = sem("x_by_dve")
        dm_scan = sem("dm_scan")
        dm_done = sem("dm_done")
        vmean_s = sem("vmean_s")
        wvc_done = sem("wvc_done")
        setup = sem("setup")
        setup2 = sem("setup2")
        neg_done = sem("neg_done")
        rotab = sem("rotab")
        rot = sem("rot")
        th_g = sem("th_g")
        sq_done = sem("sq_done")
        gr_s = sem("gr_s")
        mx_s = sem("mx_s")
        nmx_s = sem("nmx_s")
        ri_s = sem("ri_s")
        r1_s = sem("r1_s")
        top_s = sem("top_s")
        topi_s = sem("topi_s")
        topf_s = sem("topf_s")
        dlt_s = sem("dlt_s")
        e2_s = sem("e2_s")
        den_s = sem("den_s")
        phase1 = sem("phase1")
        held = sem("held")
        xa_in = sem("xa_in")
        xa_used = sem("xa_used")
        x1_s = sem("x1_s")
        x2_s = sem("x2_s")
        x2_out = sem("x2_out")
        xc_s = sem("xc_s")
        wt_s = sem("wt_s")
        oh_s = sem("oh_s")
        pick_s = sem("pick_s")
        row_s = sem("row_s")
        row2_s = sem("row2_s")
        pm_s = sem("pm_s")
        pos_s = sem("pos_s")
        run_s = sem("run_s")
        scattered = sem("scattered")
        zero_s = sem("zero_s")
        pads_s = sem("pads_s")
        padded = sem("padded")
        n_s = sem("n_s")
        tab_s = sem("tab_s")
        hi_w = sem("hi_w")
        lo_w = sem("lo_w")
        xT_f = sem("xT_f")
        xT_hi = sem("xT_hi")
        xT_lo = sem("xT_lo")
        l1_f = sem("l1_f")
        pre_s = sem("pre_s")
        sil_s = sem("sil_s")
        hT_f = sem("hT_f")
        hT_hi = sem("hT_hi")
        hT_lo = sem("hT_lo")
        l2_f = sem("l2_f")
        y_s = sem("y_s")
        gi_s = sem("gi_s")
        c1_s = sem("c1_s")
        c2_s = sem("c2_s")
        ctx_in = sem("ctx_in")
        mrow_in = sem("mrow_in")
        stat = [sem(f"stat{n}") for n in range(3)]
        aggr = [sem(f"aggr{n}") for n in range(3)]
        veps_s = [sem(f"veps{n}") for n in range(3)]
        rstd_s = [sem(f"rstd{n}") for n in range(3)]
        xn_s = [sem(f"xn{n}") for n in range(3)]
        xt_in = [sem(f"xt_in{n}") for n in range(2)]
        y_out = [sem(f"y_out{n}") for n in range(2)]
        g_done = [sem(f"g_done{n}") for n in range(CB)]
        gx_done = [sem(f"gx_done{n}") for n in range(CB)]
        o_done = [sem(f"o_done{n}") for n in range(CB)]
        st_in = [sem(f"st_in{n}") for n in range(2)]

        r_all = {"act": R_ITEMS.count("act"), "dve": R_ITEMS.count("dve")}
        x_all_ = {"act": X_ITEMS.count("act"), "dve": X_ITEMS.count("dve")}
        z_all = {"act": Z_ITEMS.count("act"), "dve": Z_ITEMS.count("dve")}

        r_by = {"act": r_by_act, "dve": r_by_dve}
        x_by = {"act": x_by_act, "dve": x_by_dve}
        z_by = {"act": z_by_act, "dve": z_by_dve}

        def r_read(b, n):
            return r_by[R_ITEMS[n]], (b + 1) * r_all[R_ITEMS[n]] + R_ITEMS[:n + 1].count(R_ITEMS[n])

        def x_read(b, n):
            return x_by[X_ITEMS[n]], (b + 1) * x_all_[X_ITEMS[n]] + X_ITEMS[:n + 1].count(X_ITEMS[n])

        def z_read(b, n):
            return z_by[Z_ITEMS[n]], (b + 1) * z_all[Z_ITEMS[n]] + Z_ITEMS[:n + 1].count(Z_ITEMS[n])

        def z_item(b, n):
            return b * len(Z_ITEMS) + n + 1

        def r_item(b, n):
            return b * len(R_ITEMS) + n + 1

        def x_item(b, n):
            return (b + 1) * len(X_ITEMS) + n + 1

        def r_free(b, n):
            who, k = previous(R_ITEMS, n, R_BANKS)
            return r_by[who], (b + 1) * r_all[who] + k

        def x_free(b, n):
            who, k = previous(X_ITEMS, n, X_BANKS)
            return x_by[who], (b + 1) * x_all_[who] + k

        def z_free(b, n):
            who, k = previous(Z_ITEMS, n, Z_BANKS)
            return z_by[who], (b + 1) * z_all[who] + k

        def done(i):
            return i + 3

        def hold(eng):
            eng.sem_inc(held, 1)

        def rbank(n):
            return psum[:, n % R_BANKS, :]

        def xbank(n):
            return psum[:, R_BANKS + n % X_BANKS, :]

        zbank = psum[:, R_BANKS + X_BANKS, :]

        def tiles(b):
            return bass.ds(b * TPB, TPB)

        block = ctx.enter_context(nc.Block())

        @block.sync
        def _(sp):
            xv = x.rearrange("(n p) d -> p n d", p=P)

            def load(name, dst, src):
                sp.dma_start(dst, src).then_inc(ld[name], 16)

            def load_x(b):
                sp.dma_start(xa[:], xv[:, tiles(b), :]).then_inc(xa_in, 16)

            load_x(0)
            for dst, src in ((ident, ident_in), (rc, rot_c), (rs, rot_s), (dec, decay.partition_broadcast(P)),
                             (sel64, sel64_in), (sel8, sel8_in), (selh, selh_in), (iota8, iota_in), (before_f, before_in), (base, base_in), (mcol, maskcol),
                             (b_k, bsk), (b_q, bt), (b_r1, rb1), (b_v, bsv), (b_o, bo), (b_r2, rb2)):
                load("const", dst[:], src)
            load("const", delta_sb, delta)
            load("wqk", w_qk[:], wqkT)
            load("wv", w_v, wvT)
            load("wg", w_g[:], wgT)
            load("wp", w_p[:], wpT)
            load("ws", w_s[:], wsT)
            load("wt", w_t[:], wtT)
            load("wo", w_o[:], woT)
            load("r", w_r1[:], rw1)
            load("r", w_r2[:], rw2)

            def context(b):
                sp.dma_start(ctx_sb[:], ctxT[bass.ds(b, 1)].rearrange("a p f -> (a p) f")
                             .rearrange("p (c s) -> p c s", c=KC)).then_inc(ctx_in, 16)
                sp.dma_start(mrow[:], maskrow[bass.ds(b, 1)].rearrange("a s -> (a s)").partition_broadcast(P)
                             ).then_inc(mrow_in, 16)

            def store_x2(b):
                sp.wait_ge(xc_s, b + 1)
                sp.dma_start(x2_dram.rearrange("(n p) d -> p n d", p=P)[:, tiles(b), :], xc[:]).then_inc(x2_out, 16)

            context(0)
            sp.wait_ge(xa_used, 1)
            load_x(1)
            load("ffn", b1_bc[:], eb1.partition_broadcast(P))
            load("ffn", b2_bc[:], eb2.partition_broadcast(P))
            with sp.Fori(1, B - 1) as b:
                sp.wait_ge(x_filled, x_item(b - 1, X_V[1]))
                sp.wait_ge(*x_read(b - 1, X_Q))
                context(b)
                sp.wait_ge(xa_used, b + 1)
                load_x(b + 1)
                store_x2(b - 1)
            sp.wait_ge(x_filled, x_item(B - 2, X_V[1]))
            sp.wait_ge(*x_read(B - 2, X_Q))
            context(B - 1)
            store_x2(B - 2)
            store_x2(B - 1)

            sp.wait_ge(phase1, 4)

            def weights(e):
                sp.dma_start(stage[:, 0, :], ew1[:, bass.ds(e, 1), :].rearrange("p a f -> p (a f)")
                             ).then_inc(st_in[0], 16)
                sp.dma_start(stage[:, 1, :], ew2[:, bass.ds(e, 1), :].rearrange("p a f -> p (a f)")
                             ).then_inc(st_in[1], 16)

            weights(0)
            load("ffn", iota_t[:], iota_t_in)

            sp.wait_ge(pads_s, 1)
            sp.wait_ge(scattered, 16 * TOPK * NT)
            for e in range(E):
                at = sp.value_load(run_i[0:1, e:e + 1], min_val=e * CAP, max_val=e * CAP + B * T)
                sp.dma_start(slot_in[bass.ds(at, P), :], zrow[:]).then_inc(padded, 16)
            with sp.Fori(1, E) as e:
                sp.wait_ge(lo_w, 2 * e)
                weights(e)
            sp.wait_ge(tab_s, 2)
            sp.wait_ge(padded, 16 * E)

            def load_tile(i, slot):
                at = sp.value_load(tab[0:1, 1, bass.ds(i, 1)], min_val=0, max_val=ROWS - P)
                sp.dma_start(xt[:, slot, :], slot_in[bass.ds(at, P), :]).then_inc(xt_in[slot], 16)

            def store_tile(i, slot):
                sp.wait_ge(y_s, done(i))
                sp.dma_start(slot_out[bass.ds(i * P, P), :], yo[:, slot, :]).then_inc(y_out[slot], 16)

            load_tile(0, 0)
            load_tile(1, 1)
            sp.wait_ge(xT_f, done(0))
            load_tile(2, 0)
            sp.wait_ge(xT_f, done(1))
            load_tile(3, 1)
            with sp.Fori(2, FT // 2) as h:
                for slot in range(2):
                    i = 2 * h + slot
                    sp.wait_ge(xT_f, done(i - 2))
                    load_tile(i, slot)
                    store_tile(i - 4, slot)
            for i in range(FT - 4, FT):
                store_tile(i, i % 2)

            x2v = x2_dram.rearrange("(n p) d -> p n d", p=P)
            outv = out.rearrange("(n p) d -> p n d", p=P)

            def load_x2(n, c):
                sp.dma_start(g_x[:, c, :], x2v[:, bass.ds(n, 1), :].rearrange("p a d -> p (a d)")
                             ).then_inc(gx_done[c], 16)

            def store_out(n, c, turn):
                sp.wait_ge(c2_s, n + 1)
                sp.dma_start(outv[:, bass.ds(n, 1), :].rearrange("p a d -> p (a d)"), g_x[:, c, :]
                             ).then_inc(o_done[c], 16)

            sp.wait_ge(x2_out, 16 * B)
            for c in range(CB):
                load_x2(c, c)
            with sp.Fori(1, NT // CB) as m:
                for c in range(CB):
                    store_out(CB * (m - 1) + c, c, m)
                for c in range(CB):
                    sp.wait_ge(o_done[c], 16 * m)
                    load_x2(CB * m + c, c)
            for c in range(CB):
                store_out(NT - CB + c, c, NT // CB)
            for c in range(CB):
                sp.wait_ge(o_done[c], 16 * (NT // CB))

        @block.tensor
        def _(pe):
            def mm(o, l, r, first, last):
                return nc.tensor.matmul(o, l, r, start=first, stop=last)

            def transpose_rows(bank, src, chunks):
                for c in range(chunks):
                    for t in range(TPB):
                        last = nc.tensor.transpose(bank[:, c * T + t * P:c * T + (t + 1) * P],
                                                   src[:, t, c * P:(c + 1) * P], ident[:])
                return last

            def filled(ring, ins):
                ins.then_inc({"r": r_filled, "x": x_filled, "z": z_filled}[ring], 1)

            def r_xt(b):
                pe.wait_ge(xn_s[0], b * TPB + TPB)
                pe.wait_ge(*r_free(b, R_XT))
                filled("r", transpose_rows(rbank(R_XT), xn, KD))

            def r_qk(b):
                pe.wait_ge(*r_read(b, R_XT))
                for t in range(TPB):
                    pe.wait_ge(*r_free(b, R_QK + t))
                    for k in range(KD):
                        last = mm(rbank(R_QK + t), xnT[:, k, t * P:(t + 1) * P], w_qk[:, k, :], k == 0, k == KD - 1)
                    filled("r", last)

            def r_v(b, t, half):
                if half == 0:
                    pe.wait_ge(*r_free(b, R_V[t]))
                last = mm(rbank(R_V[t]), xnT[:, half, t * P:(t + 1) * P], w_vc[:, half, :], half == 0, half == KD - 1)
                if half == KD - 1:
                    filled("r", last)

            def r_g(b, n, half):
                if half == 0:
                    pe.wait_ge(*r_free(b, R_G[n]))
                g = 2 * n + half
                for k in range(KD):
                    last = mm(rbank(R_G[n])[:, half * T:(half + 1) * T], w_g[:, k, g * P:(g + 1) * P],
                              xnT[:, k, :], k == 0, k == KD - 1)
                if half == 1:
                    filled("r", last)

            def r_qkt(b):
                pe.wait_ge(rot, TPB * (b + 1))
                for n in range(2):
                    pe.wait_ge(*r_free(b, R_QT + n))
                    filled("r", transpose_rows(rbank(R_QT + n), rot_a[:, :, n * D:(n + 1) * D], KD))

            def r_scores(b, h):
                if h == 0:
                    pe.wait_ge(*r_read(b, R_KT))
                pe.wait_ge(*r_free(b, R_S[h]))
                g, r = h // HPG, DH * (h % HPG)
                o = rbank(R_S[h])
                mm(o[:, 0:T], kT[r:r + DH, g, 0:P], qT[r:r + DH, g, :], True, True)
                filled("r", mm(o[:, T:SC], kT[r:r + DH, g, P:T], qT[r:r + DH, g, P:T], True, True))

            def r_out(b):
                pe.wait_ge(*r_read(b, R_S[-1]))
                pe.wait_ge(*r_read(b, R_V[1]))
                for n in range(2):
                    pe.wait_ge(*r_free(b, R_O + n))
                    for j in range(2):
                        for half in range(2):
                            h = 2 * (2 * n + j) + half
                            o = rbank(R_O + n)[DV * half:DV * (half + 1), j * T:(j + 1) * T]
                            mm(o, vc[:, 0, h * DV:(h + 1) * DV], R[:, h, 0:T], True, False)
                            last = mm(o[:, P:T], vc[:, 1, h * DV:(h + 1) * DV], R[:, h, T:SC], False, True)
                    filled("r", last)

            def r_var(b):
                pe.wait_ge(sq_done, 2 * (b + 1))
                pe.wait_ge(*r_free(b, R_VAR))
                for t in range(TPB):
                    for g in range(KV):
                        last = mm(rbank(R_VAR)[:, t * NH:(t + 1) * NH], sq[:, g, t * P:(t + 1) * P], sel64[:, g, :],
                                  g == 0, g == KV - 1)
                filled("r", last)

            def r_gt(b):
                pe.wait_ge(gr_s, b + 1)
                pe.wait_ge(*r_free(b, R_GT))
                for t in range(TPB):
                    last = nc.tensor.transpose(rbank(R_GT)[0:NH, t * P:(t + 1) * P], grt[:, t, :], ident[:])
                filled("r", last)

            def r_rb(b):
                pe.wait_ge(*r_read(b, R_GT))
                for n in range(2):
                    pe.wait_ge(*r_free(b, R_RB + n))
                    for j in range(2):
                        last = mm(rbank(R_RB + n)[:, j * T:(j + 1) * T], sel8[:, 2 * n + j, :], gr[:], True, True)
                    filled("r", last)

            def x_y(b):
                pe.wait_ge(*r_read(b, R_RB + 1))
                pe.wait_ge(*x_free(b, X_Y))
                for t in range(TPB):
                    for g in range(KV):
                        last = mm(xbank(X_Y)[:, t * D:(t + 1) * D], yT[:, g, t * P:(t + 1) * P], w_p[:, g, :],
                                  g == 0, g == KV - 1)
                filled("x", last)

            def x_t2(b):
                pe.wait_ge(xn_s[1], TPB * (b + 1))
                pe.wait_ge(*x_free(b, X_T2))
                filled("x", transpose_rows(xbank(X_T2), xn2, KD))

            def x_k(b):
                pe.wait_ge(ctx_in, 16 * (b + 1))
                pe.wait_ge(*x_free(b - 1, X_NK))
                for g in range(KD):
                    for k in range(KC):
                        last = mm(xbank(X_NK)[:, g * T:(g + 1) * T], w_s[:, k, g * P:(g + 1) * P], ctx_sb[:, k, :],
                                  k == 0, k == KC - 1)
                filled("x", last)

            def x_v(b, t):
                pe.wait_ge(*x_free(b, X_V[t]))
                o = xbank(X_V[t])[:, 0:D]
                for k in range(KC):
                    mm(o, ctx_sb[:, k, t * P:(t + 1) * P], w_s[:, k, D:2 * D], k == 0, False)
                filled("x", mm(o, ones1[:], b_v[:], False, True))

            def x_q(b):
                pe.wait_ge(*x_read(b, X_T2))
                pe.wait_ge(*x_free(b, X_Q))
                for g in range(KD):
                    for k in range(KD):
                        last = mm(xbank(X_Q)[:, g * T:(g + 1) * T], w_t[:, k, g * P:(g + 1) * P], t2T[:, k, :],
                                  k == 0, k == KD - 1)
                filled("x", last)

            def x_scores(b, t, r):
                if t == 0 and r == 0:
                    pe.wait_ge(*x_read(b, X_Q))
                    pe.wait_ge(neg_done, b + 1)
                n = X_S[t][r]
                pe.wait_ge(*x_free(b, n))
                o = xbank(n)
                for g in range(KD):
                    mm(o[:, g * T:(g + 1) * T], q2T[DH * r:DH * (r + 1), g, t * P:(t + 1) * P],
                       k2T[DH * r:DH * (r + 1), g, :], True, False)
                    last = mm(o[:, g * T:(g + 1) * T], ones1b[DH * r:DH * r + 1, :], neg[DH * r:DH * r + 1, :],
                              False, True)
                filled("x", last)

            def x_probs(b, t, r):
                n = X_P[t] + r
                pe.wait_ge(*x_read(b, X_S[t][r]))
                pe.wait_ge(*x_free(b, n))
                for s in range(TPB):
                    for g in range(KD):
                        last = nc.tensor.transpose(xbank(n)[:, (s * KD + g) * P:(s * KD + g + 1) * P],
                                                   pr[:, g * HPG + r, s * P:(s + 1) * P], ident[:])
                filled("x", last)

            def x_u(b):
                pe.wait_ge(ri_s, b + 1)
                pe.wait_ge(*x_free(b, X_RS))
                for t in range(TPB):
                    last = nc.tensor.transpose(xbank(X_RS)[0:NH, t * P:(t + 1) * P], rinv[:, t, :], ident[:])
                filled("x", last)
                pe.wait_ge(*x_read(b, X_P[1] + 2))
                pe.wait_ge(*x_read(b, X_P[1] + 3))
                pe.wait_ge(*x_free(b, X_U))
                for h in range(NH):
                    g, r = h // HPG, DH * (h % HPG)
                    for s in range(TPB):
                        last = mm(xbank(X_U)[r:r + DH, g * T:(g + 1) * T], v2[:, s, h * DH:(h + 1) * DH],
                                  pT[:, s, h, :], s == 0, s == TPB - 1)
                filled("x", last)

            def x_rb(b):
                pe.wait_ge(*x_read(b, X_RS))
                pe.wait_ge(*x_free(b, X_RB))
                for g in range(KD):
                    last = mm(xbank(X_RB)[:, g * T:(g + 1) * T], selh[:, g, :], riT[:], True, True)
                filled("x", last)

            def x_out(b):
                pe.wait_ge(*x_read(b, X_RB))
                pe.wait_ge(*x_free(b, X_O))
                for t in range(TPB):
                    o = xbank(X_O)[:, t * D:(t + 1) * D]
                    for k in range(2 * KD):
                        src = t2T if k < KD else uT
                        mm(o, src[:, k % KD, t * P:(t + 1) * P], w_o[:, k, :], k == 0, False)
                    last = mm(o, ones1[:], b_o[:], False, True)
                filled("x", last)

            def z_t3(b):
                pe.wait_ge(xn_s[2], TPB * (b + 1))
                pe.wait_ge(*z_free(b, Z_T3))
                filled("z", transpose_rows(zbank, xn3, KD))

            def z_r1(b):
                pe.wait_ge(*z_read(b, Z_T3))
                pe.wait_ge(*z_free(b, Z_R1))
                for g in range(KD):
                    for k in range(KD):
                        last = mm(zbank[:, g * T:(g + 1) * T], w_r1[:, k, g * P:(g + 1) * P], t3T[:, k, :],
                                  k == 0, k == KD - 1)
                filled("z", last)

            def z_lg(b):
                pe.wait_ge(r1_s, b + 1)
                pe.wait_ge(*z_free(b, Z_LG))
                for t in range(TPB):
                    o = zbank[:, t * E:(t + 1) * E]
                    for k in range(KD):
                        mm(o, r1[:, k, t * P:(t + 1) * P], w_r2[:, k, :], k == 0, False)
                    last = mm(o, ones1[:], b_r2[:], False, True)
                filled("z", last)

            def z_rank(b):
                pe.wait_ge(pick_s, b + 1)
                pe.wait_ge(*z_free(b, Z_RK))
                o = zbank
                mm(o[:, 0:E], before[:], pick[:, 0, :], True, True)
                mm(o[:, E:2 * E], before[:], pick[:, 1, :], True, False)
                mm(o[:, E:2 * E], onesb[:], pick[:, 0, :], False, True)
                mm(o[:, 2 * E:3 * E], onesb[:], pick[:, 0, :], True, False)
                filled("z", mm(o[:, 2 * E:3 * E], onesb[:], pick[:, 1, :], False, True))

            def turn(i, r, x, z):
                j, k = i - 1, i - 2
                if x: x_v(j, 0)
                if x: x_y(j)
                if z: z_t3(k)
                if r: r_xt(i)
                if z: z_r1(k)
                if r: r_qk(i)
                if x: x_t2(j)
                if r: r_g(i, 0, 0)
                if r: r_g(i, 0, 1)
                if x: x_q(j)
                if z: z_lg(k)
                if x: x_scores(j, 0, 0)
                if x: x_v(j, 1)
                if x: x_scores(j, 0, 1)
                if r: r_qkt(i)
                if x: x_scores(j, 0, 2)
                if r: r_v(i, 0, 0)
                if x: x_scores(j, 0, 3)
                if r: r_v(i, 0, 1)
                if r: r_scores(i, 0)
                if x: x_probs(j, 0, 0)
                if r: r_g(i, 1, 0)
                if r: r_scores(i, 1)
                if x: x_probs(j, 0, 1)
                if r: r_g(i, 1, 1)
                if r: r_scores(i, 2)
                if x: x_probs(j, 0, 2)
                if z: z_rank(k)
                if r: r_scores(i, 3)
                if x: x_probs(j, 0, 3)
                if x: x_scores(j, 1, 0)
                if x: x_scores(j, 1, 1)
                if r: r_v(i, 1, 0)
                if x: x_scores(j, 1, 2)
                if x: x_scores(j, 1, 3)
                if r: r_v(i, 1, 1)
                for h in range(4):
                    if r: r_scores(i, 4 + h)
                    if x: x_probs(j, 1, h)
                if r: r_out(i)
                if x: x_u(j)
                if r: r_var(i)
                if x: x_rb(j)
                if x: x_out(j)
                if r: r_gt(i)
                if r: x_k(i)
                if r: r_rb(i)

            for n, k in (("const", 18), ("wqk", 1), ("wv", 1), ("wg", 1), ("wp", 1)):
                pe.wait_ge(ld[n], 16 * k)
            pe.wait_ge(setup, 1)
            pe.wait_ge(wvc_done, KD)
            pe.wait_ge(ld["ws"], 16)
            pe.sem_inc(x_filled, len(X_ITEMS) - 1)
            turn(0, True, False, False)
            for n, k in (("wt", 1), ("wo", 1), ("r", 2)):
                pe.wait_ge(ld[n], 16 * k)
            turn(1, True, True, False)
            with pe.Fori(2, B) as i:
                turn(i, True, True, True)
            turn(B, False, True, True)
            turn(B + 1, False, False, True)
            pe.drain().then_inc(phase1, 1)

            PAIRS = ((0, 0), (0, 1), (1, 0))

            def turn_rows(i, turn, slot):
                pe.wait_ge(xt_in[slot], 16 * (turn + 1))
                pe.wait_ge(xT_lo, done(i - 2))
                for k in range(KD):
                    last = nc.tensor.transpose(psum[:, slot, k * P:(k + 1) * P], xt[:, slot, k * P:(k + 1) * P],
                                               ident[:])
                last.then_inc(xT_f, 1)

            def hidden(i, slot):
                e = pe.value_load(tab[0:1, 0, bass.ds(i, 1)], min_val=0, max_val=E - 1)
                pe.wait_ge(xT_lo, done(i))
                pe.wait_ge(pre_s, done(i - 2))
                for k in range(KD):
                    for n, (a, w) in enumerate(PAIRS):
                        last = mm(psum[:, 2 + slot, :], xT[:, slot, a, k * P:(k + 1) * P],
                                  w1[:, bass.ds(e, 1), w, k * H:(k + 1) * H].rearrange("p a f -> p (a f)"),
                                  k == 0 and n == 0, k == KD - 1 and n == 2)
                last.then_inc(l1_f, 1)

            def turn_hidden(i, slot):
                pe.wait_ge(sil_s, done(i))
                pe.wait_ge(hT_lo, done(i - 2))
                for k in range(KH):
                    last = nc.tensor.transpose(psum[:, 4 + slot, k * P:(k + 1) * P], hid[:, slot, k * P:(k + 1) * P],
                                               ident[:])
                last.then_inc(hT_f, 1)

            def output(i, slot):
                e = pe.value_load(tab[0:1, 0, bass.ds(i, 1)], min_val=0, max_val=E - 1)
                pe.wait_ge(hT_lo, done(i))
                pe.wait_ge(y_s, done(i - 2))
                for k in range(KH):
                    for n, (a, w) in enumerate(PAIRS):
                        last = mm(psum[:, 6 + slot, 0:D], hT[:, slot, a, k * P:(k + 1) * P],
                                  w2[:, bass.ds(e, 1), w, k * D:(k + 1) * D].rearrange("p a f -> p (a f)"),
                                  k == 0 and n == 0, k == KH - 1 and n == 2)
                last.then_inc(l2_f, 1)

            def step(turn, slot, rows=True, out=True, turned=True):
                i = 2 * turn + slot
                hidden(i, slot)
                if turned:
                    turn_hidden(i - 1, 1 - slot)
                if rows:
                    turn_rows(i + 1, turn + slot, 1 - slot)
                if out:
                    output(i - 2, slot)

            pe.sem_inc(xT_f, 2)
            pe.sem_inc(l1_f, 2)
            pe.sem_inc(hT_f, 2)
            pe.sem_inc(l2_f, 2)
            pe.wait_ge(tab_s, 2)
            turn_rows(0, 0, 0)
            pe.wait_ge(lo_w, 2 * E)
            step(0, 0, out=False, turned=False)
            step(0, 1, out=False)
            with pe.Fori(1, FT // 2 - 1) as turn:
                step(turn, 0)
                step(turn, 1)
            step(FT // 2 - 1, 0)
            step(FT // 2 - 1, 1, rows=False)
            turn_hidden(FT - 1, 1)
            output(FT - 2, 0)
            output(FT - 1, 1)

        @block.vector
        def _(dve):
            V = nc.vector

            def norm_stats(b, n, rows):
                hold(dve)
                for t in range(TPB):
                    V.bn_stats(stats[:, n, t, :], rows[:, t, :]).then_inc(stat[n], 1)
                dve.wait_ge(stat[n], TPB * (b + 1))
                hold(dve)
                for t in range(TPB):
                    V.bn_aggr(mv[:, n, t, :], stats[:, n, t, :]).then_inc(aggr[n], 1)

            def norm_rows(b, n, rows, dst):
                dve.wait_ge(rstd_s[n], b + 1)
                for t in range(TPB):
                    V.tensor_scalar(dst[:, t, :], rows[:, t, :], mv[:, n, t, 0:1], rstd[:, n, t:t + 1],
                                    ALU.subtract, ALU.mult).then_inc(xn_s[n], 1)

            def r_norm1a(b):
                dve.wait_ge(xa_in, 16 * (b + 1))
                norm_stats(b, 0, xa)

            def r_norm1b(b):
                if not isinstance(b, int) or b > 0:
                    dve.wait_ge(r_filled, r_item(b - 1, R_XT))
                norm_rows(b, 0, xa, xn)

            def r_rotate(b):
                for t in range(TPB):
                    dve.wait_ge(r_filled, r_item(b, R_QK + t))
                    p = rbank(R_QK + t)
                    V.tensor_tensor(rot_a[:, t, :], p, rc[:, t, :], ALU.mult).then_inc(rotab, 1)
                    pv = p.rearrange("p (h two j) -> p h two j", two=2, j=DH // 2)
                    sv = rs[:, t, :].rearrange("p (h two j) -> p h two j", two=2, j=DH // 2)
                    bv = rot_b[:, t, :].rearrange("p (h two j) -> p h two j", two=2, j=DH // 2)
                    V.tensor_tensor(bv[:, :, 0, :], pv[:, :, 1, :], sv[:, :, 0, :], ALU.mult).then_inc(rotab, 1)
                    V.tensor_tensor(bv[:, :, 1, :], pv[:, :, 0, :], sv[:, :, 1, :], ALU.mult
                                    ).then_inc(r_by_dve, 1)

            def r_gate(b, n):
                dve.wait_ge(th_g, 2 * b + n + 1)
                V.scalar_tensor_tensor(gate[:, 2 * n:2 * n + 2, :].rearrange("p a s -> p (a s)"),
                                       gate[:, 2 * n:2 * n + 2, :].rearrange("p a s -> p (a s)"), 1.0,
                                       rbank(R_G[n]), ALU.add, ALU.mult).then_inc(r_by_dve, 1)

            def r_decay(b, heads):
                for h in heads:
                    dve.wait_ge(r_filled, r_item(b, R_S[h]))
                    V.tensor_tensor(R[:, h, :], rbank(R_S[h])[:, 0:SC], DM[:, h, :], ALU.mult
                                    ).then_inc(r_by_dve, 1)

            def r_z(b):
                for n in range(2):
                    dve.wait_ge(sq_done, 2 * b + n + 1)
                    V.tensor_tensor(gate[:, 2 * n:2 * n + 2, :].rearrange("p a s -> p (a s)"), rbank(R_O + n),
                                    gate[:, 2 * n:2 * n + 2, :].rearrange("p a s -> p (a s)"), ALU.mult
                                    ).then_inc(r_by_dve, 1)

            def r_var(b):
                dve.wait_ge(r_filled, r_item(b, R_VAR))
                V.tensor_scalar(gvt[:].rearrange("p t h -> p (t h)"), rbank(R_VAR)[:, 0:TPB * NH], EPS, 4.0,
                                ALU.add, ALU.mult).then_inc(r_by_dve, 1)

            def r_y(b):
                dve.wait_ge(*r_read(b, R_O + 1))
                for n in range(2):
                    dve.wait_ge(r_filled, r_item(b, R_RB + n))
                    V.tensor_tensor(yT[:, 2 * n:2 * n + 2, :].rearrange("p a s -> p (a s)"), rbank(R_RB + n),
                                    gate[:, 2 * n:2 * n + 2, :].rearrange("p a s -> p (a s)"), ALU.mult
                                    ).then_inc(r_by_dve, 1)

            def x_x1(b):
                dve.wait_ge(x_filled, x_item(b, X_Y))
                dve.wait_ge(xa_used, b + 1)
                V.tensor_tensor(xb[:].rearrange("p t d -> p (t d)"), xbank(X_Y), xr[:].rearrange("p t d -> p (t d)"),
                                ALU.add).then_inc(x_by_dve, 1)
                dve.wait_ge(*x_read(b, X_Y))
                norm_stats(b, 1, xb)

            def x_norm2(b):
                norm_rows(b, 1, xb, xn2)

            def x_k(b):
                dve.wait_ge(x_filled, x_item(b - 1, X_NK))
                dve.wait_ge(mrow_in, 16 * (b + 1))
                V.tensor_scalar(neg[:], mrow[:], 0.0, NEG, ALU.is_equal, ALU.mult).then_inc(neg_done, 1)
                for g in range(KD):
                    ins = V.scalar_tensor_tensor(k2T[:, g, :], xbank(X_NK)[:, g * T:(g + 1) * T], b_k[:, g:g + 1],
                                                 mrow[:], ALU.add, ALU.mult)
                ins.then_inc(x_by_dve, 1)

            def x_q(b):
                dve.wait_ge(x_filled, x_item(b, X_Q))
                for g in range(KD):
                    ins = V.scalar_tensor_tensor(q2T[:, g, :], xbank(X_Q)[:, g * T:(g + 1) * T], b_q[:, g:g + 1],
                                                 mrow[:], ALU.add, ALU.mult)
                ins.then_inc(x_by_dve, 1)

            def x_max(b, t, rs):
                for r in rs:
                    n = X_S[t][r]
                    dve.wait_ge(x_filled, x_item(b, n))
                    V.tensor_reduce(mx[:, t, r::HPG], xbank(n).rearrange("p (g s) -> p g s", g=KD), AX.X, ALU.max
                                    ).then_inc(mx_s, 1)
                    dve.wait_ge(mx_s, HPG * (TPB * b + t) + r + 1)
                    V.tensor_scalar(nmx[:, t, r::HPG], mx[:, t, r::HPG], -SCALE, None, ALU.mult
                                    ).then_inc(nmx_s, 1)

            def x_probs(b, t, r):
                n = X_P[t] + r
                dve.wait_ge(x_filled, x_item(b, n))
                V.tensor_copy(pT[:, :, r::HPG, t * P:(t + 1) * P],
                              xbank(n).rearrange("p (s g t) -> p s g t", s=TPB, g=KD)).then_inc(x_by_dve, 1)

            def x_rinv(b):
                dve.wait_ge(*x_read(b, X_S[1][3]))
                V.reciprocal(rinv[:].rearrange("p t h -> p (t h)"), rsum[:].rearrange("p t h -> p (t h)")
                             ).then_inc(ri_s, 1)

            def x_u(b):
                dve.wait_ge(*x_read(b, X_U))
                dve.wait_ge(x_filled, x_item(b, X_RB))
                V.tensor_tensor(uT[:].rearrange("p g t -> p (g t)"), xbank(X_RB),
                                u_raw[:].rearrange("p g t -> p (g t)"), ALU.mult).then_inc(x_by_dve, 1)

            def x_x2(b):
                dve.wait_ge(x_filled, x_item(b, X_O))
                dve.wait_ge(x2_out, 16 * b)
                flat_c = xc[:].rearrange("p t d -> p (t d)")
                V.tensor_tensor(flat_c, xbank(X_O), xb[:].rearrange("p t d -> p (t d)"), ALU.add
                                ).then_inc(x_by_dve, 1)
                dve.wait_ge(*x_read(b, X_O))
                norm_stats(b, 2, xc)

            def x_norm3(b):
                dve.wait_ge(scattered, 16 * TOPK * TPB * b)
                norm_rows(b, 2, xc, xn3)
                flat_c = xc[:].rearrange("p t d -> p (t d)")
                dve.wait_ge(xn_s[2], TPB * (b + 1))
                V.tensor_tensor(flat_c, flat_c, xn3[:].rearrange("p t d -> p (t d)"), ALU.add).then_inc(xc_s, 1)

            def z_r1(b):
                dve.wait_ge(*z_read(b, Z_R1))
                V.scalar_tensor_tensor(r1[:].rearrange("p g t -> p (g t)"), r1th[:].rearrange("p g t -> p (g t)"), 1.0,
                                       r1[:].rearrange("p g t -> p (g t)"), ALU.add, ALU.mult).then_inc(r1_s, 1)

            def z_route(b):
                dve.wait_ge(z_filled, z_item(b, Z_LG))
                V.tensor_copy(lg[:].rearrange("p t e -> p (t e)"), zbank[:, 0:TPB * E]
                              ).then_inc(z_by_dve, 1)
                dve.wait_ge(*z_read(b, Z_LG))
                hold(dve)
                for t in range(TPB):
                    V.max(top[:, t, :], lg[:, t, :]).then_inc(top_s, 1)
                dve.wait_ge(top_s, TPB * (b + 1))
                hold(dve)
                for t in range(TPB):
                    V.max_index(topi[:, t, :], top[:, t, :], lg[:, t, :]).then_inc(topi_s, 1)
                V.tensor_tensor(dlt[:], top[:, :, 1], top[:, :, 0], ALU.subtract).then_inc(dlt_s, 1)
                dve.wait_ge(topi_s, TPB * (b + 1))
                V.tensor_copy(topf[:], topi[:, :, 0:2]).then_inc(topf_s, 1)

            def z_pick(b):
                dve.wait_ge(topf_s, b + 1)
                for t in range(TPB):
                    for k in range(TOPK):
                        V.tensor_scalar(oh[:, t, k, :], iota8[:], topf[:, t, k:k + 1], None, ALU.is_equal
                                        ).then_inc(oh_s, 1)
                dve.wait_ge(oh_s, TPB * TOPK * (b + 1))
                V.tensor_tensor(pick[:], oh[:, :, 0, :], oh[:, :, 1, :], ALU.add).then_inc(pick_s, 1)
                dve.wait_ge(e2_s, b + 1)
                V.tensor_scalar(den[:], e2[:], 1.0, None, ALU.add).then_inc(den_s, 1)
                dve.wait_ge(den_s, b + 1)
                V.reciprocal(wt[:, :, 0], den[:]).then_inc(wt_s, 1)
                dve.wait_ge(wt_s, 2 * b + 1)
                V.tensor_tensor(wt[:, :, 1], wt[:, :, 0], e2[:], ALU.mult).then_inc(wt_s, 1)
                dve.wait_ge(wt_s, 2 * (b + 1))
                V.tensor_copy(wts[:, tiles(b), :], wt[:])

            def z_slots(b):
                dve.wait_ge(z_filled, z_item(b, Z_RK))
                rank = zbank
                V.tensor_tensor(row[:], rank[:, 0:TPB * E].rearrange("p (t e) -> p t e", t=TPB),
                                run[:].unsqueeze(1).to_broadcast([P, TPB, E]), ALU.add).then_inc(row_s, 1)
                dve.wait_ge(row_s, b + 1)
                V.tensor_tensor(run[:], rank[:, TPB * E:(TPB + 1) * E], run[:], ALU.add).then_inc(z_by_dve, 1)
                V.tensor_tensor(pm[:], oh[:], row[:].unsqueeze(2).to_broadcast([P, TPB, TOPK, E]), ALU.mult
                                ).then_inc(pm_s, 1)
                dve.wait_ge(pm_s, b + 1)
                V.tensor_reduce(posf[:].rearrange("p t k -> p (t k)"), pm[:].rearrange("p t k e -> p (t k) e"), AX.X,
                                ALU.add).then_inc(row2_s, 1)
                dve.wait_ge(row2_s, b + 1)
                dve.wait_ge(scattered, 16 * TOPK * TPB * b)
                V.tensor_copy(posu[:], posf[:]).then_inc(pos_s, 1)
                V.tensor_copy(rows_in[:, tiles(b), :], posf[:])
                V.tensor_copy(eid[:, tiles(b), :], topf[:])

            def turn(i, r, x, z):
                j, k = i - 1, i - 2
                if r: r_norm1a(i)
                if r: r_norm1b(i)
                if x: x_x1(j)
                if x: x_norm2(j)
                if z: z_r1(k)
                if r: r_rotate(i)
                if x: x_q(j)
                if r: r_gate(i, 0)
                if x: x_max(j, 0, (0,))
                if z: z_route(k)
                if x: x_max(j, 0, (1, 2, 3))
                if r: r_decay(i, (0, 1))
                if z: z_pick(k)
                if x: x_probs(j, 0, 1)
                if r: r_gate(i, 1)
                if r: r_decay(i, (2, 3))
                if x: x_probs(j, 0, 3)
                if x: x_max(j, 1, (0, 1))
                if z: z_slots(k)
                if x: x_max(j, 1, (2, 3))
                if r: r_decay(i, (4, 5))
                if x: x_probs(j, 1, 1)
                if r: r_decay(i, (6, 7))
                if x: x_rinv(j)
                if x: x_probs(j, 1, 3)
                if r: r_z(i)
                if r: r_var(i)
                if x: x_u(j)
                if x: x_x2(j)
                if r: x_k(i)
                if r: r_y(i)
                if x: x_norm3(j)

            dve.sem_inc(r_by_dve, r_all["dve"])
            dve.sem_inc(x_by_dve, x_all_["dve"] - 1)
            dve.sem_inc(z_by_dve, z_all["dve"])
            V.memset(mhalf[:], -0.5)
            V.memset(ones1b[:], 1.0)
            V.memset(onesb[:], 1.0)
            V.memset(zrow[:], 0.0).then_inc(zero_s, 1)
            V.memset(ones1[:], 1.0).then_inc(setup, 1)
            dve.wait_ge(ld["wv"], 16)
            V.tensor_reduce(vmean[:].rearrange("p k h -> p (k h)"), w_v.rearrange("p k (h j) -> p (k h) j", h=NH), AX.X,
                            ALU.add).then_inc(vmean_s, 1)
            dve.wait_ge(vmean_s, 1)
            V.tensor_scalar(vmean[:], vmean[:], 1.0 / DV, None, ALU.mult).then_inc(vmean_s, 1)
            dve.wait_ge(vmean_s, 2)
            for k in range(KD):
                V.tensor_tensor(w_vc[:, k, :].rearrange("p (h j) -> p h j", h=NH),
                                w_v[:, k, :].rearrange("p (h j) -> p h j", h=NH),
                                vmean[:, k, :].unsqueeze(2).to_broadcast([P, NH, DV]), ALU.subtract
                                ).then_inc(wvc_done, 1)
            dve.wait_ge(ld["const"], 18 * 16)
            dve.wait_ge(ld["r"], 32)
            V.tensor_copy(run[:], base[:])
            V.tensor_copy(before[:], before_f)
            V.tensor_scalar(b_r1h[:], b_r1[:], 0.5, None, ALU.mult)
            V.tensor_scalar(w_r2[:], w_r2[:], 0.5, None, ALU.mult).then_inc(setup2, 1)
            for h in range(NH):
                V.tensor_tensor_scan(DM[:, h, 0:T], dec[:, h:h + 1].to_broadcast([P, T]), delta_sb, 0.0,
                                     ALU.mult, ALU.add).then_inc(dm_scan, 1)
            dve.wait_ge(dm_scan, NH)
            V.tensor_copy(DM[:, :, T:SC], DM[:, :, 0:P]).then_inc(dm_done, 1)
            dve.wait_ge(dm_done, 1)
            turn(0, True, False, False)
            turn(1, True, True, False)
            with dve.Fori(2, B) as i:
                turn(i, True, True, True)
            turn(B, False, True, True)
            turn(B + 1, False, False, True)
            dve.drain().then_inc(phase1, 1)

            steps = [0]

            def after(ins):
                steps[0] += 1
                ins.then_inc(n_s, 1)
                dve.wait_ge(n_s, steps[0])

            for count in (xT_lo, pre_s, hT_lo, y_s):
                dve.sem_inc(count, 2)
            dve.wait_ge(phase1, 4)
            V.tensor_copy(run_i[:], run[:]).then_inc(pads_s, 1)
            V.memset(ones_e[:], 1.0)
            after(V.tensor_tensor(n_sl[:], run[:], base[:], ALU.subtract))
            after(V.tensor_scalar(n_i[:], n_sl[:], float(P - 1), None, ALU.add))
            after(V.tensor_scalar(n_i[:], n_i[:], P.bit_length() - 1, None, ALU.logical_shift_right))
            after(V.tensor_copy(n_t[:], n_i[:]))
            after(V.tensor_tensor_scan(cum[:], ones_e[:], n_t[:], 0.0, ALU.mult, ALU.add))
            dve.wait_ge(ld["ffn"], 16 * 3)
            after(V.tensor_tensor(past[:], iota_t[:].unsqueeze(2).to_broadcast([P, FT, E]),
                                  cum[:].unsqueeze(1).to_broadcast([P, FT, E]), ALU.is_ge))
            after(V.tensor_reduce(t_e[:], past[:], AX.X, ALU.add))
            after(V.tensor_tensor(past_t[:], past[:], n_t[:].unsqueeze(1).to_broadcast([P, FT, E]), ALU.mult))
            after(V.tensor_reduce(t_s[:], past_t[:], AX.X, ALU.add))
            after(V.tensor_scalar(t_ok[:], t_e[:], float(E), None, ALU.is_lt))
            after(V.tensor_tensor(t_row[:], iota_t[:], t_s[:], ALU.subtract))
            after(V.tensor_scalar(t_row[:], t_row[:], float(P), None, ALU.mult))
            after(V.scalar_tensor_tensor(t_row[:], t_e[:], float(CAP), t_row[:], ALU.mult, ALU.add))
            V.tensor_tensor(tab[:, 0, :], t_e[:], t_ok[:], ALU.mult).then_inc(tab_s, 1)
            V.tensor_tensor(tab[:, 1, :], t_row[:], t_ok[:], ALU.mult).then_inc(tab_s, 1)
            after(V.tensor_tensor(shift[:], cum[:], n_t[:], ALU.subtract))
            after(V.tensor_scalar(shift[:], shift[:], float(P), None, ALU.mult))
            after(V.tensor_tensor(shift[:], shift[:], base[:], ALU.subtract))
            rows_flat = rows_in[:].rearrange("p n k -> p (n k)")
            for e in range(E):
                after(V.tensor_scalar(part[:], eid[:].rearrange("p n k -> p (n k)"), float(e), shift[:, e:e + 1],
                                      ALU.is_equal, ALU.mult))
                after(V.tensor_tensor(rows_flat, rows_flat, part[:], ALU.add))
            V.tensor_copy(slots[:].rearrange("p n k -> p (n k)"), rows_flat).then_inc(tab_s, 1)

            def low_weights(e):
                dve.wait_ge(hi_w, 2 * (e + 1))
                for n, w in enumerate((w1, w2)):
                    V.tensor_tensor(w[:, bass.ds(e, 1), 1, :].rearrange("p a f -> p (a f)"), stage[:, n, :],
                                    w[:, bass.ds(e, 1), 0, :].rearrange("p a f -> p (a f)").bitcast(f32),
                                    ALU.subtract).then_inc(lo_w, 1)

            with dve.Fori(0, E) as e:
                low_weights(e)

            def low_rows(i, slot):
                dve.wait_ge(xT_hi, done(i))
                V.tensor_tensor(xT[:, slot, 1, :], psum[:, slot, 0:KD * P], xT[:, slot, 0, :].bitcast(f32),
                                ALU.subtract).then_inc(xT_lo, 1)

            def add_bias(i, slot):
                e = dve.value_load(tab[0:1, 0, bass.ds(i, 1)], min_val=0, max_val=E - 1)
                dve.wait_ge(l1_f, done(i))
                V.tensor_tensor(hid[:, slot, :], psum[:, 2 + slot, :],
                                b1_bc[:, bass.ds(e, 1), :].rearrange("p a f -> p (a f)"), ALU.add).then_inc(pre_s, 1)

            def low_hidden(i, slot):
                dve.wait_ge(hT_hi, done(i))
                V.tensor_tensor(hT[:, slot, 1, :], psum[:, 4 + slot, :], hT[:, slot, 0, :].bitcast(f32),
                                ALU.subtract).then_inc(hT_lo, 1)

            def output(i, turn, slot):
                e = dve.value_load(tab[0:1, 0, bass.ds(i, 1)], min_val=0, max_val=E - 1)
                dve.wait_ge(l2_f, done(i))
                dve.wait_ge(y_out[slot], 16 * turn)
                V.tensor_tensor(yo[:, slot, :], psum[:, 6 + slot, 0:D],
                                b2_bc[:, bass.ds(e, 1), :].rearrange("p a f -> p (a f)"), ALU.add).then_inc(y_s, 1)

            def step(turn, slot, rows=True, out=True, turned=True):
                i = 2 * turn + slot
                add_bias(i, slot)
                if turned:
                    low_hidden(i - 1, 1 - slot)
                if rows:
                    low_rows(i + 1, 1 - slot)
                if out:
                    output(i - 2, turn - 1, slot)

            dve.wait_ge(tab_s, 2)
            low_rows(0, 0)
            step(0, 0, out=False, turned=False)
            step(0, 1, out=False)
            with dve.Fori(1, FT // 2 - 1) as turn:
                step(turn, 0)
                step(turn, 1)
            step(FT // 2 - 1, 0)
            step(FT // 2 - 1, 1, rows=False)
            low_hidden(FT - 1, 1)
            output(FT - 2, FT // 2 - 1, 0)
            output(FT - 1, FT // 2 - 1, 1)

            def combine(turn):
                for c in range(CB):
                    n = CB * turn + c
                    dve.wait_ge(g_done[c], 16 * TOPK * (turn + 1))
                    dve.wait_ge(gx_done[c], 16 * (turn + 1))
                    for k, count in ((0, c1_s), (1, c2_s)):
                        if k:
                            dve.wait_ge(c1_s, n + 1)
                        V.scalar_tensor_tensor(g_x[:, c, :], g_in[:, c, k, :],
                                               wts[:, bass.ds(n, 1), k:k + 1].rearrange("p a k -> p (a k)"),
                                               g_x[:, c, :], ALU.mult, ALU.add).then_inc(count, 1)

            combine(0)
            with dve.Fori(1, NT // CB) as turn:
                combine(turn)

        @block.scalar
        def _(act):
            A = nc.scalar

            def copy(dst, src, ring, name=None):
                A.activation(dst, src, ACT.Copy).then_inc({"r": r_by_act, "x": x_by_act, "z": z_by_act}[ring], 1)

            def flat(a):
                return a.rearrange("p c s -> p (c s)")

            def r_xt(b):
                act.wait_ge(r_filled, r_item(b, R_XT))
                copy(flat(xnT[:]), rbank(R_XT), "r")

            def r_v(b, t):
                act.wait_ge(r_filled, r_item(b, R_V[t]))
                copy(vc[:, t, :], rbank(R_V[t]), "r")

            def r_g(b, n):
                act.wait_ge(r_filled, r_item(b, R_G[n]))
                A.activation(flat(gate[:, 2 * n:2 * n + 2, :]), rbank(R_G[n]), ACT.Tanh, scale=0.5).then_inc(th_g, 1)

            def r_qkt(b):
                act.wait_ge(r_filled, r_item(b, R_QT))
                copy(flat(qT[:]), rbank(R_QT), "r")
                act.wait_ge(r_filled, r_item(b, R_KT))
                copy(flat(kT[:]), rbank(R_KT), "r")

            def r_sq(b):
                for n in range(2):
                    act.wait_ge(r_filled, r_item(b, R_O + n))
                    A.activation(flat(sq[:, 2 * n:2 * n + 2, :]), rbank(R_O + n), ACT.Square
                                 ).then_inc(sq_done, 1)

            def r_gt(b):
                act.wait_ge(r_filled, r_item(b, R_GT))
                copy(gr[:], rbank(R_GT)[0:NH, 0:T], "r")

            def x_t2(b):
                act.wait_ge(x_filled, x_item(b, X_T2))
                copy(flat(t2T[:]), xbank(X_T2), "x")

            def x_v(b, t):
                act.wait_ge(x_filled, x_item(b, X_V[t]))
                A.activation(v2[:, t, :], xbank(X_V[t])[:, 0:D], ACT.Copy, scale=mcol[:, bass.ds(b * TPB + t, 1)]
                             ).then_inc(x_by_act, 1)

            def x_exp(b, t, r):
                n = X_S[t][r]
                act.wait_ge(nmx_s, HPG * (TPB * b + t) + r + 1)
                if t:
                    act.wait_ge(x_filled, x_item(b, X_P[0] + r))
                for g in range(KD):
                    h = g * HPG + r
                    ins = A.activation(pr[:, h, :], xbank(n)[:, g * T:(g + 1) * T], ACT.Exp,
                                       bias=nmx[:, t, h:h + 1], scale=SCALE, accum_out=rsum[:, t, h:h + 1])
                ins.then_inc(x_by_act, 1)

            def x_probs(b, t, r):
                n = X_P[t] + r
                act.wait_ge(x_filled, x_item(b, n))
                for s in range(TPB):
                    ins = A.activation(pT[:, s, r::HPG, t * P:(t + 1) * P],
                                       xbank(n)[:, s * 2 * P:(s + 1) * 2 * P].rearrange("p (g t) -> p g t", g=KD),
                                       ACT.Copy)
                ins.then_inc(x_by_act, 1)

            def x_u(b):
                act.wait_ge(x_filled, x_item(b, X_RS))
                copy(riT[:], xbank(X_RS)[0:NH, 0:T], "x")
                act.wait_ge(x_filled, x_item(b, X_U))
                copy(flat(u_raw[:]), xbank(X_U), "x")

            def z_t3(b):
                act.wait_ge(z_filled, z_item(b, Z_T3))
                copy(flat(t3T[:]), zbank, "z")

            def z_r1(b):
                act.wait_ge(z_filled, z_item(b, Z_R1))
                for g in range(KD):
                    A.activation(r1th[:, g, :], zbank[:, g * T:(g + 1) * T], ACT.Tanh, bias=b_r1h[:, g:g + 1],
                                 scale=0.5)
                    ins = A.activation(r1[:, g, :], zbank[:, g * T:(g + 1) * T], ACT.Identity,
                                       bias=b_r1[:, g:g + 1])
                ins.then_inc(z_by_act, 1)

            def z_route(b):
                act.wait_ge(dlt_s, b + 1)
                A.activation(e2[:], dlt[:], ACT.Exp).then_inc(e2_s, 1)

            def turn(i, r, x, z):
                j, k = i - 1, i - 2
                if x: x_v(j, 0)
                if z: z_t3(k)
                if r: r_xt(i)
                if z: z_r1(k)
                if x: x_t2(j)
                if r: r_g(i, 0)
                if x: x_exp(j, 0, 0)
                if x: x_v(j, 1)
                if r: r_qkt(i)
                if x: x_exp(j, 0, 1)
                if x: x_exp(j, 0, 2)
                if r: r_v(i, 0)
                if x: x_exp(j, 0, 3)
                if z: z_route(k)
                if x: x_probs(j, 0, 0)
                if r: r_g(i, 1)
                if x: x_probs(j, 0, 2)
                if x: x_exp(j, 1, 0)
                if x: x_exp(j, 1, 1)
                if x: x_exp(j, 1, 2)
                if r: r_v(i, 1)
                if x: x_exp(j, 1, 3)
                if x: x_probs(j, 1, 0)
                if x: x_probs(j, 1, 2)
                if r: r_sq(i)
                if x: x_u(j)
                if r: r_gt(i)

            act.sem_inc(r_by_act, r_all["act"])
            act.sem_inc(x_by_act, x_all_["act"])
            act.sem_inc(z_by_act, z_all["act"])
            act.wait_ge(ld["const"], 18 * 16)
            act.wait_ge(setup2, 1)
            turn(0, True, False, False)
            turn(1, True, True, False)
            with act.Fori(2, B) as i:
                turn(i, True, True, True)
            turn(B, False, True, True)
            turn(B + 1, False, False, True)
            act.drain().then_inc(phase1, 1)

            act.sem_inc(xT_hi, 2)
            act.sem_inc(sil_s, 2)
            act.sem_inc(hT_hi, 2)
            act.wait_ge(phase1, 4)

            def high_weights(e):
                for n, w in enumerate((w1, w2)):
                    act.wait_ge(st_in[n], 16 * (e + 1))
                    A.activation(w[:, bass.ds(e, 1), 0, :].rearrange("p a f -> p (a f)"), stage[:, n, :], ACT.Copy
                                 ).then_inc(hi_w, 1)

            with act.Fori(0, E) as e:
                high_weights(e)

            def high_rows(i, slot):
                act.wait_ge(xT_f, done(i))
                act.wait_ge(l1_f, done(i - 2))
                A.activation(xT[:, slot, 0, :], psum[:, slot, 0:KD * P], ACT.Copy).then_inc(xT_hi, 1)

            def silu(i, slot):
                act.wait_ge(pre_s, done(i))
                A.activation(hid[:, slot, :], hid[:, slot, :], ACT.Silu).then_inc(sil_s, 1)

            def high_hidden(i, slot):
                act.wait_ge(hT_f, done(i))
                act.wait_ge(l2_f, done(i - 2))
                A.activation(hT[:, slot, 0, :], psum[:, 4 + slot, :], ACT.Copy).then_inc(hT_hi, 1)

            def step(turn, slot, rows=True, turned=True):
                i = 2 * turn + slot
                silu(i, slot)
                if turned:
                    high_hidden(i - 1, 1 - slot)
                if rows:
                    high_rows(i + 1, 1 - slot)

            high_rows(0, 0)
            step(0, 0, turned=False)
            step(0, 1)
            with act.Fori(1, FT // 2 - 1) as turn:
                step(turn, 0)
                step(turn, 1)
            step(FT // 2 - 1, 0)
            step(FT // 2 - 1, 1, rows=False)
            high_hidden(FT - 1, 1)

        @block.gpsimd
        def _(pool):
            G = nc.gpsimd

            def root(b, n):
                pool.wait_ge(aggr[n], TPB * (b + 1))
                hold(pool)
                G.tensor_scalar(veps[:, n, :], mv[:, n, :, 1], EPS, None, ALU.add).then_inc(veps_s[n], 1)
                pool.wait_ge(veps_s[n], b + 1)
                G.tensor_tensor(rstd[:, n, :], veps[:, n, :], mhalf[:, 0:TPB], ALU.pow).then_inc(rstd_s[n], 1)

            def rotate(b):
                for t in range(TPB):
                    pool.wait_ge(*r_read(b, R_QK + t))
                    G.tensor_tensor(rot_a[:, t, :], rot_a[:, t, :], rot_b[:, t, :], ALU.add).then_inc(rot, 1)

            def groups(b):
                pool.wait_ge(*r_read(b, R_VAR))
                G.tensor_tensor(grt[:].rearrange("p t h -> p (t h)"), gvt[:].rearrange("p t h -> p (t h)"),
                                mhalf[:], ALU.pow).then_inc(gr_s, 1)

            def keep_x(b):
                pool.wait_ge(xn_s[0], TPB * (b + 1))
                if not isinstance(b, int) or b > 0:
                    pool.wait_ge(*x_read(b - 1, X_Y))
                hold(pool)
                G.tensor_copy(xr[:], xa[:]).then_inc(xa_used, 1)

            def scatter(b):
                pool.wait_ge(pos_s, b + 1)
                hold(pool)
                for t in range(TPB):
                    for k in range(TOPK):
                        G.indirect_dma_start(slot_in[:, :], bass.IndirectOffsetOnAxis(ap=posu[:, t, k:k + 1], axis=0),
                                             xn3[:, t, :], None).then_inc(scattered, 16)

            def turn(i, r, x, z):
                if r: root(i, 0)
                if x: root(i - 1, 1)
                if r: keep_x(i)
                if r: rotate(i)
                if z: scatter(i - 2)
                if r: groups(i)
                if x: root(i - 1, 2)

            pool.wait_ge(setup, 1)
            turn(0, True, False, False)
            turn(1, True, True, False)
            with pool.Fori(2, B) as i:
                turn(i, True, True, True)
            turn(B, False, True, True)
            turn(B + 1, False, False, True)
            pool.drain().then_inc(phase1, 1)

            def gather(turn):
                if not isinstance(turn, int):
                    for c in range(CB):
                        pool.wait_ge(g_done[c], 16 * TOPK * turn)
                hold(pool)
                G.tensor_copy(gi[:], slots[:, bass.ds(CB * turn, CB), :]).then_inc(gi_s, 1)
                for c in range(CB):
                    pool.wait_ge(gi_s, turn + 1)
                    if not isinstance(turn, int):
                        pool.wait_ge(c2_s, CB * (turn - 1) + c + 1)
                    hold(pool)
                    for k in range(TOPK):
                        G.indirect_dma_start(g_in[:, c, k, :], None, slot_out[:, :],
                                             bass.IndirectOffsetOnAxis(ap=gi[:, c, k:k + 1], axis=0)
                                             ).then_inc(g_done[c], 16)

            pool.wait_ge(tab_s, 3)
            for slot in range(2):
                pool.wait_ge(y_out[slot], 16 * (FT // 2))
            gather(0)
            with pool.Fori(1, NT // CB) as turn:
                gather(turn)

    return nc


def shape_constants():
    import numpy as np

    f = np.float32
    vec = (np.arange(0, D, 2, dtype=f) + f(0.4 * D)) / f(1.4 * D)
    pos = np.arange(T, dtype=f)
    scale = vec[None, :] ** (pos[:, None] / f(512.0))
    half = D // 2
    inv = f(1.0) / f(10000.0) ** (np.arange(half, dtype=f) / f(half))
    ang = pos[:, None] * inv[None, :]
    sin, cos = np.sin(ang), np.cos(ang)
    cs, sn = [], []
    for s in (scale, f(1.0) / scale):
        c = (cos * s).reshape(T, NH, 1, DH // 2)
        n = (sin * s).reshape(T, NH, 1, DH // 2)
        cs.append(np.concatenate([c, c], 2).reshape(T, D))
        sn.append(np.concatenate([-n, n], 2).reshape(T, D))
    rot_c = np.concatenate(cs, 1).reshape(TPB, P, 2 * D).transpose(1, 0, 2)
    rot_s = np.concatenate(sn, 1).reshape(TPB, P, 2 * D).transpose(1, 0, 2)
    delta = (np.arange(P)[:, None] == np.arange(T)).astype(f) * f(DH ** -0.5)
    v = np.arange(512).reshape(KV, P)
    head = v // DV
    sel64 = (head[:, :, None] == np.arange(NH)).astype(f).transpose(1, 0, 2) / f(DV)
    sel8 = (head[None] == np.arange(NH)[:, None, None]).astype(f)
    selh = ((np.arange(D) // DH).reshape(1, KD, P) == np.arange(NH)[:, None, None]).astype(f)
    iota = np.tile(np.arange(E, dtype=f), (P, 1))
    return {"rot_c": rot_c, "rot_s": rot_s, "delta": delta, "ident_in": np.eye(P, dtype=f),
            "sel64_in": sel64, "sel8_in": sel8, "selh_in": selh, "iota_in": iota,
            "iota_t_in": np.tile(np.arange(FT, dtype=f), (P, 1)),
            "before_in": np.triu(np.ones((P, P), f), 1),
            "base_in": np.tile(np.arange(E, dtype=f) * f(CAP), (P, 1))}


def kernel(**inputs):
    import numpy as np
    import concourse.bacc as bacc
    from concourse import mybir as mb
    from concourse.bass_utils import run_bass_kernel_spmd as run

    a = {k: np.asarray(v) for k, v in inputs.items()}

    def chunks(w):
        return w.reshape(w.shape[0] // P, P, w.shape[1]).transpose(1, 0, 2)

    def halves(w):
        return w.reshape(NH, DH // 2, 2, D).transpose(0, 2, 1, 3).reshape(D, D)

    wqkv = a["L0_attn_w_qkv"]
    wsrc, bsrc = a["L0_xattn_W_src"], a["L0_xattn_b_src"]
    mask = a["mask_BxS2_fk1"]
    arrays = {
        "x": a["x"].reshape(B * T, D),
        "ctxT": a["ctx_2048"].reshape(B, T, KC, P).transpose(0, 3, 2, 1).reshape(B, P, KC * T),
        "maskrow": mask, "maskcol": mask.reshape(NT, P).T,
        "wqkT": chunks(np.concatenate([halves(wqkv[0:D]), halves(wqkv[D:2 * D])], 0).T),
        "wvT": chunks(wqkv[2 * D:].T), "wgT": chunks(a["L0_attn_w_gated"].T), "wpT": chunks(a["L0_attn_w_proj"].T),
        "decay": a["L0_attn_decay"], "wsT": chunks(wsrc.T), "bsk": bsrc[0:D].reshape(KD, P).T,
        "bsv": bsrc[D:].reshape(1, D), "wtT": chunks(a["L0_xattn_W_tgt"].T),
        "bt": a["L0_xattn_b_tgt"].reshape(KD, P).T, "woT": chunks(a["L0_xattn_W_out"].T),
        "bo": a["L0_xattn_b_out"].reshape(1, D), "rw1": chunks(a["L0_ffn_rw1"]),
        "rb1": a["L0_ffn_rb1"].reshape(KD, P).T, "rw2": chunks(a["L0_ffn_rw2"]), "rb2": a["L0_ffn_rb2"].reshape(1, E),
        "ew1": a["L0_ffn_ew1"].reshape(E, KD, P, H).transpose(2, 0, 1, 3).reshape(P, E, KD * H),
        "eb1": a["L0_ffn_eb1"],
        "ew2": a["L0_ffn_ew2"].reshape(E, KH, P, D).transpose(2, 0, 1, 3).reshape(P, E, KH * D), "eb2": a["L0_ffn_eb2"],
        **shape_constants(),
    }
    nc = bacc.Bacc("TRN2", target_bir_lowering=False, num_devices=1)
    feed, args = {}, {}
    for name, v in arrays.items():
        v = np.ascontiguousarray(v)
        feed["in_" + name] = v
        args[name] = nc.dram_tensor("in_" + name, v.shape, mb.dt.from_np(v.dtype), kind="ExternalInput").ap()
    args["out"] = nc.dram_tensor("out", (B * T, D), mb.dt.float32, kind="ExternalOutput").ap()
    build(nc, **args)
    r = run(nc, [feed], core_ids=[0])
    return r.results[0]["out"].reshape(B, T, D)
```

```python
import concourse.bass as bass
from concourse import mybir
from contextlib import ExitStack

B, T, D, CTX = 16, 256, 256, 512
P = 128
NT = B * T // P
TPB = T // P
KD, KC = D // P, CTX // P
NH = 8
DV = 512 // NH
DH = D // NH
HPG = P // DH
KV = 512 // P
E, H = 8, 512
KH = H // P
SC = T + P
EPS = 1e-5
BANK = 512
NEG = -1e30

R_ITEMS = (["dve"] * 4 + ["act"] * 2 + ["dve", "act"] + ["dve"] * 4 + ["act"] + ["dve"] * 4 + ["dve"] * 3 + ["act"]
           + [None] + ["dve"] * 2)
(R_XT, R_QK, R_G, R_QT, R_KT, R_V, R_S, R_O, R_VAR, R_GT, R_RB) = (
    0, 1, (3, 11), 4, 5, (7, 12), (6, 8, 9, 10, 13, 14, 15, 16), 17, 19, 20, 22)
X_ITEMS = (["dve"] * 3 + ["act"] * 5 + ["act", "dve"] * 2 + ["act"] * 4 + ["act", "dve"] * 2
           + ["act", "act", "dve", "dve", "dve", "act"])
(X_Y, X_T2, X_Q, X_S, X_V1, X_P, X_RS, X_U, X_RB, X_NK, X_O, X_NV) = (
    0, 1, 2, ((4, 5, 6, 7), (12, 13, 14, 15)), 3, (8, 16), 20, 21, 22, 23, 24, 25)
Z_ITEMS = ["act", "act", "dve", "dve"]
Z_T3, Z_R1, Z_LG, Z_RK = 0, 1, 2, 3
R_BANKS, X_BANKS, Z_BANKS = 3, 4, 1
TOPK = 2
CAP = B * T + P
FT = (TOPK * B * T + E * (P - 1)) // P
FT += -FT % 4
CONSTS = 17
EARLY = 4
ROWS = E * CAP + P
C_ID, C_W, C_E, ROW = D, D + 1, D + 3, D + 4
SCALE = DH ** -0.5


def previous(items, n, ring):
    before = [i for i in range(n) if i % ring == n % ring and items[i]]
    if before:
        m = before[-1]
        return items[m], items[:m + 1].count(items[m])
    m = max(i for i in range(len(items)) if i % ring == n % ring and items[i])
    return items[m], items[:m + 1].count(items[m]) - items.count(items[m])


def number(items, n):
    return n + 1 - items[:n + 1].count(None)


def build(nc, x, ctxT, maskrow, maskcol, wqkT, wvT, wgT, wpT, decay, wsT, bsk, bsv, wtT, bt, woT, bo,
          rw1, rb1, rw2, rb2, ew1, eb1, ew2, eb2, rot_c, rot_s, delta, ident_in, sel64_in, sel8_in,
          selh_in, iota_in, iota_t_in, before_in, base_in, pad_in, ids_in, parity_in, out):
    f32, bf16, u32 = mybir.dt.float32, mybir.dt.bfloat16, mybir.dt.uint32
    f32r, i32 = mybir.dt.float32r, mybir.dt.int32
    ALU = mybir.AluOpType
    ACT = mybir.ActivationFunctionType
    AX = mybir.AxisListType

    slot_in = nc.dram_tensor("slot_in", (ROWS, ROW), f32, kind="Internal").ap()

    ctx = ExitStack()
    with ctx:
        def sb(name, shape, dt=f32, stack=None):
            return (stack or ctx).enter_context(nc.sbuf_tensor(name, shape, dt))

        def sem(name):
            return ctx.enter_context(nc.semaphore(name))

        psum = ctx.enter_context(nc.psum_tensor("psum", [P, 8, BANK], f32))

        run = sb("run", [P, E])
        base = sb("base", [P, E])
        pad = sb("pad", [P, ROW])
        iota_t = sb("iota_t", [P, FT])
        parity = sb("parity", [P, FT])
        n_sl = sb("n_sl", [P, E])
        n_i = sb("n_i", [P, E], i32)
        n_t = sb("n_t", [P, E])
        cum = sb("cum", [P, E])
        ones_e = sb("ones_e", [P, E])
        past = sb("past", [P, FT, E])
        past_t = sb("past_t", [P, FT, E])
        t_e = sb("t_e", [P, FT])
        t_s = sb("t_s", [P, FT])
        t_ok = sb("t_ok", [P, FT])
        t_row = sb("t_row", [P, FT])
        t_pad = sb("t_pad", [P, FT])
        tab_f = sb("tab_f", [P, FT])
        before_t = sb("before_t", [P, FT])
        before_i = sb("before_i", [P, FT], i32)
        run_i = sb("run_i", [P, E], i32)
        tab = sb("tab", [P, 3, FT], i32)
        b_raw = sb("b_raw", [P, E * (H + D) // P])
        b_parts = sb("b_parts", [P, 2, E * (H + D) // P], f32r)
        ones2 = sb("ones2", [2, P], f32r)
        ident = sb("ident", [P, P])

        one = ExitStack()

        def s1(name, shape, dt=f32):
            return sb(name, shape, dt, one)

        w_qk = s1("w_qk", [P, 2, KD, 2 * D], f32r)
        w_vc = s1("w_vc", [P, 2, KD, 512], f32r)
        w_g = s1("w_g", [P, 2, KD, 512], f32r)
        rc = s1("rc", [P, TPB, 2 * D])
        rs = s1("rs", [P, TPB, 2 * D])
        DM = s1("DM", [P, NH, SC])
        rot_a = s1("rot_a", [P, TPB, 2 * D])
        vc = s1("vc", [P, TPB, 512])
        R = s1("R", [P, NH, SC])
        sq = s1("sq", [P, KV, T])
        rot_b = sq[:].rearrange("p g t -> p (g t)").rearrange("p (t f) -> p t f", t=TPB)
        gate = s1("gate", [P, KV, T])
        w_p = s1("w_p", [P, KV, D])
        w_s = s1("w_s", [P, 2, KC, 2 * D], f32r)
        w_t = s1("w_t", [P, 2, KD, D], f32r)
        w_o = s1("w_o", [P, 2, 2 * KD, D], f32r)
        b_k = s1("b_k", [P, KD])
        b_q = s1("b_q", [P, KD])
        sel64 = s1("sel64", [P, KV, NH])
        sel8 = s1("sel8", [2 * NH, KV, P], f32r)
        selh = s1("selh", [2 * NH, KD, P], f32r)
        xa = s1("xa", [P, TPB, D])
        xr = s1("xr", [P, TPB, D])
        xb = s1("xb", [P, TPB, D])
        xn = s1("xn", [P, TPB, D])
        xn2 = s1("xn2", [P, TPB, D])
        xnT = s1("xnT", [P, 2, KD, T], f32r)
        qT = s1("qT", [P, KD, T])
        kT = s1("kT", [P, KD, T])
        t2T = s1("t2T", [P, 2, KD, T], f32r)
        ctx_raw = s1("ctx_raw", [P, KC, T])
        ctx_sb = s1("ctx_sb", [P, 2, KC, T], f32r)
        mrow = s1("mrow", [P, T])
        neg = s1("neg", [P, T], bf16)
        k2T = s1("k2T", [P, KD, T])
        q2T = s1("q2T", [P, KD, T])
        v2 = s1("v2", [P, TPB, D])
        riT = s1("riT", [2 * NH, T], f32r)
        pr = s1("pr", [P, NH, T])
        pT = s1("pT", [P, TPB, NH, T])
        pT_flat = pT[:].rearrange("p a h t -> p (a h t)")
        qk_raw, g_raw, vc_raw = (pT_flat[:, n * KD * 512:(n + 1) * KD * 512] for n in range(3))
        sel8_raw = pT_flat[0:2 * NH, 3 * KD * 512:3 * KD * 512 + KV * P]
        selh_raw = pT_flat[0:2 * NH, 3 * KD * 512 + KV * P:3 * KD * 512 + (KV + KD) * P]
        o_raw, t_raw = qk_raw, g_raw[:, 0:KD * D]
        s_raw = pr[:].rearrange("p h t -> p (h t)")
        uT = s1("uT", [P, 2, KD, T], f32r)
        u_raw = q2T
        gr = s1("gr", [2 * NH, T], f32r)
        w_r1 = s1("w_r1", [P, KD, D])
        w_r2 = s1("w_r2", [P, KD, E])
        b_r1 = s1("b_r1", [P, KD])
        b_r1h = s1("b_r1h", [P, KD])
        b_vo_raw = s1("b_vo_raw", [P, 2 * D // P])
        b_vo_parts = s1("b_vo_parts", [P, 2, 2 * D // P], f32r)
        b_vo = s1("b_vo", [2, 2 * D], f32r)
        b_r2 = s1("b_r2", [P, E])
        mcol = s1("mcol", [P, NT])
        dec = s1("dec", [P, NH])
        ones1 = s1("ones1", [2, P])
        ones1b = s1("ones1b", [P, P], bf16)
        iota8 = s1("iota8", [P, E])
        xc = s1("xc", [P, TPB, D])
        before = s1("before", [P, P], bf16)
        onesb = s1("onesb", [P, P], bf16)
        xn3 = s1("xn3", [P, TPB, ROW])
        ids = s1("ids", [P, NT])
        vmean = s1("vmean", [P, KD, NH])

        stats = s1("stats", [P, 3, TPB, 6])
        mv = s1("mv", [P, 3, TPB, 2])
        veps = s1("veps", [P, 3, TPB])
        rstd = s1("rstd", [P, 3, TPB])
        mhalf = s1("mhalf", [P, TPB * NH])
        before_f = R[:, 5, 0:P]
        w_v = R[:, 0:3, :].rearrange("p h s -> p (h s)")[:, 0:KD * 512].rearrange("p (k v) -> p k v", k=KD)
        gvt = s1("gvt", [P, TPB, NH])
        grt = s1("grt", [P, TPB, NH])
        gr_parts = s1("gr_parts", [P, TPB, 2, NH], f32r)
        ri_parts = s1("ri_parts", [P, TPB, 2, NH], f32r)

        delta_sb = R[:, 4, 0:T]

        mx = s1("mx", [P, 2, NH])
        nmx = s1("nmx", [P, 2, NH])
        rsum = s1("rsum", [P, TPB, NH])
        rinv = s1("rinv", [P, TPB, NH])
        t3T = s1("t3T", [P, KD, T])
        r1 = s1("r1", [P, KD, T])
        r1th = s1("r1th", [P, KD, T])
        u_f = r1th
        lg = s1("lg", [P, TPB, E])
        top = s1("top", [P, TPB, E])
        topi = s1("topi", [P, TPB, E], u32)
        topf = s1("topf", [P, TPB, 2])
        dlt = s1("dlt", [P, TPB])
        e2 = s1("e2", [P, TPB])
        den = s1("den", [P, TPB])
        wt = s1("wt", [P, TPB, TOPK])
        oh = s1("oh", [P, TPB, TOPK, E])
        pick = s1("pick", [P, TPB, E], bf16)
        row = s1("row", [P, TPB, E])
        pm = s1("pm", [P, TPB, TOPK, E])
        posf = s1("posf", [P, TPB, TOPK])
        posu = s1("posu", [P, TPB, TOPK], u32)

        one.close()
        two = ctx

        def s2(name, shape, dt=f32):
            return sb(name, shape, dt, two)

        w12 = s2("w12", [P, E, 2, 2, KD * H], f32r)
        bias = s2("bias", [2, E * (H + D)], f32r)
        xt = s2("xt", [P, 2, ROW])
        xT = s2("xT", [P, 2, 2, KD * P], f32r)
        hid = s2("hid", [P, 2, H])
        hT = s2("hT", [P, 2, 2, KH * P], f32r)
        yo = s2("yo", [P, 4, D])
        w_part = s2("w_part", [P, 2, TOPK])
        w_tile = s2("w_tile", [P, FT])
        id_tile = s2("id_tile", [P, FT])
        yi = s2("yi", [P, 4], u32)
        ld = {n: sem("ld_" + n) for n in ("ident", "rot", "decay", "const", "wqk", "wv", "wg", "wp", "ws", "wt", "wo", "r", "r2", "ffn")}
        r_filled = sem("r_filled")
        x_filled = sem("x_filled")
        r_by_act = sem("r_by_act")
        r_by_dve = sem("r_by_dve")
        x_by_act = sem("x_by_act")
        z_filled = sem("z_filled")
        z_by_act = sem("z_by_act")
        z_by_dve = sem("z_by_dve")
        x_by_dve = sem("x_by_dve")
        dm_scan = sem("dm_scan")
        dm_done = sem("dm_done")
        vmean_s = sem("vmean_s")
        wvc_done = sem("wvc_done")
        setup = sem("setup")
        ones_s = sem("ones_s")
        setup2 = sem("setup2")
        neg_done = sem("neg_done")
        rotab = sem("rotab")
        rot = sem("rot")
        th_g = sem("th_g")
        sq_done = sem("sq_done")
        gr_s = sem("gr_s")
        grt_s = sem("grt_s")
        rinv_s = sem("rinv_s")
        t2T_hi = sem("t2T_hi")
        uT_hi = sem("uT_hi")
        uT_lo = sem("uT_lo")
        xnT_hi = sem("xnT_hi")
        ctx_hi = sem("ctx_hi")
        ctx_lo = sem("ctx_lo")
        const_hi = sem("const_hi")
        const_lo = sem("const_lo")
        sel_s = sem("sel_s")
        bvo_s = sem("bvo_s")
        bvo_in = sem("bvo_in")
        mx_s = sem("mx_s")
        nmx_s = sem("nmx_s")
        ri_s = sem("ri_s")
        r1_s = sem("r1_s")
        top_s = sem("top_s")
        topi_s = sem("topi_s")
        topf_s = sem("topf_s")
        dlt_s = sem("dlt_s")
        e2_s = sem("e2_s")
        den_s = sem("den_s")
        phase1 = sem("phase1")
        held = sem("held")
        xa_in = sem("xa_in")
        xa_used = sem("xa_used")
        x2_out = sem("x2_out")
        xc_s = sem("xc_s")
        wt_s = sem("wt_s")
        oh_s = sem("oh_s")
        pick_s = sem("pick_s")
        row_s = sem("row_s")
        row2_s = sem("row2_s")
        pm_s = sem("pm_s")
        pos_s = sem("pos_s")
        scattered = sem("scattered")
        pads_s = sem("pads_s")
        padded = sem("padded")
        n_s = sem("n_s")
        tab_s = sem("tab_s")
        hi_w = sem("hi_w")
        lo_w = sem("lo_w")
        xT_f = sem("xT_f")
        xT_hi = sem("xT_hi")
        xT_lo = sem("xT_lo")
        l1_f = sem("l1_f")
        sil_s = sem("sil_s")
        hT_f = sem("hT_f")
        hT_hi = sem("hT_hi")
        hT_lo = sem("hT_lo")
        l2_f = sem("l2_f")
        y_s = sem("y_s")
        wpart_s = sem("wpart_s")
        picked = sem("picked")
        yi_s = sem("yi_s")
        b_parts_s = sem("b_parts_s")
        bias_in = sem("bias_in")
        added = [sem(f"added{n}") for n in range(2)]
        freed = sem("freed")
        ctx_in = sem("ctx_in")
        mrow_in = sem("mrow_in")
        stat = [sem(f"stat{n}") for n in range(3)]
        aggr = [sem(f"aggr{n}") for n in range(3)]
        veps_s = [sem(f"veps{n}") for n in range(3)]
        rstd_s = [sem(f"rstd{n}") for n in range(3)]
        xn_s = [sem(f"xn{n}") for n in range(3)]
        xt_in = [sem(f"xt_in{n}") for n in range(2)]
        w_in = [sem(f"w_in{e}") for e in range(E)]

        r_all = {"act": R_ITEMS.count("act"), "dve": R_ITEMS.count("dve")}
        x_all_ = {"act": X_ITEMS.count("act"), "dve": X_ITEMS.count("dve")}
        z_all = {"act": Z_ITEMS.count("act"), "dve": Z_ITEMS.count("dve")}

        r_by = {"act": r_by_act, "dve": r_by_dve}
        x_by = {"act": x_by_act, "dve": x_by_dve}
        z_by = {"act": z_by_act, "dve": z_by_dve}

        def r_read(b, n):
            return r_by[R_ITEMS[n]], (b + 1) * r_all[R_ITEMS[n]] + R_ITEMS[:n + 1].count(R_ITEMS[n])

        def x_read(b, n):
            return x_by[X_ITEMS[n]], (b + 1) * x_all_[X_ITEMS[n]] + X_ITEMS[:n + 1].count(X_ITEMS[n])

        def z_read(b, n):
            return z_by[Z_ITEMS[n]], (b + 1) * z_all[Z_ITEMS[n]] + Z_ITEMS[:n + 1].count(Z_ITEMS[n])

        def z_item(b, n):
            return b * len(Z_ITEMS) + n + 1

        def r_item(b, n):
            return b * number(R_ITEMS, len(R_ITEMS) - 1) + number(R_ITEMS, n)

        def x_item(b, n):
            return (b + 1) * len(X_ITEMS) + n + 1

        def r_free(b, n):
            who, k = previous(R_ITEMS, n, R_BANKS)
            return r_by[who], (b + 1) * r_all[who] + k

        def x_free(b, n):
            who, k = previous(X_ITEMS, n, X_BANKS)
            return x_by[who], (b + 1) * x_all_[who] + k

        def z_free(b, n):
            who, k = previous(Z_ITEMS, n, Z_BANKS)
            return z_by[who], (b + 1) * z_all[who] + k

        def done(i):
            return i + 3

        def hold(eng):
            eng.sem_inc(held, 1)

        def rbank(n):
            return psum[:, n % R_BANKS, :]

        def xbank(n):
            return psum[:, R_BANKS + n % X_BANKS, :]

        zbank = psum[:, R_BANKS + X_BANKS, :]

        def tiles(b):
            return bass.ds(b * TPB, TPB)

        C_QK, C_G, C_V, C_S, C_T, C_O = 1, 2, 3, 4, 5, 6

        block = ctx.enter_context(nc.Block())

        @block.sync
        def _(sp):
            xv = x.rearrange("(n p) d -> p n d", p=P)
            outv = out.rearrange("(n p) d -> p n d", p=P)

            def load(name, dst, src):
                sp.dma_start(dst, src).then_inc(ld[name], 16)

            def load_x(b):
                sp.dma_start(xa[:], xv[:, tiles(b), :]).then_inc(xa_in, 16)

            load_x(0)
            load("ident", ident[:], ident_in)
            load("wqk", qk_raw.rearrange("p (k f) -> p k f", k=KD), wqkT)
            load("rot", rc[:], rot_c)
            load("rot", rs[:], rot_s)
            load("wg", g_raw.rearrange("p (k f) -> p k f", k=KD), wgT)
            load("wv", w_v, wvT)
            load("decay", dec[:], decay.partition_broadcast(P))
            load("decay", delta_sb, delta)
            consts = [(sel64[:], sel64_in), (sel8_raw.rearrange("p (g v) -> p g v", g=KV), sel8_in), (before_f, before_in),
                      (selh_raw.rearrange("p (g v) -> p g v", g=KD), selh_in), (iota8[:], iota_in), (base[:], base_in), (mcol[:], maskcol),
                      (b_k[:], bsk), (b_q[:], bt), (b_r1[:], rb1), (b_vo_raw[:, 0:D // P], bsv),
                      (b_vo_raw[:, D // P:], bo), (b_r2[:], rb2.partition_broadcast(P)), (pad[:], pad_in), (ids[:], ids_in),
                      (iota_t[:], iota_t_in), (parity[:], parity_in)]
            assert len(consts) == CONSTS
            for dst, src in consts[0:3]:
                load("const", dst, src)
            load("ws", s_raw.rearrange("p (k f) -> p k f", k=KC), wsT)
            for dst, src in consts[3:]:
                load("const", dst, src)
            load("r2", w_r2[:], rw2)

            def context(b):
                sp.dma_start(ctx_raw[:], ctxT[bass.ds(b, 1)].rearrange("a p f -> (a p) f")
                             .rearrange("p (c s) -> p c s", c=KC)).then_inc(ctx_in, 16)
                sp.dma_start(mrow[:], maskrow[bass.ds(b, 1)].rearrange("a s -> (a s)").partition_broadcast(P)
                             ).then_inc(mrow_in, 16)

            def store_x2(b):
                sp.wait_ge(xc_s, b + 1)
                sp.dma_start(outv[:, tiles(b), :], xc[:]).then_inc(x2_out, 16)

            context(0)
            sp.wait_ge(xa_used, 1)
            load_x(1)
            load("wp", w_p[:], wpT)
            sp.wait_ge(const_lo, C_G)
            load("wt", t_raw.rearrange("p (k f) -> p k f", k=KD), wtT)
            load("wo", o_raw.rearrange("p (k f) -> p k f", k=2 * KD), woT)
            load("r", w_r1[:], rw1)
            load("ffn", b_raw[:, 0:E * H // P], eb1)
            load("ffn", b_raw[:, E * H // P:], eb2)
            with sp.Fori(1, B - 1) as b:
                sp.wait_ge(x_filled, x_item(b - 1, X_V1))
                sp.wait_ge(*x_read(b - 1, X_Q))
                context(b)
                sp.wait_ge(xa_used, b + 1)
                load_x(b + 1)
                store_x2(b - 1)
            sp.wait_ge(x_filled, x_item(B - 2, X_V1))
            sp.wait_ge(*x_read(B - 2, X_Q))
            context(B - 1)
            store_x2(B - 2)

            def weights(e):
                for n, src in enumerate((ew1, ew2)):
                    sp.dma_start(w12[:, e, n, 1, :].bitcast(f32), src[:, e, :]).then_inc(w_in[e], 16)

            sp.wait_ge(*r_read(B - 1, R_RB + 1))
            for e in range(EARLY):
                weights(e)
            sp.wait_ge(*x_read(B - 1, X_O))
            for e in range(EARLY, E):
                weights(e)
            store_x2(B - 1)
            sp.wait_ge(ld["const"], CONSTS * 16)
            sp.dma_start(out[B * T:B * T + P, :], pad[:, 0:D]).then_inc(x2_out, 16)
            sp.wait_ge(pads_s, 1)
            for e in range(E):
                at = sp.value_load(run_i[0:1, e:e + 1], min_val=e * CAP, max_val=e * CAP + B * T)
                sp.dma_start(slot_in[bass.ds(at, P), :], pad[:]).then_inc(padded, 16)
            sp.dma_start(slot_in[E * CAP:ROWS, :], pad[:]).then_inc(padded, 16)
            sp.wait_ge(tab_s, 4)
            sp.wait_ge(padded, 16 * (E + 1))
            sp.wait_ge(scattered, 16 * TOPK * NT)
            sp.wait_ge(phase1, 4)

            def load_tile(i, slot):
                at = sp.value_load(tab[0:1, 1, bass.ds(i, 1)], min_val=0, max_val=ROWS - P)
                sp.dma_start(xt[:, slot, :], slot_in[bass.ds(at, P), :]).then_inc(xt_in[slot], 16)

            for i in range(2):
                load_tile(i, i)
            for i in range(2, 4):
                sp.wait_ge(xT_f, done(i - 2))
                sp.wait_ge(picked, i - 1)
                load_tile(i, i % 2)
            with sp.Fori(2, FT // 2) as h:
                for slot in range(2):
                    i = 2 * h + slot
                    sp.wait_ge(xT_f, done(i - 2))
                    hold(sp)
                    sp.wait_ge(picked, i - 1)
                    hold(sp)
                    load_tile(i, slot)

        @block.tensor
        def _(pe):
            def mm(o, l, r, first, last):
                return nc.tensor.matmul(o, l, r, start=first, stop=last)

            PAIRS = ((0, 0), (0, 1), (1, 0))

            def product(o, chunks, left, right, ends=True):
                for k in range(chunks):
                    for n, (a, w) in enumerate(PAIRS):
                        last = mm(o, left(k, a), right(k, w), k == 0 and n == 0,
                                  ends and k == chunks - 1 and n == 2)
                return last

            def transpose_rows(bank, src, chunks):
                for c in range(chunks):
                    for t in range(TPB):
                        last = nc.tensor.transpose(bank[:, c * T + t * P:c * T + (t + 1) * P],
                                                   src[:, t, c * P:(c + 1) * P], ident[:])
                return last

            def filled(ring, ins):
                ins.then_inc({"r": r_filled, "x": x_filled, "z": z_filled}[ring], 1)

            def r_xt(b):
                pe.wait_ge(xn_s[0], b * TPB + TPB)
                pe.wait_ge(*r_free(b, R_XT))
                filled("r", transpose_rows(rbank(R_XT), xn, KD))

            def r_qk(b):
                pe.wait_ge(*r_read(b, R_XT))
                for t in range(TPB):
                    pe.wait_ge(*r_free(b, R_QK + t))
                    last = product(rbank(R_QK + t), KD, lambda k, a: xnT[:, a, k, t * P:(t + 1) * P],
                                   lambda k, a: w_qk[:, a, k, :])
                    filled("r", last)

            def r_v(b, t, half):
                if half == 0:
                    pe.wait_ge(*r_free(b, R_V[t]))
                for n, (a, w) in enumerate(PAIRS):
                    last = mm(rbank(R_V[t]), xnT[:, a, half, t * P:(t + 1) * P], w_vc[:, w, half, :],
                              half == 0 and n == 0, half == KD - 1 and n == 2)
                if half == KD - 1:
                    filled("r", last)

            def r_g(b, n, half):
                if half == 0:
                    pe.wait_ge(*r_free(b, R_G[n]))
                g = 2 * n + half
                last = product(rbank(R_G[n])[:, half * T:(half + 1) * T], KD,
                               lambda k, a: w_g[:, a, k, g * P:(g + 1) * P], lambda k, a: xnT[:, a, k, :])
                if half == 1:
                    filled("r", last)

            def r_qkt(b):
                pe.wait_ge(rot, TPB * (b + 1))
                for n in range(2):
                    pe.wait_ge(*r_free(b, R_QT + n))
                    filled("r", transpose_rows(rbank(R_QT + n), rot_a[:, :, n * D:(n + 1) * D], KD))

            def r_scores(b, h):
                if h == 0:
                    pe.wait_ge(*r_read(b, R_KT))
                pe.wait_ge(*r_free(b, R_S[h]))
                g, r = h // HPG, DH * (h % HPG)
                o = rbank(R_S[h])
                mm(o[:, 0:T], kT[r:r + DH, g, 0:P], qT[r:r + DH, g, :], True, True)
                filled("r", mm(o[:, T:SC], kT[r:r + DH, g, P:T], qT[r:r + DH, g, P:T], True, True))

            def r_out(b):
                pe.wait_ge(*r_read(b, R_V[1]))
                for n in range(2):
                    pe.wait_ge(*r_read(b, R_S[4 * n + 3]))
                    pe.wait_ge(*r_free(b, R_O + n))
                    for j in range(2):
                        for half in range(2):
                            h = 2 * (2 * n + j) + half
                            o = rbank(R_O + n)[DV * half:DV * (half + 1), j * T:(j + 1) * T]
                            mm(o, vc[:, 0, h * DV:(h + 1) * DV], R[:, h, 0:T], True, False)
                            last = mm(o[:, P:T], vc[:, 1, h * DV:(h + 1) * DV], R[:, h, T:SC], False, True)
                    filled("r", last)

            def r_var(b):
                pe.wait_ge(sq_done, 2 * (b + 1))
                pe.wait_ge(*r_free(b, R_VAR))
                for t in range(TPB):
                    for g in range(KV):
                        last = mm(rbank(R_VAR)[:, t * NH:(t + 1) * NH], sq[:, g, t * P:(t + 1) * P], sel64[:, g, :],
                                  g == 0, g == KV - 1)
                filled("r", last)

            def r_gt(b):
                pe.wait_ge(gr_s, 2 * (b + 1))
                pe.wait_ge(*r_free(b, R_GT))
                for t in range(TPB):
                    last = nc.tensor.transpose(rbank(R_GT)[0:2 * NH, t * P:(t + 1) * P],
                                               gr_parts[:, t].rearrange("p a h -> p (a h)").bitcast(f32), ident[:])
                filled("r", last)

            def r_rb(b):
                pe.wait_ge(*r_read(b, R_GT))
                for n in range(2):
                    pe.wait_ge(*r_free(b, R_RB + n))
                    for j in range(2):
                        last = mm(rbank(R_RB + n)[:, j * T:(j + 1) * T], sel8[:, 2 * n + j, :], gr[:], True, True)
                    filled("r", last)

            def x_y(b):
                pe.wait_ge(*r_read(b, R_RB + 1))
                pe.wait_ge(*x_free(b, X_Y))
                for t in range(TPB):
                    for g in range(KV):
                        last = mm(xbank(X_Y)[:, t * D:(t + 1) * D], gate[:, g, t * P:(t + 1) * P], w_p[:, g, :],
                                  g == 0, g == KV - 1)
                filled("x", last)

            def x_t2(b):
                pe.wait_ge(xn_s[1], TPB * (b + 1))
                pe.wait_ge(*x_free(b, X_T2))
                filled("x", transpose_rows(xbank(X_T2), xn2, KD))

            def x_k(b):
                pe.wait_ge(ctx_lo, b + 1)
                pe.wait_ge(*x_free(b - 1, X_NK))
                for g in range(KD):
                    last = product(xbank(X_NK)[:, g * T:(g + 1) * T], KC,
                                   lambda k, a: w_s[:, a, k, g * P:(g + 1) * P], lambda k, a: ctx_sb[:, a, k, :])
                filled("x", last)

            def x_v(b, t):
                pe.wait_ge(*(x_free(b, X_V1) if t else x_free(b - 1, X_NV)))
                o = xbank(X_V1 if t else X_NV)[:, 0:D]
                product(o, KC, lambda k, a: ctx_sb[:, a, k, t * P:(t + 1) * P], lambda k, a: w_s[:, a, k, D:2 * D],
                        ends=False)
                filled("x", mm(o, ones2[:], b_vo[:, 0:D], False, True))

            def x_q(b):
                pe.wait_ge(*x_read(b, X_T2))
                pe.wait_ge(*x_free(b, X_Q))
                for g in range(KD):
                    last = product(xbank(X_Q)[:, g * T:(g + 1) * T], KD,
                                   lambda k, a: w_t[:, a, k, g * P:(g + 1) * P], lambda k, a: t2T[:, a, k, :])
                filled("x", last)

            def x_scores(b, t, r):
                if t == 0 and r == 0:
                    pe.wait_ge(*x_read(b, X_Q))
                    pe.wait_ge(neg_done, b + 1)
                n = X_S[t][r]
                pe.wait_ge(*x_free(b, n))
                o = xbank(n)
                for g in range(KD):
                    mm(o[:, g * T:(g + 1) * T], q2T[DH * r:DH * (r + 1), g, t * P:(t + 1) * P],
                       k2T[DH * r:DH * (r + 1), g, :], True, False)
                    last = mm(o[:, g * T:(g + 1) * T], ones1b[DH * r:DH * r + 1, :], neg[DH * r:DH * r + 1, :],
                              False, True)
                filled("x", last)

            def x_probs(b, t, r):
                n = X_P[t] + r
                pe.wait_ge(*x_read(b, X_S[t][r]))
                pe.wait_ge(*x_free(b, n))
                for s in range(TPB):
                    for g in range(KD):
                        last = nc.tensor.transpose(xbank(n)[:, (s * KD + g) * P:(s * KD + g + 1) * P],
                                                   pr[:, g * HPG + r, s * P:(s + 1) * P], ident[:])
                filled("x", last)

            def x_u(b):
                pe.wait_ge(ri_s, 2 * (b + 1))
                pe.wait_ge(*x_free(b, X_RS))
                for t in range(TPB):
                    last = nc.tensor.transpose(xbank(X_RS)[0:2 * NH, t * P:(t + 1) * P],
                                               ri_parts[:, t].rearrange("p a h -> p (a h)").bitcast(f32), ident[:])
                filled("x", last)
                pe.wait_ge(*x_read(b, X_P[1] + 2))
                pe.wait_ge(*x_read(b, X_P[1] + 3))
                pe.wait_ge(*x_free(b, X_U))
                for h in range(NH):
                    g, r = h // HPG, DH * (h % HPG)
                    for s in range(TPB):
                        last = mm(xbank(X_U)[r:r + DH, g * T:(g + 1) * T], v2[:, s, h * DH:(h + 1) * DH],
                                  pT[:, s, h, :], s == 0, s == TPB - 1)
                filled("x", last)

            def x_rb(b):
                pe.wait_ge(*x_read(b, X_RS))
                pe.wait_ge(*x_free(b, X_RB))
                for g in range(KD):
                    last = mm(xbank(X_RB)[:, g * T:(g + 1) * T], selh[:, g, :], riT[:], True, True)
                filled("x", last)

            def x_out(b, t):
                if t == 0:
                    pe.wait_ge(uT_lo, b + 1)
                    pe.wait_ge(*x_free(b, X_O))
                o = xbank(X_O)[:, t * D:(t + 1) * D]
                product(o, 2 * KD, lambda k, a: (t2T if k < KD else uT)[:, a, k % KD, t * P:(t + 1) * P],
                        lambda k, a: w_o[:, a, k, :], ends=False)
                last = mm(o, ones2[:], b_vo[:, D:2 * D], False, True)
                if t == TPB - 1:
                    filled("x", last)

            def z_t3(b):
                pe.wait_ge(xn_s[2], TPB * (b + 1))
                pe.wait_ge(*z_free(b, Z_T3))
                filled("z", transpose_rows(zbank, xn3, KD))

            def z_r1(b, g):
                if g == 0:
                    pe.wait_ge(*z_read(b, Z_T3))
                    pe.wait_ge(*z_free(b, Z_R1))
                for k in range(KD):
                    last = mm(zbank[:, g * T:(g + 1) * T], w_r1[:, k, g * P:(g + 1) * P], t3T[:, k, :],
                              k == 0, k == KD - 1)
                if g == KD - 1:
                    filled("z", last)

            def z_lg(b):
                pe.wait_ge(r1_s, b + 1)
                pe.wait_ge(*z_free(b, Z_LG))
                for t in range(TPB):
                    for k in range(KD):
                        last = mm(zbank[:, t * E:(t + 1) * E], r1[:, k, t * P:(t + 1) * P], w_r2[:, k, :],
                                  k == 0, k == KD - 1)
                filled("z", last)

            def z_rank(b):
                pe.wait_ge(pick_s, b + 1)
                pe.wait_ge(*z_free(b, Z_RK))
                o = zbank
                mm(o[:, 0:E], before[:], pick[:, 0, :], True, True)
                mm(o[:, E:2 * E], before[:], pick[:, 1, :], True, False)
                mm(o[:, E:2 * E], onesb[:], pick[:, 0, :], False, True)
                mm(o[:, 2 * E:3 * E], onesb[:], pick[:, 0, :], True, False)
                filled("z", mm(o[:, 2 * E:3 * E], onesb[:], pick[:, 1, :], False, True))

            def turn(i, r, x, z):
                j, k = i - 1, i - 2
                if r: r_xt(i)
                if x: x_v(j, 0)
                if x: x_y(j)
                if z: z_t3(k)
                if r: r_qk(i)
                if z: z_r1(k, 0)
                if x: x_t2(j)
                if z: z_r1(k, 1)
                if r: r_g(i, 0, 0)
                if r: r_g(i, 0, 1)
                if x: x_q(j)
                if z: z_lg(k)
                if x: x_v(j, 1)
                if x: x_scores(j, 0, 0)
                if x: x_scores(j, 0, 1)
                if r: r_qkt(i)
                if x: x_scores(j, 0, 2)
                if r: r_v(i, 0, 0)
                if x: x_scores(j, 0, 3)
                if x: x_probs(j, 0, 0)
                if r: r_scores(i, 0)
                if r: r_v(i, 0, 1)
                if r: r_scores(i, 1)
                if x: x_probs(j, 0, 1)
                if r: r_scores(i, 2)
                if x: x_probs(j, 0, 2)
                if z: z_rank(k)
                if r: r_scores(i, 3)
                if x: x_probs(j, 0, 3)
                if x: x_scores(j, 1, 0)
                if r: r_g(i, 1, 0)
                if x: x_scores(j, 1, 1)
                if r: r_g(i, 1, 1)
                if x: x_scores(j, 1, 2)
                if r: r_v(i, 1, 0)
                if x: x_scores(j, 1, 3)
                if r: r_v(i, 1, 1)
                for h in range(4):
                    if r: r_scores(i, 4 + h)
                    if x: x_probs(j, 1, h)
                if r: r_out(i)
                if x: x_u(j)
                if r: r_var(i)
                if x: x_rb(j)
                if r: x_k(i)
                elif x: pe.drain().then_inc(x_filled, 1)
                if x: x_out(j, 0)
                if r: r_gt(i)
                if x: x_out(j, 1)
                if r: r_rb(i)

            pe.wait_ge(ld["ident"], 16)
            pe.sem_inc(x_filled, X_NK)
            r_xt(0)
            pe.wait_ge(const_lo, C_QK)
            r_qk(0)
            pe.wait_ge(const_lo, C_G)
            r_g(0, 0, 0)
            r_g(0, 0, 1)
            r_qkt(0)
            pe.wait_ge(const_lo, C_V)
            r_v(0, 0, 0)
            r_scores(0, 0)
            r_v(0, 0, 1)
            for h in range(1, 4):
                r_scores(0, h)
            r_g(0, 1, 0)
            r_g(0, 1, 1)
            r_v(0, 1, 0)
            r_v(0, 1, 1)
            for h in range(4, NH):
                r_scores(0, h)
            r_out(0)
            pe.wait_ge(ld["const"], CONSTS * 16)
            r_var(0)
            r_gt(0)
            pe.wait_ge(const_lo, C_S)
            x_k(0)
            pe.drain().then_inc(x_filled, 1)
            pe.wait_ge(bvo_in, 4 * 16)
            pe.wait_ge(sel_s, 2)
            r_rb(0)
            pe.wait_ge(ld["wp"], 16)
            pe.wait_ge(ld["r"], 16)
            pe.wait_ge(const_lo, C_O)
            turn(1, True, True, False)
            with pe.Fori(2, B - 1) as i:
                turn(i, True, True, True)
            turn(B - 1, True, True, True)
            turn(B, False, True, True)
            turn(B + 1, False, False, True)
            pe.drain().then_inc(phase1, 1)

            def turn_rows(i, half, slot):
                pe.wait_ge(xt_in[slot], 16 * (half + 1))
                pe.wait_ge(xT_lo, done(i - 2))
                for k in range(KD):
                    last = nc.tensor.transpose(psum[:, slot, k * P:(k + 1) * P], xt[:, slot, k * P:(k + 1) * P],
                                               ident[:])
                last.then_inc(xT_f, 1)

            def hidden(i, e, slot):
                pe.wait_ge(xT_lo, done(i))
                pe.wait_ge(sil_s, done(i - 2))
                o = psum[:, 2 + slot, :]
                for k in range(KD):
                    for n, (a, w) in enumerate(PAIRS):
                        mm(o, xT[:, slot, a, k * P:(k + 1) * P],
                           w12[:, bass.ds(e, 1), 0, w, k * H:(k + 1) * H].rearrange("p a f -> p (a f)"),
                           k == 0 and n == 0, False)
                mm(o, ones2[:], bias[:, bass.ds(e * H, H)], False, True).then_inc(l1_f, 1)

            def turn_hidden(i, slot):
                pe.wait_ge(sil_s, done(i))
                pe.wait_ge(hT_lo, done(i - 2))
                for k in range(KH):
                    last = nc.tensor.transpose(psum[:, 4 + slot, k * P:(k + 1) * P], hid[:, slot, k * P:(k + 1) * P],
                                               ident[:])
                last.then_inc(hT_f, 1)

            def output(i, e, slot):
                pe.wait_ge(hT_lo, done(i))
                pe.wait_ge(y_s, done(i - 2))
                o = psum[:, 6 + slot, 0:D]
                for k in range(KH):
                    for n, (a, w) in enumerate(PAIRS):
                        mm(o, hT[:, slot, a, k * P:(k + 1) * P],
                           w12[:, bass.ds(e, 1), 1, w, k * D:(k + 1) * D].rearrange("p a f -> p (a f)"),
                           k == 0 and n == 0, False)
                mm(o, ones2[:], bias[:, bass.ds(e * D + E * H, D)], False, True).then_inc(l2_f, 1)

            experts = {}

            def expert(i):
                return pe.value_load(tab[0:1, 0, bass.ds(i, 1)], min_val=0, max_val=E - 1)

            def step(i, half, k, rows=True, out=True, turned=True):
                slot = k % 2
                if rows:
                    turn_rows(i + 1, half + slot, 1 - slot)
                if k == 0:
                    experts[k] = expert(i)
                hidden(i, experts[k], slot)
                if turned:
                    turn_hidden(i - 1, 1 - slot)
                if out:
                    output(i - 2, experts[k - 2] if k > 1 else expert(i - 2), slot)
                if k < 3:
                    experts[k + 1] = expert(i + 1)

            pe.sem_inc(xT_f, 2)
            pe.sem_inc(l1_f, 2)
            pe.sem_inc(hT_f, 2)
            pe.sem_inc(l2_f, 2)
            pe.wait_ge(tab_s, 4)
            pe.wait_ge(bias_in, 4 * 16)
            turn_rows(0, 0, 0)
            pe.wait_ge(lo_w, 2 * E)
            step(0, 0, 0, out=False, turned=False)
            step(1, 0, 1, out=False)
            step(2, 1, 2)
            step(3, 1, 3)
            with pe.Fori(1, FT // 4 - 1) as turn:
                for k in range(4):
                    step(4 * turn + k, 2 * turn + k // 2, k)
            for k in range(3):
                step(FT - 4 + k, FT // 2 - 2 + k // 2, k)
            step(FT - 1, FT // 2 - 1, 3, rows=False)
            turn_hidden(FT - 1, 1)
            output(FT - 2, expert(FT - 2), 0)
            output(FT - 1, expert(FT - 1), 1)

        @block.vector
        def _(dve):
            V = nc.vector

            def norm_stats(b, n, rows):
                hold(dve)
                for t in range(TPB):
                    V.bn_stats(stats[:, n, t, :], rows[:, t, :]).then_inc(stat[n], 1)
                dve.wait_ge(stat[n], TPB * (b + 1))
                hold(dve)
                for t in range(TPB):
                    V.bn_aggr(mv[:, n, t, :], stats[:, n, t, :]).then_inc(aggr[n], 1)

            def norm_rows(b, n, rows, dst):
                dve.wait_ge(rstd_s[n], b + 1)
                for t in range(TPB):
                    V.tensor_scalar(dst[:, t, :], rows[:, t, :], mv[:, n, t, 0:1], rstd[:, n, t:t + 1],
                                    ALU.subtract, ALU.mult).then_inc(xn_s[n], 1)

            def r_norm1a(b):
                dve.wait_ge(xa_in, 16 * (b + 1))
                norm_stats(b, 0, xa)

            def r_norm1b(b):
                if not isinstance(b, int) or b > 0:
                    dve.wait_ge(r_filled, r_item(b - 1, R_XT))
                norm_rows(b, 0, xa, xn)

            def r_low(b):
                dve.wait_ge(xnT_hi, b + 1)
                V.tensor_tensor(xnT[:, 1].rearrange("p c s -> p (c s)"), rbank(R_XT),
                                xnT[:, 0].rearrange("p c s -> p (c s)").bitcast(f32), ALU.subtract
                                ).then_inc(r_by_dve, 1)

            def r_rotate(b, tiles_):
                for t in tiles_:
                    dve.wait_ge(r_filled, r_item(b, R_QK + t))
                    p = rbank(R_QK + t)
                    V.tensor_tensor(rot_a[:, t, :], p, rc[:, t, :], ALU.mult).then_inc(rotab, 1)
                    pv = p.rearrange("p (h two j) -> p h two j", two=2, j=DH // 2)
                    sv = rs[:, t, :].rearrange("p (h two j) -> p h two j", two=2, j=DH // 2)
                    bv = rot_b[:, t, :].rearrange("p (h two j) -> p h two j", two=2, j=DH // 2)
                    V.tensor_tensor(bv[:, :, 0, :], pv[:, :, 1, :], sv[:, :, 0, :], ALU.mult).then_inc(rotab, 1)
                    V.tensor_tensor(bv[:, :, 1, :], pv[:, :, 0, :], sv[:, :, 1, :], ALU.mult
                                    ).then_inc(r_by_dve, 1)

            def r_gate(b, n):
                dve.wait_ge(th_g, 2 * b + n + 1)
                V.scalar_tensor_tensor(gate[:, 2 * n:2 * n + 2, :].rearrange("p a s -> p (a s)"),
                                       gate[:, 2 * n:2 * n + 2, :].rearrange("p a s -> p (a s)"), 1.0,
                                       rbank(R_G[n]), ALU.add, ALU.mult).then_inc(r_by_dve, 1)

            def r_decay(b, heads):
                for h in heads:
                    dve.wait_ge(r_filled, r_item(b, R_S[h]))
                    V.tensor_tensor(R[:, h, :], rbank(R_S[h])[:, 0:SC], DM[:, h, :], ALU.mult
                                    ).then_inc(r_by_dve, 1)

            def r_z(b):
                for n in range(2):
                    dve.wait_ge(sq_done, 2 * b + n + 1)
                    V.tensor_tensor(gate[:, 2 * n:2 * n + 2, :].rearrange("p a s -> p (a s)"), rbank(R_O + n),
                                    gate[:, 2 * n:2 * n + 2, :].rearrange("p a s -> p (a s)"), ALU.mult
                                    ).then_inc(r_by_dve, 1)

            def r_var(b):
                dve.wait_ge(r_filled, r_item(b, R_VAR))
                V.tensor_scalar(gvt[:].rearrange("p t h -> p (t h)"), rbank(R_VAR)[:, 0:TPB * NH], EPS, 4.0,
                                ALU.add, ALU.mult).then_inc(r_by_dve, 1)

            def r_y(b):
                dve.wait_ge(*r_read(b, R_O + 1))
                for n in range(2):
                    dve.wait_ge(r_filled, r_item(b, R_RB + n))
                    V.tensor_tensor(gate[:, 2 * n:2 * n + 2, :].rearrange("p a s -> p (a s)"), rbank(R_RB + n),
                                    gate[:, 2 * n:2 * n + 2, :].rearrange("p a s -> p (a s)"), ALU.mult
                                    ).then_inc(r_by_dve, 1)

            def x_x1(b):
                dve.wait_ge(x_filled, x_item(b, X_Y))
                dve.wait_ge(xa_used, b + 1)
                V.tensor_tensor(xb[:].rearrange("p t d -> p (t d)"), xbank(X_Y), xr[:].rearrange("p t d -> p (t d)"),
                                ALU.add).then_inc(x_by_dve, 1)
                dve.wait_ge(*x_read(b, X_Y))
                norm_stats(b, 1, xb)

            def x_norm2(b):
                norm_rows(b, 1, xb, xn2)

            def x_k(b):
                dve.wait_ge(x_filled, x_item(b - 1, X_NK))
                dve.wait_ge(mrow_in, 16 * (b + 1))
                V.tensor_scalar(neg[:], mrow[:], 0.0, NEG, ALU.is_equal, ALU.mult).then_inc(neg_done, 1)
                for g in range(KD):
                    ins = V.scalar_tensor_tensor(k2T[:, g, :], xbank(X_NK)[:, g * T:(g + 1) * T], b_k[:, g:g + 1],
                                                 mrow[:], ALU.add, ALU.mult)
                ins.then_inc(x_by_dve, 1)

            def x_q(b):
                dve.wait_ge(x_filled, x_item(b, X_Q))
                for g in range(KD):
                    ins = V.scalar_tensor_tensor(q2T[:, g, :], xbank(X_Q)[:, g * T:(g + 1) * T], b_q[:, g:g + 1],
                                                 mrow[:], ALU.add, ALU.mult)
                ins.then_inc(x_by_dve, 1)

            def x_max(b, t, rs):
                for r in rs:
                    n = X_S[t][r]
                    dve.wait_ge(x_filled, x_item(b, n))
                    V.tensor_reduce(mx[:, t, r::HPG], xbank(n).rearrange("p (g s) -> p g s", g=KD), AX.X, ALU.max
                                    ).then_inc(mx_s, 1)
                    dve.wait_ge(mx_s, HPG * (TPB * b + t) + r + 1)
                    V.tensor_scalar(nmx[:, t, r::HPG], mx[:, t, r::HPG], -SCALE, None, ALU.mult
                                    ).then_inc(nmx_s, 1)

            def x_probs(b, t, r):
                n = X_P[t] + r
                dve.wait_ge(x_filled, x_item(b, n))
                V.tensor_copy(pT[:, :, r::HPG, t * P:(t + 1) * P],
                              xbank(n).rearrange("p (s g t) -> p s g t", s=TPB, g=KD)).then_inc(x_by_dve, 1)

            def x_rinv(b):
                dve.wait_ge(*x_read(b, X_S[1][3]))
                V.reciprocal(rinv[:].rearrange("p t h -> p (t h)"), rsum[:].rearrange("p t h -> p (t h)")
                             ).then_inc(rinv_s, 1)
                dve.wait_ge(rinv_s, b + 1)
                V.tensor_copy(ri_parts[:, :, 0, :], rinv[:]).then_inc(ri_s, 1)
                dve.wait_ge(ri_s, 2 * b + 1)
                V.tensor_tensor(ri_parts[:, :, 1, :], rinv[:], ri_parts[:, :, 0, :].bitcast(f32), ALU.subtract
                                ).then_inc(ri_s, 1)

            def low_t2(b):
                dve.wait_ge(t2T_hi, b + 1)
                V.tensor_tensor(t2T[:, 1].rearrange("p g t -> p (g t)"), xbank(X_T2),
                                t2T[:, 0].rearrange("p g t -> p (g t)").bitcast(f32), ALU.subtract
                                ).then_inc(x_by_dve, 1)

            def x_u(b):
                dve.wait_ge(*x_read(b, X_U))
                dve.wait_ge(x_filled, x_item(b, X_RB))
                flat_u = u_f[:].rearrange("p g t -> p (g t)")
                V.tensor_tensor(flat_u, xbank(X_RB), u_raw[:].rearrange("p g t -> p (g t)"), ALU.mult
                                ).then_inc(x_by_dve, 1)
                dve.wait_ge(uT_hi, b + 1)
                V.tensor_tensor(uT[:, 1].rearrange("p g t -> p (g t)"), flat_u,
                                uT[:, 0].rearrange("p g t -> p (g t)").bitcast(f32), ALU.subtract
                                ).then_inc(uT_lo, 1)

            def x_x2(b):
                dve.wait_ge(x_filled, x_item(b, X_O))
                dve.wait_ge(x2_out, 16 * b)
                flat_c = xc[:].rearrange("p t d -> p (t d)")
                V.tensor_tensor(flat_c, xbank(X_O), xb[:].rearrange("p t d -> p (t d)"), ALU.add
                                ).then_inc(x_by_dve, 1)
                dve.wait_ge(*x_read(b, X_O))
                norm_stats(b, 2, xc)

            def x_norm3(b):
                dve.wait_ge(scattered, 16 * TOPK * TPB * b)
                norm_rows(b, 2, xc, xn3[:, :, 0:D])

            def z_sum(b):
                dve.wait_ge(xn_s[2], TPB * (b + 1))
                V.tensor_tensor(xc[:], xc[:], xn3[:, :, 0:D], ALU.add).then_inc(xc_s, 1)

            def z_r1(b):
                dve.wait_ge(*z_read(b, Z_R1))
                V.scalar_tensor_tensor(r1[:].rearrange("p g t -> p (g t)"), r1th[:].rearrange("p g t -> p (g t)"), 1.0,
                                       r1[:].rearrange("p g t -> p (g t)"), ALU.add, ALU.mult).then_inc(r1_s, 1)

            def z_route(b):
                dve.wait_ge(z_filled, z_item(b, Z_LG))
                V.tensor_tensor(lg[:], zbank[:, 0:TPB * E].rearrange("p (t e) -> p t e", t=TPB),
                                b_r2[:].unsqueeze(1).to_broadcast([P, TPB, E]), ALU.add).then_inc(z_by_dve, 1)
                dve.wait_ge(*z_read(b, Z_LG))
                hold(dve)
                for t in range(TPB):
                    V.max(top[:, t, :], lg[:, t, :]).then_inc(top_s, 1)
                dve.wait_ge(top_s, TPB * (b + 1))
                hold(dve)
                for t in range(TPB):
                    V.max_index(topi[:, t, :], top[:, t, :], lg[:, t, :]).then_inc(topi_s, 1)
                V.tensor_tensor(dlt[:], top[:, :, 1], top[:, :, 0], ALU.subtract).then_inc(dlt_s, 1)
                dve.wait_ge(topi_s, TPB * (b + 1))
                V.tensor_copy(topf[:], topi[:, :, 0:2]).then_inc(topf_s, 1)

            def z_pick(b):
                dve.wait_ge(topf_s, b + 1)
                for t in range(TPB):
                    for k in range(TOPK):
                        V.tensor_scalar(oh[:, t, k, :], iota8[:], topf[:, t, k:k + 1], None, ALU.is_equal
                                        ).then_inc(oh_s, 1)
                dve.wait_ge(oh_s, TPB * TOPK * (b + 1))
                V.tensor_tensor(pick[:], oh[:, :, 0, :], oh[:, :, 1, :], ALU.add).then_inc(pick_s, 1)
                dve.wait_ge(e2_s, b + 1)
                V.tensor_scalar(den[:], e2[:], 1.0, None, ALU.add).then_inc(den_s, 1)
                dve.wait_ge(den_s, b + 1)
                V.reciprocal(wt[:, :, 0], den[:]).then_inc(wt_s, 1)
                dve.wait_ge(wt_s, 2 * b + 1)
                V.tensor_tensor(wt[:, :, 1], wt[:, :, 0], e2[:], ALU.mult).then_inc(wt_s, 1)
                dve.wait_ge(wt_s, 2 * (b + 1))
                V.tensor_copy(xn3[:, :, C_ID], ids[:, tiles(b)])
                V.tensor_copy(xn3[:, :, C_W:C_W + TOPK], wt[:])
                V.tensor_copy(xn3[:, :, C_E], topf[:, :, 0])

            def z_slots(b):
                dve.wait_ge(z_filled, z_item(b, Z_RK))
                rank = zbank
                V.tensor_tensor(row[:], rank[:, 0:TPB * E].rearrange("p (t e) -> p t e", t=TPB),
                                run[:].unsqueeze(1).to_broadcast([P, TPB, E]), ALU.add).then_inc(row_s, 1)
                dve.wait_ge(row_s, b + 1)
                V.tensor_tensor(run[:], rank[:, TPB * E:(TPB + 1) * E], run[:], ALU.add).then_inc(z_by_dve, 1)
                V.tensor_tensor(pm[:], oh[:], row[:].unsqueeze(2).to_broadcast([P, TPB, TOPK, E]), ALU.mult
                                ).then_inc(pm_s, 1)
                dve.wait_ge(pm_s, b + 1)
                V.tensor_reduce(posf[:].rearrange("p t k -> p (t k)"), pm[:].rearrange("p t k e -> p (t k) e"), AX.X,
                                ALU.add).then_inc(row2_s, 1)
                dve.wait_ge(row2_s, b + 1)
                dve.wait_ge(scattered, 16 * TOPK * TPB * b)
                V.tensor_copy(posu[:], posf[:]).then_inc(pos_s, 1)

            def turn(i, r, x, z):
                j, k = i - 1, i - 2
                more = not isinstance(i, int) or i < B - 1
                if r: r_low(i)
                if x: x_x1(j)
                if z: z_sum(k)
                if x: x_norm2(j)
                if r: r_rotate(i, (0,))
                if x: low_t2(j)
                if r: r_rotate(i, (1,))
                if z: z_r1(k)
                if x: x_q(j)
                if r: r_gate(i, 0)
                if x: x_max(j, 0, (0,))
                if z: z_route(k)
                if x: x_max(j, 0, (1, 2, 3))
                if r: r_decay(i, (0, 1))
                if z: z_pick(k)
                if x: x_probs(j, 0, 1)
                if r: r_decay(i, (2, 3))
                if x: x_probs(j, 0, 3)
                if more: r_norm1a(i + 1)
                if x: x_max(j, 1, (0, 1))
                if z: z_slots(k)
                if r: r_gate(i, 1)
                if x: x_max(j, 1, (2, 3))
                if more: r_norm1b(i + 1)
                if r: r_decay(i, (4, 5))
                if x: x_probs(j, 1, 1)
                if r: r_decay(i, (6, 7))
                if x: x_rinv(j)
                if x: x_probs(j, 1, 3)
                if r: r_z(i)
                if r: r_var(i)
                if x: x_u(j)
                if r: x_k(i)
                elif x: dve.drain().then_inc(x_by_dve, 1)
                if r: r_y(i)
                if x: x_x2(j)
                if x: x_norm3(j)

            def low_weights(e):
                dve.wait_ge(hi_w, 2 * (e + 1))
                for n in range(2):
                    V.tensor_tensor(w12[:, e, n, 1, :], w12[:, e, n, 1, :].bitcast(f32),
                                    w12[:, e, n, 0, :].bitcast(f32), ALU.subtract).then_inc(lo_w, 1)

            dve.sem_inc(r_by_dve, r_all["dve"])
            dve.sem_inc(x_by_dve, x_all_["dve"] - 2)
            dve.sem_inc(z_by_dve, z_all["dve"])
            V.memset(mhalf[:], -0.5)
            V.memset(ones1[:], 1.0).then_inc(ones_s, 1)
            dve.wait_ge(ones_s, 1)
            V.tensor_copy(ones2[:], ones1[0:2, :])
            V.memset(ones1b[:], 1.0)
            V.memset(onesb[:], 1.0).then_inc(setup, 1)
            def low_const(n, w, raw):
                dve.wait_ge(const_hi, n)
                flat_w = w.rearrange("p a k f -> p a (k f)")
                V.tensor_tensor(flat_w[:, 1], raw, flat_w[:, 0].bitcast(f32), ALU.subtract
                                ).then_inc(const_lo, 1)

            r_norm1a(0)
            r_norm1b(0)
            low_const(C_QK, w_qk[:], qk_raw)
            r_low(0)
            low_const(C_G, w_g[:], g_raw)
            dve.wait_ge(ld["wv"], 16)
            V.tensor_reduce(vmean[:].rearrange("p k h -> p (k h)"), w_v.rearrange("p k (h j) -> p (k h) j", h=NH), AX.X,
                            ALU.add).then_inc(vmean_s, 1)
            dve.wait_ge(vmean_s, 1)
            V.tensor_scalar(vmean[:], vmean[:], 1.0 / DV, None, ALU.mult).then_inc(vmean_s, 1)
            dve.wait_ge(vmean_s, 2)
            for k in range(KD):
                V.tensor_tensor(vc_raw[:, k * 512:(k + 1) * 512].rearrange("p (h j) -> p h j", h=NH),
                                w_v[:, k, :].rearrange("p (h j) -> p h j", h=NH),
                                vmean[:, k, :].unsqueeze(2).to_broadcast([P, NH, DV]), ALU.subtract
                                ).then_inc(wvc_done, 1)
            dve.wait_ge(ld["rot"], 2 * 16)
            r_rotate(0, range(TPB))
            low_const(C_V, w_vc[:], vc_raw)
            dve.wait_ge(ld["decay"], 2 * 16)
            for h in range(NH):
                V.tensor_tensor_scan(DM[:, h, 0:T], dec[:, h:h + 1].to_broadcast([P, T]), delta_sb, 0.0,
                                     ALU.mult, ALU.add).then_inc(dm_scan, 1)
            dve.wait_ge(dm_scan, NH)
            V.tensor_copy(DM[:, :, T:SC], DM[:, :, 0:P]).then_inc(dm_done, 1)
            dve.wait_ge(dm_done, 1)
            r_gate(0, 0)
            dve.wait_ge(ld["const"], CONSTS * 16)
            dve.wait_ge(ld["r2"], 16)
            V.tensor_copy(run[:], base[:])
            V.tensor_copy(before[:], before_f).then_inc(setup2, 1)
            V.tensor_scalar(b_r1h[:], b_r1[:], 0.5, None, ALU.mult)
            V.tensor_scalar(w_r2[:], w_r2[:], 0.5, None, ALU.mult).then_inc(setup2, 1)
            dve.wait_ge(setup2, 2)
            r_decay(0, range(4))
            r_gate(0, 1)
            r_decay(0, range(4, NH))
            V.tensor_copy(sel8[:].rearrange("p g v -> p (g v)"), sel8_raw).then_inc(sel_s, 1)
            V.tensor_copy(selh[:].rearrange("p g v -> p (g v)"), selh_raw).then_inc(sel_s, 1)
            r_norm1a(1)
            r_norm1b(1)
            r_z(0)
            r_var(0)
            low_const(C_S, w_s[:], s_raw)
            low_const(C_T, w_t[:], t_raw)
            low_const(C_O, w_o[:], o_raw)
            V.tensor_copy(b_vo_parts[:, 0, :], b_vo_raw[:]).then_inc(bvo_s, 1)
            dve.wait_ge(bvo_s, 1)
            V.tensor_tensor(b_vo_parts[:, 1, :], b_vo_raw[:], b_vo_parts[:, 0, :].bitcast(f32), ALU.subtract
                            ).then_inc(bvo_s, 1)
            x_k(0)
            dve.drain().then_inc(x_by_dve, 1)
            r_y(0)
            dve.wait_ge(ld["ffn"], 2 * 16)
            V.tensor_copy(b_parts[:, 0, :], b_raw[:]).then_inc(b_parts_s, 1)
            dve.wait_ge(b_parts_s, 1)
            V.tensor_tensor(b_parts[:, 1, :], b_raw[:], b_parts[:, 0, :].bitcast(f32), ALU.subtract
                            ).then_inc(b_parts_s, 1)
            turn(1, True, True, False)
            with dve.Fori(2, B - 1) as i:
                turn(i, True, True, True)
            turn(B - 1, True, True, True)
            turn(B, False, True, True)
            for e in range(4):
                low_weights(e)
            z_sum(B - 1)
            z_r1(B - 1)
            for e in range(4, 6):
                low_weights(e)
            z_route(B - 1)
            z_pick(B - 1)
            z_slots(B - 1)
            dve.drain().then_inc(phase1, 1)

            steps = [0]

            def after(ins):
                steps[0] += 1
                ins.then_inc(n_s, 1)
                dve.wait_ge(n_s, steps[0])

            for count in (xT_lo, hT_lo):
                dve.sem_inc(count, 2)
            dve.wait_ge(*z_read(B - 1, Z_RK))
            V.tensor_copy(run_i[:], run[:]).then_inc(pads_s, 1)
            V.memset(ones_e[:], 1.0)
            after(V.tensor_tensor(n_sl[:], run[:], base[:], ALU.subtract))
            after(V.tensor_scalar(n_i[:], n_sl[:], float(P - 1), None, ALU.add))
            after(V.tensor_scalar(n_i[:], n_i[:], P.bit_length() - 1, None, ALU.logical_shift_right))
            after(V.tensor_copy(n_t[:], n_i[:]))
            after(V.tensor_tensor_scan(cum[:], ones_e[:], n_t[:], 0.0, ALU.mult, ALU.add))
            after(V.tensor_tensor(past[:], iota_t[:].unsqueeze(2).to_broadcast([P, FT, E]),
                                  cum[:].unsqueeze(1).to_broadcast([P, FT, E]), ALU.is_ge))
            after(V.tensor_reduce(t_e[:], past[:], AX.X, ALU.add))
            after(V.tensor_tensor(past_t[:], past[:], n_t[:].unsqueeze(1).to_broadcast([P, FT, E]), ALU.mult))
            after(V.tensor_reduce(t_s[:], past_t[:], AX.X, ALU.add))
            after(V.tensor_scalar(t_ok[:], t_e[:], float(E), None, ALU.is_lt))
            after(V.tensor_tensor(t_row[:], iota_t[:], t_s[:], ALU.subtract))
            after(V.tensor_scalar(t_row[:], t_row[:], float(P), None, ALU.mult))
            after(V.scalar_tensor_tensor(t_row[:], t_e[:], float(CAP), t_row[:], ALU.mult, ALU.add))
            after(V.tensor_scalar(t_pad[:], t_ok[:], -float(E * CAP), float(E * CAP), ALU.mult, ALU.add))
            after(V.tensor_tensor(t_row[:], t_row[:], t_ok[:], ALU.mult))
            V.tensor_tensor(tab[:, 0, :], t_e[:], t_ok[:], ALU.mult).then_inc(tab_s, 1)
            V.tensor_tensor(tab_f[:], t_e[:], t_ok[:], ALU.mult).then_inc(tab_s, 1)
            V.tensor_tensor(tab[:, 1, :], t_row[:], t_pad[:], ALU.add).then_inc(tab_s, 1)
            after(V.tensor_tensor(before_t[:], t_s[:], iota_t[:], ALU.subtract))
            after(V.tensor_tensor(before_t[:], before_t[:], t_ok[:], ALU.mult))
            after(V.tensor_tensor(before_t[:], before_t[:], iota_t[:], ALU.add))
            after(V.tensor_tensor(before_i[:], before_t[:], parity[:], ALU.add))
            after(V.tensor_scalar(before_i[:], before_i[:], 1, None, ALU.logical_shift_right))
            V.tensor_scalar(tab[:, 2, :], before_i[:], 1.0, 16.0, ALU.max, ALU.mult).then_inc(tab_s, 1)
            for e in range(6, E):
                low_weights(e)
            dve.wait_ge(phase1, 4)

            def low_rows(i, slot):
                dve.wait_ge(xT_hi, done(i))
                V.tensor_tensor(xT[:, slot, 1, :], psum[:, slot, 0:KD * P], xT[:, slot, 0, :].bitcast(f32),
                                ALU.subtract).then_inc(xT_lo, 1)

            def low_hidden(i, slot):
                dve.wait_ge(hT_hi, done(i))
                V.tensor_tensor(hT[:, slot, 1, :], psum[:, 4 + slot, :], hT[:, slot, 0, :].bitcast(f32),
                                ALU.subtract).then_inc(hT_lo, 1)

            def pick_weight(i, half, slot):
                dve.wait_ge(xt_in[slot], 16 * (half + 1))
                e = tab_f[:, bass.ds(i, 1)]
                for k, same in enumerate((ALU.is_equal, ALU.not_equal)):
                    V.tensor_scalar(w_part[:, slot, k:k + 1], xt[:, slot, C_E:C_E + 1], e,
                                    xt[:, slot, C_W + k:C_W + k + 1], same, ALU.mult).then_inc(wpart_s, 1)
                V.tensor_copy(id_tile[:, bass.ds(i, 1)], xt[:, slot, C_ID:C_ID + 1])
                dve.wait_ge(wpart_s, 2 * (i + 1))
                V.tensor_tensor(w_tile[:, bass.ds(i, 1)], w_part[:, slot, 0:1], w_part[:, slot, 1:2], ALU.add
                                ).then_inc(picked, 1)

            def number(i, place):
                dve.wait_ge(freed, i + 1)
                V.tensor_copy(yi[:, place:place + 1], id_tile[:, bass.ds(i, 1)]).then_inc(yi_s, 1)

            def step(i, half, k, rows=True, out=True, turned=True):
                slot = k % 2
                if rows:
                    low_rows(i + 1, 1 - slot)
                    pick_weight(i + 1, half + slot, 1 - slot)
                if out:
                    number(i - 3, (k + 1) % 4)
                if turned:
                    low_hidden(i - 1, 1 - slot)

            dve.wait_ge(tab_s, 4)
            low_rows(0, 0)
            pick_weight(0, 0, 0)
            step(0, 0, 0, out=False, turned=False)
            step(1, 0, 1, out=False)
            step(2, 1, 2, out=False)
            step(3, 1, 3)
            with dve.Fori(1, FT // 4 - 1) as turn:
                for k in range(4):
                    step(4 * turn + k, 2 * turn + k // 2, k)
            for k in range(3):
                step(FT - 4 + k, FT // 2 - 2 + k // 2, k)
            step(FT - 1, FT // 2 - 1, 3, rows=False)
            low_hidden(FT - 1, 1)
            for i in range(FT - 3, FT):
                number(i, i % 4)

        @block.scalar
        def _(act):
            A = nc.scalar

            def copy(dst, src, ring, name=None):
                A.activation(dst, src, ACT.Copy).then_inc({"r": r_by_act, "x": x_by_act, "z": z_by_act}[ring], 1)

            def flat(a):
                return a.rearrange("p c s -> p (c s)")

            def r_xt(b):
                act.wait_ge(r_filled, r_item(b, R_XT))
                A.activation(flat(xnT[:, 0]), rbank(R_XT), ACT.Copy).then_inc(xnT_hi, 1)

            def r_v(b, t):
                act.wait_ge(r_filled, r_item(b, R_V[t]))
                copy(vc[:, t, :], rbank(R_V[t]), "r")

            def r_g(b, n):
                act.wait_ge(r_filled, r_item(b, R_G[n]))
                A.activation(flat(gate[:, 2 * n:2 * n + 2, :]), rbank(R_G[n]), ACT.Tanh, scale=0.5).then_inc(th_g, 1)

            def r_qkt(b):
                act.wait_ge(r_filled, r_item(b, R_QT))
                copy(flat(qT[:]), rbank(R_QT), "r")
                act.wait_ge(r_filled, r_item(b, R_KT))
                copy(flat(kT[:]), rbank(R_KT), "r")

            def r_sq(b):
                for n in range(2):
                    act.wait_ge(r_filled, r_item(b, R_O + n))
                    A.activation(flat(sq[:, 2 * n:2 * n + 2, :]), rbank(R_O + n), ACT.Square
                                 ).then_inc(sq_done, 1)

            def r_gt(b):
                act.wait_ge(r_filled, r_item(b, R_GT))
                copy(gr[:], rbank(R_GT)[0:2 * NH, 0:T], "r")

            def x_t2(b):
                act.wait_ge(x_filled, x_item(b, X_T2))
                A.activation(flat(t2T[:, 0]), xbank(X_T2), ACT.Copy).then_inc(t2T_hi, 1)

            def keep_x(b):
                act.wait_ge(xn_s[0], TPB * (b + 1))
                if not isinstance(b, int) or b > 0:
                    act.wait_ge(*x_read(b - 1, X_Y))
                A.activation(flat(xr[:]), flat(xa[:]), ACT.Copy).then_inc(xa_used, 1)

            def high_context(b):
                act.wait_ge(ctx_in, 16 * (b + 1))
                A.activation(flat(ctx_sb[:, 0]), flat(ctx_raw[:]), ACT.Copy).then_inc(ctx_hi, 1)

            def x_v(b, t):
                act.wait_ge(x_filled, x_item(b, X_V1) if t else x_item(b - 1, X_NV))
                A.activation(v2[:, t, :], xbank(X_V1 if t else X_NV)[:, 0:D], ACT.Copy, scale=mcol[:, bass.ds(b * TPB + t, 1)]
                             ).then_inc(x_by_act, 1)

            def x_exp(b, t, r):
                n = X_S[t][r]
                act.wait_ge(nmx_s, HPG * (TPB * b + t) + r + 1)
                if t:
                    act.wait_ge(x_filled, x_item(b, X_P[0] + r))
                for g in range(KD):
                    h = g * HPG + r
                    ins = A.activation(pr[:, h, :], xbank(n)[:, g * T:(g + 1) * T], ACT.Exp,
                                       bias=nmx[:, t, h:h + 1], scale=SCALE, accum_out=rsum[:, t, h:h + 1])
                ins.then_inc(x_by_act, 1)

            def x_probs(b, t, r):
                n = X_P[t] + r
                act.wait_ge(x_filled, x_item(b, n))
                for s in range(TPB):
                    ins = A.activation(pT[:, s, r::HPG, t * P:(t + 1) * P],
                                       xbank(n)[:, s * 2 * P:(s + 1) * 2 * P].rearrange("p (g t) -> p g t", g=KD),
                                       ACT.Copy)
                ins.then_inc(x_by_act, 1)

            def x_u(b):
                act.wait_ge(x_filled, x_item(b, X_RS))
                copy(riT[:], xbank(X_RS)[0:2 * NH, 0:T], "x")
                act.wait_ge(x_filled, x_item(b, X_U))
                copy(flat(u_raw[:]), xbank(X_U), "x")
                act.wait_ge(*x_read(b, X_RB))
                A.activation(flat(uT[:, 0]), flat(u_f[:]), ACT.Copy).then_inc(uT_hi, 1)

            def z_t3(b):
                act.wait_ge(z_filled, z_item(b, Z_T3))
                copy(flat(t3T[:]), zbank, "z")

            def z_r1(b):
                act.wait_ge(z_filled, z_item(b, Z_R1))
                for g in range(KD):
                    A.activation(r1th[:, g, :], zbank[:, g * T:(g + 1) * T], ACT.Tanh, bias=b_r1h[:, g:g + 1],
                                 scale=0.5)
                    ins = A.activation(r1[:, g, :], zbank[:, g * T:(g + 1) * T], ACT.Identity,
                                       bias=b_r1[:, g:g + 1])
                ins.then_inc(z_by_act, 1)

            def z_route(b):
                act.wait_ge(dlt_s, b + 1)
                A.activation(e2[:], dlt[:], ACT.Exp).then_inc(e2_s, 1)

            def turn(i, r, x, z):
                j, k = i - 1, i - 2
                if r: r_xt(i)
                if x: x_v(j, 0)
                if z: z_t3(k)
                if x: x_t2(j)
                if z: z_r1(k)
                if r: keep_x(i)
                if r: r_g(i, 0)
                if x: x_v(j, 1)
                if x: x_exp(j, 0, 0)
                if r: r_qkt(i)
                if x: x_exp(j, 0, 1)
                if x: x_exp(j, 0, 2)
                if r: r_v(i, 0)
                if x: x_exp(j, 0, 3)
                if z: z_route(k)
                if x: x_probs(j, 0, 0)
                if x: x_probs(j, 0, 2)
                if r: high_context(i)
                if r: r_g(i, 1)
                if x: x_exp(j, 1, 0)
                if x: x_exp(j, 1, 1)
                if x: x_exp(j, 1, 2)
                if r: r_v(i, 1)
                if x: x_exp(j, 1, 3)
                if x: x_probs(j, 1, 0)
                if x: x_probs(j, 1, 2)
                if r: r_sq(i)
                if x: x_u(j)
                if r: r_gt(i)

            def high_weights(e):
                act.wait_ge(w_in[e], 2 * 16)
                for n in range(2):
                    A.activation(w12[:, e, n, 0, :], w12[:, e, n, 1, :].bitcast(f32), ACT.Copy).then_inc(hi_w, 1)

            act.sem_inc(r_by_act, r_all["act"])
            act.sem_inc(x_by_act, x_all_["act"] - 1)
            act.sem_inc(z_by_act, z_all["act"])

            def high_const(w, raw, sem_, count):
                act.wait_ge(sem_, count)
                flat_w = w.rearrange("p a k f -> p a (k f)")
                A.activation(flat_w[:, 0], raw, ACT.Copy).then_inc(const_hi, 1)

            high_const(w_qk[:], qk_raw, ld["wqk"], 16)
            r_xt(0)
            high_const(w_g[:], g_raw, ld["wg"], 16)
            high_const(w_vc[:], vc_raw, wvc_done, KD)
            r_g(0, 0)
            r_qkt(0)
            r_v(0, 0)
            keep_x(0)
            r_g(0, 1)
            high_const(w_s[:], s_raw, ld["ws"], 16)
            high_const(w_t[:], t_raw, ld["wt"], 16)
            high_const(w_o[:], o_raw, ld["wo"], 16)
            r_v(0, 1)
            high_context(0)
            r_sq(0)
            r_gt(0)
            act.wait_ge(ld["const"], CONSTS * 16)
            act.wait_ge(setup2, 2)
            turn(1, True, True, False)
            with act.Fori(2, B - 1) as i:
                turn(i, True, True, True)
            turn(B - 1, True, True, True)
            turn(B, False, True, True)
            for e in range(4):
                high_weights(e)
            z_t3(B - 1)
            high_weights(4)
            z_r1(B - 1)
            high_weights(5)
            z_route(B - 1)
            for e in range(6, E):
                high_weights(e)
            act.drain().then_inc(phase1, 1)

            act.sem_inc(xT_hi, 2)
            act.sem_inc(sil_s, 2)
            act.sem_inc(hT_hi, 2)
            act.sem_inc(y_s, 2)
            act.wait_ge(phase1, 4)

            def high_rows(i, slot):
                act.wait_ge(xT_f, done(i))
                act.wait_ge(l1_f, done(i - 2))
                A.activation(xT[:, slot, 0, :], psum[:, slot, 0:KD * P], ACT.Copy).then_inc(xT_hi, 1)

            def silu(i, slot):
                act.wait_ge(l1_f, done(i))
                act.wait_ge(hT_f, done(i - 2))
                A.activation(hid[:, slot, :], psum[:, 2 + slot, :], ACT.Silu).then_inc(sil_s, 1)

            def high_hidden(i, slot):
                act.wait_ge(hT_f, done(i))
                act.wait_ge(l2_f, done(i - 2))
                A.activation(hT[:, slot, 0, :], psum[:, 4 + slot, :], ACT.Copy).then_inc(hT_hi, 1)

            def weigh(i, place):
                act.wait_ge(l2_f, done(i))
                act.wait_ge(freed, i + 1)
                act.wait_ge(picked, i + 1)
                A.activation(yo[:, place, :], psum[:, 6 + place % 2, 0:D], ACT.Copy, scale=w_tile[:, bass.ds(i, 1)]
                             ).then_inc(y_s, 1)

            def step(i, half, k, rows=True, out=True, turned=True):
                slot = k % 2
                if rows:
                    high_rows(i + 1, 1 - slot)
                if out:
                    weigh(i - 3, (k + 1) % 4)
                if turned:
                    high_hidden(i - 1, 1 - slot)
                silu(i, slot)

            high_rows(0, 0)
            step(0, 0, 0, out=False, turned=False)
            step(1, 0, 1, out=False)
            step(2, 1, 2, out=False)
            step(3, 1, 3)
            with act.Fori(1, FT // 4 - 1) as turn:
                for k in range(4):
                    step(4 * turn + k, 2 * turn + k // 2, k)
            for k in range(3):
                step(FT - 4 + k, FT // 2 - 2 + k // 2, k)
            step(FT - 1, FT // 2 - 1, 3, rows=False)
            high_hidden(FT - 1, 1)
            for i in range(FT - 3, FT):
                weigh(i, i % 4)

        @block.gpsimd
        def _(pool):
            G = nc.gpsimd

            def root(b, n):
                pool.wait_ge(aggr[n], TPB * (b + 1))
                hold(pool)
                G.tensor_scalar(veps[:, n, :], mv[:, n, :, 1], EPS, None, ALU.add).then_inc(veps_s[n], 1)
                pool.wait_ge(veps_s[n], b + 1)
                G.tensor_tensor(rstd[:, n, :], veps[:, n, :], mhalf[:, 0:TPB], ALU.pow).then_inc(rstd_s[n], 1)

            def rotate(b):
                for t in range(TPB):
                    pool.wait_ge(*r_read(b, R_QK + t))
                    G.tensor_tensor(rot_a[:, t, :], rot_a[:, t, :], rot_b[:, t, :], ALU.add).then_inc(rot, 1)

            def groups(b):
                pool.wait_ge(*r_read(b, R_VAR))
                G.tensor_tensor(grt[:].rearrange("p t h -> p (t h)"), gvt[:].rearrange("p t h -> p (t h)"),
                                mhalf[:], ALU.pow).then_inc(grt_s, 1)
                pool.wait_ge(grt_s, b + 1)
                hold(pool)
                G.tensor_copy(gr_parts[:, :, 0, :], grt[:]).then_inc(gr_s, 1)
                pool.wait_ge(gr_s, 2 * b + 1)
                G.tensor_tensor(gr_parts[:, :, 1, :], grt[:], gr_parts[:, :, 0, :].bitcast(f32), ALU.subtract
                                ).then_inc(gr_s, 1)

            def low_context(b):
                pool.wait_ge(ctx_hi, b + 1)
                hold(pool)
                G.tensor_tensor(ctx_sb[:, 1].rearrange("p c s -> p (c s)"),
                                ctx_raw[:].rearrange("p c s -> p (c s)"),
                                ctx_sb[:, 0].rearrange("p c s -> p (c s)").bitcast(f32), ALU.subtract
                                ).then_inc(ctx_lo, 1)

            def scatter(b):
                pool.wait_ge(pos_s, b + 1)
                hold(pool)
                for t in range(TPB):
                    for k in range(TOPK):
                        G.indirect_dma_start(slot_in[:, :], bass.IndirectOffsetOnAxis(ap=posu[:, t, k:k + 1], axis=0),
                                             xn3[:, t, :], None).then_inc(scattered, 16)

            def turn(i, r, x, z):
                if isinstance(i, int) and i == 0: root(0, 0)
                if x: root(i - 1, 1)
                if r: rotate(i)
                if r: low_context(i)
                if not isinstance(i, int) or i < B - 1: root(i + 1, 0)
                if z: scatter(i - 2)
                if r: groups(i)
                if x: root(i - 1, 2)

            pool.wait_ge(setup, 1)
            turn(0, True, False, False)
            pool.wait_ge(bvo_s, 2)
            for part in range(2):
                for n in range(2):
                    pool.dma_start(b_vo[part:part + 1, n * D:(n + 1) * D],
                                   b_vo_parts[:, part, n * D // P:(n + 1) * D // P]).then_inc(bvo_in, 16)
            turn(1, True, True, False)
            with pool.Fori(2, B - 1) as i:
                turn(i, True, True, True)
            turn(B - 1, True, True, True)
            turn(B, False, True, True)
            turn(B + 1, False, False, True)
            pool.drain().then_inc(phase1, 1)

            def add_tile(i, half, k):
                slot = k % 2
                if not isinstance(i, int) or i > 1:
                    others = pool.value_load(tab[0:1, 2, bass.ds(i, 1)], min_val=16, max_val=16 * FT)
                    pool.wait_ge(added[slot], 16 * half)
                    pool.sem_inc(freed, 1)
                pool.wait_ge(y_s, done(i))
                hold(pool)
                pool.wait_ge(yi_s, i + 1)
                hold(pool)
                if not isinstance(i, int) or i > 1:
                    pool.wait_ge(added[1 - slot], others)
                    hold(pool)
                elif i == 1:
                    pool.wait_ge(added[0], 16)
                G.indirect_dma_start(out[:, :], bass.IndirectOffsetOnAxis(ap=yi[:, k:k + 1], axis=0),
                                     yo[:, k, :], None, compute_op=ALU.add).then_inc(added[slot], 16)

            pool.wait_ge(phase1, 4)
            pool.wait_ge(b_parts_s, 2)
            for part in range(2):
                pool.dma_start(bias[part:part + 1, 0:E * H], b_parts[:, part, 0:E * H // P]).then_inc(bias_in, 16)
                pool.dma_start(bias[part:part + 1, E * H:], b_parts[:, part, E * H // P:]).then_inc(bias_in, 16)
            pool.sem_inc(freed, 4)
            pool.wait_ge(x2_out, 16 * (B + 1))
            for k in range(4):
                add_tile(k, k // 2, k)
            with pool.Fori(1, FT // 4) as turn:
                for k in range(4):
                    add_tile(4 * turn + k, 2 * turn + k // 2, k)
            for slot in range(2):
                pool.wait_ge(added[slot], 16 * (FT // 2))

    return nc


def shape_constants():
    import numpy as np

    f = np.float32
    vec = (np.arange(0, D, 2, dtype=f) + f(0.4 * D)) / f(1.4 * D)
    pos = np.arange(T, dtype=f)
    scale = vec[None, :] ** (pos[:, None] / f(512.0))
    half = D // 2
    inv = f(1.0) / f(10000.0) ** (np.arange(half, dtype=f) / f(half))
    ang = pos[:, None] * inv[None, :]
    sin, cos = np.sin(ang), np.cos(ang)
    cs, sn = [], []
    for s in (scale, f(1.0) / scale):
        c = (cos * s).reshape(T, NH, 1, DH // 2)
        n = (sin * s).reshape(T, NH, 1, DH // 2)
        cs.append(np.concatenate([c, c], 2).reshape(T, D))
        sn.append(np.concatenate([-n, n], 2).reshape(T, D))
    rot_c = np.concatenate(cs, 1).reshape(TPB, P, 2 * D).transpose(1, 0, 2)
    rot_s = np.concatenate(sn, 1).reshape(TPB, P, 2 * D).transpose(1, 0, 2)
    delta = (np.arange(P)[:, None] == np.arange(T)).astype(f) * f(DH ** -0.5)
    v = np.arange(512).reshape(KV, P)
    head = v // DV
    sel64 = (head[:, :, None] == np.arange(NH)).astype(f).transpose(1, 0, 2) / f(DV)
    sel8 = (head[None] == np.arange(NH)[:, None, None]).astype(f)
    selh = ((np.arange(D) // DH).reshape(1, KD, P) == np.arange(NH)[:, None, None]).astype(f)
    iota = np.tile(np.arange(E, dtype=f), (P, 1))
    return {"rot_c": rot_c, "rot_s": rot_s, "delta": delta, "ident_in": np.eye(P, dtype=f),
            "sel64_in": sel64, "sel8_in": np.concatenate([sel8, sel8]), "selh_in": np.concatenate([selh, selh]), "iota_in": iota,
            "iota_t_in": np.tile(np.arange(FT, dtype=f), (P, 1)),
            "before_in": np.triu(np.ones((P, P), f), 1),
            "pad_in": np.where(np.arange(ROW)[None, :] == C_ID, B * T + np.arange(P)[:, None], 0).astype(f),
            "parity_in": np.tile(np.arange(FT) % 2, (P, 1)).astype(f),
            "ids_in": np.arange(B * T, dtype=f).reshape(NT, P).T,
            "base_in": np.tile(np.arange(E, dtype=f) * f(CAP), (P, 1))}


def kernel(**inputs):
    import numpy as np
    import concourse.bacc as bacc
    from concourse import mybir as mb
    from concourse.bass_utils import run_bass_kernel_spmd as run

    a = {k: np.asarray(v) for k, v in inputs.items()}

    def chunks(w):
        return w.reshape(w.shape[0] // P, P, w.shape[1]).transpose(1, 0, 2)

    def halves(w):
        return w.reshape(NH, DH // 2, 2, D).transpose(0, 2, 1, 3).reshape(D, D)

    wqkv = a["L0_attn_w_qkv"]
    wsrc, bsrc = a["L0_xattn_W_src"], a["L0_xattn_b_src"]
    mask = a["mask_BxS2_fk1"]
    arrays = {
        "x": a["x"].reshape(B * T, D),
        "ctxT": a["ctx_2048"].reshape(B, T, KC, P).transpose(0, 3, 2, 1).reshape(B, P, KC * T),
        "maskrow": mask, "maskcol": mask.reshape(NT, P).T,
        "wqkT": chunks(np.concatenate([halves(wqkv[0:D]), halves(wqkv[D:2 * D])], 0).T),
        "wvT": chunks(wqkv[2 * D:].T), "wgT": chunks(a["L0_attn_w_gated"].T), "wpT": chunks(a["L0_attn_w_proj"].T),
        "decay": a["L0_attn_decay"], "wsT": chunks(wsrc.T), "bsk": bsrc[0:D].reshape(KD, P).T,
        "bsv": bsrc[D:].reshape(P, D // P), "wtT": chunks(a["L0_xattn_W_tgt"].T),
        "bt": a["L0_xattn_b_tgt"].reshape(KD, P).T, "woT": chunks(a["L0_xattn_W_out"].T),
        "bo": a["L0_xattn_b_out"].reshape(P, D // P), "rw1": chunks(a["L0_ffn_rw1"]),
        "rb1": a["L0_ffn_rb1"].reshape(KD, P).T, "rw2": chunks(a["L0_ffn_rw2"]), "rb2": a["L0_ffn_rb2"],
        "ew1": a["L0_ffn_ew1"].reshape(E, KD, P, H).transpose(2, 0, 1, 3).reshape(P, E, KD * H),
        "eb1": a["L0_ffn_eb1"].reshape(P, E * H // P),
        "ew2": a["L0_ffn_ew2"].reshape(E, KH, P, D).transpose(2, 0, 1, 3).reshape(P, E, KH * D), "eb2": a["L0_ffn_eb2"].reshape(P, E * D // P),
        **shape_constants(),
    }
    nc = bacc.Bacc("TRN2", target_bir_lowering=False, num_devices=1)
    feed, args = {}, {}
    for name, v in arrays.items():
        v = np.ascontiguousarray(v)
        feed["in_" + name] = v
        args[name] = nc.dram_tensor("in_" + name, v.shape, mb.dt.from_np(v.dtype), kind="ExternalInput").ap()
    args["out"] = nc.dram_tensor("out", (B * T + P, D), mb.dt.float32, kind="ExternalOutput").ap()
    build(nc, **args)
    r = run(nc, [feed], core_ids=[0])
    return r.results[0]["out"][0:B * T].reshape(B, T, D)
```
